# Optimizing a Trainium2 kernel written in Bass

```python
import numpy as np
import jax
import jax.numpy as jnp

def _softmax(x, axis=-1):
    return jax.nn.softmax(x, axis=axis)

def _gelu(x):
    return jax.nn.gelu(x, approximate=True)

def _silu(x):
    return jax.nn.silu(x)

def _sigmoid(x):
    return jax.nn.sigmoid(x)

def _layernorm(x, axis=-1, eps=1e-05):
    m = jnp.mean(x, axis=axis, keepdims=True)
    v = jnp.var(x, axis=axis, keepdims=True)
    return (x - m) / jnp.sqrt(v + eps)

def _scatter_add(tgt, idx, src, axis=0):
    return tgt.at[idx].add(src)

def _segment_sum(src, seg, n):
    return jax.ops.segment_sum(src, seg, n)
kernel_name = 'mk_seq_postln_d2_jaxref_r8_312384'

def setup_inputs(seed: int=0):
    np.random.seed(seed)
    _w = jnp.asarray

    def _L0_attn_setup():
        import jax, jax.numpy as jnp
        import numpy as np
        from jax import lax
        BATCH = 2
        SEQ = 256
        HID = 256
        EXPAND = 2
        INTER = EXPAND * HID
        HEADS = 64
        PDIM = INTER // HEADS
        NSTATE = 128
        G = 1
        HPG = HEADS // G
        KCONV = 4
        GTS = G * NSTATE
        CONV_DIM = INTER + 2 * GTS
        PROJ_DIM = 2 * INTER + 2 * GTS + HEADS
        EPS = 1e-05
        MUP = (0.25, 0.5, 0.5, 0.5, 1.0)

        def _mup_vector():
            return jnp.concatenate([jnp.full((INTER,), MUP[0], jnp.float32), jnp.full((INTER,), MUP[1], jnp.float32), jnp.full((GTS,), MUP[2], jnp.float32), jnp.full((GTS,), MUP[3], jnp.float32), jnp.full((HEADS,), MUP[4], jnp.float32)])

        def _forward(hidden_states, in_proj_w, conv_w, conv_b, A_log, D, dt_bias, norm_w, out_proj_w):
            b, l, _ = hidden_states.shape
            proj = hidden_states @ in_proj_w * _mup_vector()
            z = proj[..., :INTER]
            xBC = proj[..., INTER:INTER + CONV_DIM]
            dt = proj[..., INTER + CONV_DIM:]
            xBC_cl = jnp.swapaxes(xBC, 1, 2)
            conv = lax.conv_general_dilated(xBC_cl, conv_w[:, None, :], window_strides=(1,), padding=((KCONV - 1, 0),), feature_group_count=CONV_DIM)
            xBC = jax.nn.silu(jnp.swapaxes(conv + conv_b[None, :, None], 1, 2))
            x = xBC[..., :INTER].reshape(b, l, G, HPG, PDIM)
            Bm = xBC[..., INTER:INTER + GTS].reshape(b, l, G, NSTATE)
            Cm = xBC[..., INTER + GTS:].reshape(b, l, G, NSTATE)
            dt = jax.nn.softplus(dt + dt_bias)
            A = -jnp.exp(A_log)
            dA = jnp.exp(dt * A).reshape(b, l, G, HPG)
            dtx = dt.reshape(b, l, G, HPG)[..., None] * x

            def step(state, inp):
                dA_t, dtx_t, B_t, C_t = inp
                state = state * dA_t[..., None, None] + jnp.einsum('bgcp,bgn->bgcpn', dtx_t, B_t)
                y_t = jnp.einsum('bgn,bgcpn->bgcp', C_t, state)
                return (state, y_t)
            inputs = (jnp.moveaxis(dA, 1, 0), jnp.moveaxis(dtx, 1, 0), jnp.moveaxis(Bm, 1, 0), jnp.moveaxis(Cm, 1, 0))
            state0 = jnp.zeros((b, G, HPG, PDIM, NSTATE), hidden_states.dtype)
            _, ys = lax.scan(step, state0, inputs)
            y = jnp.moveaxis(ys, 0, 1) + D.reshape(1, 1, G, HPG, 1) * x
            y = y.reshape(b, l, INTER)
            yg = y.reshape(b, l, G, INTER // G)
            var = jnp.mean(jnp.square(yg), axis=-1, keepdims=True)
            yn = (yg * lax.rsqrt(var + EPS)).reshape(b, l, INTER) * norm_w
            out = yn * jax.nn.silu(z)
            return out @ out_proj_w
        key = jax.random.key(seed)
        ks = jax.random.split(key, 8)
        hidden_states = jax.random.normal(ks[0], (BATCH, SEQ, HID), jnp.float32)
        in_proj_w = jax.random.normal(ks[1], (HID, PROJ_DIM), jnp.float32) * 0.02
        conv_w = jax.random.normal(ks[2], (CONV_DIM, KCONV), jnp.float32) * 0.2
        conv_b = jnp.zeros((CONV_DIM,), jnp.float32)
        A_log = jnp.log(jnp.arange(1, HEADS + 1, dtype=jnp.float32))
        D = jnp.ones((HEADS,), jnp.float32)
        dt_bias = jax.random.uniform(ks[3], (HEADS,), jnp.float32)
        norm_w = jnp.ones((INTER,), jnp.float32)
        out_proj_w = jax.random.normal(ks[4], (INTER, HID), jnp.float32) * 0.02
        return dict(hidden_states=hidden_states, in_proj_w=in_proj_w, conv_w=conv_w, conv_b=conv_b, A_log=A_log, D=D, dt_bias=dt_bias, norm_w=norm_w, out_proj_w=out_proj_w)
    _L0_attn_in = _L0_attn_setup()

    def _L0_ffn_setup():
        import jax, jax.numpy as jnp
        import numpy as np
        B, S, D, R, E = (4, 256, 256, 64, 8)
        SCALING = 64.0 / 16.0
        key = jax.random.key(seed)
        k1, k2, k3, k4 = jax.random.split(key, 4)
        x = jax.random.normal(k1, (B, S, D), dtype=jnp.float32)
        A = jax.random.normal(k2, (E, R, D), dtype=jnp.float32) * 0.02
        Bw = jax.random.normal(k3, (E, D, R), dtype=jnp.float32) * 0.02
        Wg = jax.random.normal(k4, (E, D), dtype=jnp.float32) * 0.02
        return {'x': x, 'A': A, 'Bw': Bw, 'Wg': Wg}
    _L0_ffn_in = _L0_ffn_setup()

    def _L1_attn_setup():
        import math
        import jax, jax.numpy as jnp
        import numpy as np
        B, T, DIM = (2, 256, 256)
        HEADS, HEAD_DIM = (16, 128)
        KV_GROUPS = 4
        N_KV = HEADS // KV_GROUPS
        LATENT = 64
        SEL_TOPK, SEL_HEADS, SEL_DIM = (64, 1, 64)
        SOFTCAP = 30.0
        EPS = 1e-06

        def _alibi_slopes(n):

            def pot(p):
                start = 2.0 ** (-2.0 ** (-(math.log2(p) - 3)))
                return [start * start ** i for i in range(p)]
            if math.log2(n).is_integer():
                return pot(n)
            cp = 2 ** int(math.floor(math.log2(n)))
            s = pot(cp)
            s += _alibi_slopes(2 * cp)[0::2][:n - cp]
            return s

        def _alibi_bias(h, t):
            slopes = jnp.asarray(_alibi_slopes(h), jnp.float32)
            pos = jnp.arange(t)
            dist = jnp.clip(pos[:, None] - pos[None, :], 0, None).astype(jnp.float32)
            return -slopes[:, None, None] * dist

        def _rope_emb(t, d):
            inv = 1.0 / 10000.0 ** (jnp.arange(0, d, 2, dtype=jnp.float32) / d)
            f = jnp.arange(t, dtype=jnp.float32)[:, None] * inv[None, :]
            return jnp.concatenate([f, f], axis=-1)

        def _apply_rotary(x, emb):
            cos = jnp.cos(emb)[None, :, None, :]
            sin = jnp.sin(emb)[None, :, None, :]
            x1, x2 = (x[..., 0::2], x[..., 1::2])
            c, s = (cos[..., 0::2], sin[..., 0::2])
            r = jnp.stack([x1 * c - x2 * s, x1 * s + x2 * c], axis=-1)
            return r.reshape(x.shape)

        def _rmsnorm(x, w):
            return x * jax.lax.rsqrt(jnp.mean(x * x, axis=-1, keepdims=True) + EPS) * w

        def _forward(x, w_q, b_q, w_down, b_down, w_up, b_up, w_o, b_o, qn_w, kn_w, gate_w, gate_b):
            b, t, _ = x.shape
            q = (x @ w_q + b_q).reshape(b, t, HEADS, HEAD_DIM)
            kv = (x @ w_down + b_down) @ w_up + b_up
            k = kv[..., :N_KV * HEAD_DIM].reshape(b, t, N_KV, HEAD_DIM)
            v = kv[..., N_KV * HEAD_DIM:].reshape(b, t, N_KV, HEAD_DIM)
            q = _rmsnorm(q, qn_w)
            k = _rmsnorm(k, kn_w)
            emb = _rope_emb(t, HEAD_DIM)
            q = _apply_rotary(q, emb)
            k = _apply_rotary(k, emb)
            k = jnp.repeat(k, KV_GROUPS, axis=2)
            v = jnp.repeat(v, KV_GROUPS, axis=2)
            q = q.transpose(0, 2, 1, 3)
            k = k.transpose(0, 2, 1, 3)
            v = v.transpose(0, 2, 1, 3)
            qs = jax.lax.stop_gradient(q[:, :SEL_HEADS, :, :SEL_DIM].astype(jnp.float32))
            ks = jax.lax.stop_gradient(k[:, :SEL_HEADS, :, :SEL_DIM].astype(jnp.float32))
            s = jnp.einsum('bhqd,bhkd->bhqk', qs, ks) / math.sqrt(SEL_DIM)
            tri = jnp.triu(jnp.ones((t, t), bool), 1)
            s = jnp.where(tri, -jnp.inf, s)
            idx = jax.lax.top_k(s, SEL_TOPK)[1]
            sel = jnp.zeros((b, SEL_HEADS, t, t), bool)
            bi = jnp.arange(b)[:, None, None, None]
            hi = jnp.arange(SEL_HEADS)[None, :, None, None]
            ti = jnp.arange(t)[None, None, :, None]
            sel = sel.at[bi, hi, ti, idx].set(True)
            sel = sel | jnp.eye(t, dtype=bool)[None, None]
            sel = sel & ~tri
            sel = jnp.any(sel, axis=1, keepdims=True)
            amask = jnp.where(sel, 0.0, -jnp.inf).astype(jnp.float32)
            scores = jnp.einsum('bhqd,bhkd->bhqk', q, k) / math.sqrt(HEAD_DIM)
            scores = jnp.tanh(scores / SOFTCAP) * SOFTCAP
            scores = scores + _alibi_bias(HEADS, t)[None] + amask
            attn = jax.nn.softmax(scores, axis=-1)
            y = jnp.einsum('bhqk,bhkd->bhqd', attn, v)
            gate = jax.nn.sigmoid(jnp.einsum('bhtd,hde->bhte', y, gate_w) + gate_b[None, :, None, :])
            y = (y * gate).transpose(0, 2, 1, 3).reshape(b, t, HEADS * HEAD_DIM)
            return y @ w_o + b_o
        key = jax.random.key(seed)
        ks = jax.random.split(key, 6)
        sd = 0.02
        return {'x': jax.random.normal(ks[0], (B, T, DIM), jnp.float32), 'w_q': jax.random.normal(ks[1], (DIM, HEADS * HEAD_DIM), jnp.float32) * sd, 'b_q': jnp.zeros((HEADS * HEAD_DIM,), jnp.float32), 'w_down': jax.random.normal(ks[2], (DIM, LATENT), jnp.float32) * sd, 'b_down': jnp.zeros((LATENT,), jnp.float32), 'w_up': jax.random.normal(ks[3], (LATENT, 2 * N_KV * HEAD_DIM), jnp.float32) * sd, 'b_up': jnp.zeros((2 * N_KV * HEAD_DIM,), jnp.float32), 'w_o': jax.random.normal(ks[4], (HEADS * HEAD_DIM, DIM), jnp.float32) * sd, 'b_o': jnp.zeros((DIM,), jnp.float32), 'qn_w': jnp.ones((HEAD_DIM,), jnp.float32), 'kn_w': jnp.ones((HEAD_DIM,), jnp.float32), 'gate_w': jax.random.normal(ks[5], (HEADS, HEAD_DIM, HEAD_DIM), jnp.float32) * (1.0 / math.sqrt(HEAD_DIM)), 'gate_b': jnp.zeros((HEADS, HEAD_DIM), jnp.float32)}
    _L1_attn_in = _L1_attn_setup()

    def _L1_ffn_setup():
        import math
        import jax, jax.numpy as jnp
        import numpy as np
        from jax import lax
        D = 256
        I = 128
        E = 32
        K = 4
        NG = 8
        TKG = 3
        NSH = 2
        SCALE = 2.5
        CF = 1.25
        B, S = (2, 256)

        def _router(x, router_w, e_bias):
            scores = jax.nn.sigmoid(x @ router_w.T)
            sc = scores + e_bias[None, :]
            T = x.shape[0]
            gs = sc.reshape(T, NG, E // NG)
            group_scores = lax.top_k(gs, 2)[0].sum(-1)
            _, gidx = lax.top_k(group_scores, TKG)
            gmask = jnp.zeros((T, NG), sc.dtype).at[jnp.arange(T)[:, None], gidx].set(1.0)
            smask = jnp.repeat(gmask, E // NG, axis=1)
            masked = jnp.where(smask > 0, sc, 0.0)
            _, topk_idx = lax.top_k(masked, K)
            topk_w = jnp.take_along_axis(scores, topk_idx, axis=1)
            topk_w = topk_w / (topk_w.sum(-1, keepdims=True) + 1e-20)
            topk_w = topk_w * SCALE
            return (topk_idx.astype(jnp.int32), topk_w)

        def _moe_forward(hidden_states, router_w, e_bias, W_gate, W_up, W_down, shared_gate, shared_up, shared_down):
            b, s, d = hidden_states.shape
            T = b * s
            C = int(math.ceil(CF * T / E))
            EC = E * C
            x = hidden_states.reshape(T, d)
            topk_idx, topk_w = _router(x, router_w, e_bias)
            expert_flat = topk_idx.reshape(-1)
            w_flat = topk_w.reshape(-1)
            tok_flat = jnp.repeat(jnp.arange(T, dtype=jnp.int32), K)
            sort_ix = jnp.argsort(expert_flat)
            e_sorted = expert_flat[sort_ix]
            tok_s = tok_flat[sort_ix]
            w_s = w_flat[sort_ix]
            counts = jnp.zeros(E, jnp.int32).at[e_sorted].add(1)
            group_start = jnp.concatenate([jnp.zeros(1, jnp.int32), jnp.cumsum(counts)[:-1].astype(jnp.int32)])
            pos = jnp.arange(T * K, dtype=jnp.int32) - group_start[e_sorted]
            valid = pos < C
            dest = e_sorted * C + jnp.where(valid, pos, 0)
            slots_token = jnp.zeros(EC, jnp.int32).at[dest].add(jnp.where(valid, tok_s, 0))
            slots_w = jnp.zeros(EC, w_s.dtype).at[dest].add(jnp.where(valid, w_s, 0.0))
            Xp = x[slots_token].reshape(E, C, d)
            G = jnp.einsum('ecd,edi->eci', Xp, W_gate)
            U = jnp.einsum('ecd,edi->eci', Xp, W_up)
            Y = jnp.einsum('eci,eid->ecd', jax.nn.silu(G) * U, W_down)
            Yf = Y.reshape(EC, d) * slots_w[:, None]
            out = jnp.zeros((T, d), x.dtype).at[slots_token].add(Yf)
            shared = jax.nn.silu(x @ shared_gate.T) * (x @ shared_up.T) @ shared_down.T
            return (out + shared).reshape(b, s, d)
        key = jax.random.key(seed)
        ks = jax.random.split(key, 8)

        def rn(k, shape, scale=0.02):
            return jax.random.normal(k, shape, jnp.float32) * scale
        return {'hidden_states': jax.random.normal(ks[0], (B, S, D), jnp.float32), 'router_w': rn(ks[1], (E, D)), 'e_bias': jnp.zeros((E,), jnp.float32), 'W_gate': rn(ks[2], (E, D, I)), 'W_up': rn(ks[3], (E, D, I)), 'W_down': rn(ks[4], (E, I, D)), 'shared_gate': rn(ks[5], (I * NSH, D)), 'shared_up': rn(ks[6], (I * NSH, D)), 'shared_down': rn(ks[7], (D, I * NSH))}
    _L1_ffn_in = _L1_ffn_setup()
    _d = {'L0_attn_hidden_states': _L0_attn_in['hidden_states'], 'L0_attn_in_proj_w': _L0_attn_in['in_proj_w'], 'L0_attn_conv_w': _L0_attn_in['conv_w'], 'L0_attn_conv_b': _L0_attn_in['conv_b'], 'L0_attn_A_log': _L0_attn_in['A_log'], 'L0_attn_D': _L0_attn_in['D'], 'L0_attn_dt_bias': _L0_attn_in['dt_bias'], 'L0_attn_norm_w': _L0_attn_in['norm_w'], 'L0_attn_out_proj_w': _L0_attn_in['out_proj_w'], 'L0_ffn_A': _L0_ffn_in['A'], 'L0_ffn_Bw': _L0_ffn_in['Bw'], 'L0_ffn_Wg': _L0_ffn_in['Wg'], 'L1_attn_w_q': _L1_attn_in['w_q'], 'L1_attn_b_q': _L1_attn_in['b_q'], 'L1_attn_w_down': _L1_attn_in['w_down'], 'L1_attn_b_down': _L1_attn_in['b_down'], 'L1_attn_w_up': _L1_attn_in['w_up'], 'L1_attn_b_up': _L1_attn_in['b_up'], 'L1_attn_w_o': _L1_attn_in['w_o'], 'L1_attn_b_o': _L1_attn_in['b_o'], 'L1_attn_qn_w': _L1_attn_in['qn_w'], 'L1_attn_kn_w': _L1_attn_in['kn_w'], 'L1_attn_gate_w': _L1_attn_in['gate_w'], 'L1_attn_gate_b': _L1_attn_in['gate_b'], 'L1_ffn_router_w': _L1_ffn_in['router_w'], 'L1_ffn_e_bias': _L1_ffn_in['e_bias'], 'L1_ffn_W_gate': _L1_ffn_in['W_gate'], 'L1_ffn_W_up': _L1_ffn_in['W_up'], 'L1_ffn_W_down': _L1_ffn_in['W_down'], 'L1_ffn_shared_gate': _L1_ffn_in['shared_gate'], 'L1_ffn_shared_up': _L1_ffn_in['shared_up'], 'L1_ffn_shared_down': _L1_ffn_in['shared_down']}
    _x0 = _d['L0_attn_hidden_states']
    _d['L0_attn_hidden_states'] = jax.random.normal(jax.random.fold_in(jax.random.key(seed), 1), (2, 512, 256), dtype=_x0.dtype)
    del _x0
    return _d

def reference(L0_attn_hidden_states, L0_attn_in_proj_w, L0_attn_conv_w, L0_attn_conv_b, L0_attn_A_log, L0_attn_D, L0_attn_dt_bias, L0_attn_norm_w, L0_attn_out_proj_w, L0_ffn_A, L0_ffn_Bw, L0_ffn_Wg, L1_attn_w_q, L1_attn_b_q, L1_attn_w_down, L1_attn_b_down, L1_attn_w_up, L1_attn_b_up, L1_attn_w_o, L1_attn_b_o, L1_attn_qn_w, L1_attn_kn_w, L1_attn_gate_w, L1_attn_gate_b, L1_ffn_router_w, L1_ffn_e_bias, L1_ffn_W_gate, L1_ffn_W_up, L1_ffn_W_down, L1_ffn_shared_gate, L1_ffn_shared_up, L1_ffn_shared_down):

    def _L0_attn_ref(hidden_states, in_proj_w, conv_w, conv_b, A_log, D, dt_bias, norm_w, out_proj_w):
        import jax, jax.numpy as jnp
        import numpy as np
        from jax import lax
        BATCH = 2
        SEQ = 256
        HID = 256
        EXPAND = 2
        INTER = EXPAND * HID
        HEADS = 64
        PDIM = INTER // HEADS
        NSTATE = 128
        G = 1
        HPG = HEADS // G
        KCONV = 4
        GTS = G * NSTATE
        CONV_DIM = INTER + 2 * GTS
        PROJ_DIM = 2 * INTER + 2 * GTS + HEADS
        EPS = 1e-05
        MUP = (0.25, 0.5, 0.5, 0.5, 1.0)

        def _mup_vector():
            return jnp.concatenate([jnp.full((INTER,), MUP[0], jnp.float32), jnp.full((INTER,), MUP[1], jnp.float32), jnp.full((GTS,), MUP[2], jnp.float32), jnp.full((GTS,), MUP[3], jnp.float32), jnp.full((HEADS,), MUP[4], jnp.float32)])

        def _forward(hidden_states, in_proj_w, conv_w, conv_b, A_log, D, dt_bias, norm_w, out_proj_w):
            b, l, _ = hidden_states.shape
            proj = hidden_states @ in_proj_w * _mup_vector()
            z = proj[..., :INTER]
            xBC = proj[..., INTER:INTER + CONV_DIM]
            dt = proj[..., INTER + CONV_DIM:]
            xBC_cl = jnp.swapaxes(xBC, 1, 2)
            conv = lax.conv_general_dilated(xBC_cl, conv_w[:, None, :], window_strides=(1,), padding=((KCONV - 1, 0),), feature_group_count=CONV_DIM)
            xBC = jax.nn.silu(jnp.swapaxes(conv + conv_b[None, :, None], 1, 2))
            x = xBC[..., :INTER].reshape(b, l, G, HPG, PDIM)
            Bm = xBC[..., INTER:INTER + GTS].reshape(b, l, G, NSTATE)
            Cm = xBC[..., INTER + GTS:].reshape(b, l, G, NSTATE)
            dt = jax.nn.softplus(dt + dt_bias)
            A = -jnp.exp(A_log)
            dA = jnp.exp(dt * A).reshape(b, l, G, HPG)
            dtx = dt.reshape(b, l, G, HPG)[..., None] * x

            def step(state, inp):
                dA_t, dtx_t, B_t, C_t = inp
                state = state * dA_t[..., None, None] + jnp.einsum('bgcp,bgn->bgcpn', dtx_t, B_t)
                y_t = jnp.einsum('bgn,bgcpn->bgcp', C_t, state)
                return (state, y_t)
            inputs = (jnp.moveaxis(dA, 1, 0), jnp.moveaxis(dtx, 1, 0), jnp.moveaxis(Bm, 1, 0), jnp.moveaxis(Cm, 1, 0))
            state0 = jnp.zeros((b, G, HPG, PDIM, NSTATE), hidden_states.dtype)
            _, ys = lax.scan(step, state0, inputs)
            y = jnp.moveaxis(ys, 0, 1) + D.reshape(1, 1, G, HPG, 1) * x
            y = y.reshape(b, l, INTER)
            yg = y.reshape(b, l, G, INTER // G)
            var = jnp.mean(jnp.square(yg), axis=-1, keepdims=True)
            yn = (yg * lax.rsqrt(var + EPS)).reshape(b, l, INTER) * norm_w
            out = yn * jax.nn.silu(z)
            return out @ out_proj_w
        return _forward(hidden_states, in_proj_w, conv_w, conv_b, A_log, D, dt_bias, norm_w, out_proj_w)

    def _L0_ffn_ref(x, A, Bw, Wg):
        import jax, jax.numpy as jnp
        import numpy as np
        B, S, D, R, E = (4, 256, 256, 64, 8)
        SCALING = 64.0 / 16.0
        bsz, seq_len, dim = x.shape
        xf = x.reshape(-1, dim)
        logits = jnp.einsum('nd,ed->ne', xf, Wg)
        prob = jax.nn.softmax(logits, axis=-1)
        gate = jnp.argmax(prob, axis=-1)
        prob_sel = jnp.take_along_axis(prob, gate[:, None], axis=1)
        mask = jax.nn.one_hot(gate, E, dtype=xf.dtype)
        h = jnp.einsum('nd,erd->ner', xf, A)
        h = h * mask[:, :, None]
        y = jnp.einsum('ner,eor->no', h, Bw)
        y = y * SCALING * prob_sel
        return y.reshape(bsz, seq_len, -1)

    def _L1_attn_ref(x, w_q, b_q, w_down, b_down, w_up, b_up, w_o, b_o, qn_w, kn_w, gate_w, gate_b):
        import math
        import jax, jax.numpy as jnp
        import numpy as np
        B, T, DIM = (2, 256, 256)
        HEADS, HEAD_DIM = (16, 128)
        KV_GROUPS = 4
        N_KV = HEADS // KV_GROUPS
        LATENT = 64
        SEL_TOPK, SEL_HEADS, SEL_DIM = (64, 1, 64)
        SOFTCAP = 30.0
        EPS = 1e-06

        def _alibi_slopes(n):

            def pot(p):
                start = 2.0 ** (-2.0 ** (-(math.log2(p) - 3)))
                return [start * start ** i for i in range(p)]
            if math.log2(n).is_integer():
                return pot(n)
            cp = 2 ** int(math.floor(math.log2(n)))
            s = pot(cp)
            s += _alibi_slopes(2 * cp)[0::2][:n - cp]
            return s

        def _alibi_bias(h, t):
            slopes = jnp.asarray(_alibi_slopes(h), jnp.float32)
            pos = jnp.arange(t)
            dist = jnp.clip(pos[:, None] - pos[None, :], 0, None).astype(jnp.float32)
            return -slopes[:, None, None] * dist

        def _rope_emb(t, d):
            inv = 1.0 / 10000.0 ** (jnp.arange(0, d, 2, dtype=jnp.float32) / d)
            f = jnp.arange(t, dtype=jnp.float32)[:, None] * inv[None, :]
            return jnp.concatenate([f, f], axis=-1)

        def _apply_rotary(x, emb):
            cos = jnp.cos(emb)[None, :, None, :]
            sin = jnp.sin(emb)[None, :, None, :]
            x1, x2 = (x[..., 0::2], x[..., 1::2])
            c, s = (cos[..., 0::2], sin[..., 0::2])
            r = jnp.stack([x1 * c - x2 * s, x1 * s + x2 * c], axis=-1)
            return r.reshape(x.shape)

        def _rmsnorm(x, w):
            return x * jax.lax.rsqrt(jnp.mean(x * x, axis=-1, keepdims=True) + EPS) * w

        def _forward(x, w_q, b_q, w_down, b_down, w_up, b_up, w_o, b_o, qn_w, kn_w, gate_w, gate_b):
            b, t, _ = x.shape
            q = (x @ w_q + b_q).reshape(b, t, HEADS, HEAD_DIM)
            kv = (x @ w_down + b_down) @ w_up + b_up
            k = kv[..., :N_KV * HEAD_DIM].reshape(b, t, N_KV, HEAD_DIM)
            v = kv[..., N_KV * HEAD_DIM:].reshape(b, t, N_KV, HEAD_DIM)
            q = _rmsnorm(q, qn_w)
            k = _rmsnorm(k, kn_w)
            emb = _rope_emb(t, HEAD_DIM)
            q = _apply_rotary(q, emb)
            k = _apply_rotary(k, emb)
            k = jnp.repeat(k, KV_GROUPS, axis=2)
            v = jnp.repeat(v, KV_GROUPS, axis=2)
            q = q.transpose(0, 2, 1, 3)
            k = k.transpose(0, 2, 1, 3)
            v = v.transpose(0, 2, 1, 3)
            qs = jax.lax.stop_gradient(q[:, :SEL_HEADS, :, :SEL_DIM].astype(jnp.float32))
            ks = jax.lax.stop_gradient(k[:, :SEL_HEADS, :, :SEL_DIM].astype(jnp.float32))
            s = jnp.einsum('bhqd,bhkd->bhqk', qs, ks) / math.sqrt(SEL_DIM)
            tri = jnp.triu(jnp.ones((t, t), bool), 1)
            s = jnp.where(tri, -jnp.inf, s)
            idx = jax.lax.top_k(s, SEL_TOPK)[1]
            sel = jnp.zeros((b, SEL_HEADS, t, t), bool)
            bi = jnp.arange(b)[:, None, None, None]
            hi = jnp.arange(SEL_HEADS)[None, :, None, None]
            ti = jnp.arange(t)[None, None, :, None]
            sel = sel.at[bi, hi, ti, idx].set(True)
            sel = sel | jnp.eye(t, dtype=bool)[None, None]
            sel = sel & ~tri
            sel = jnp.any(sel, axis=1, keepdims=True)
            amask = jnp.where(sel, 0.0, -jnp.inf).astype(jnp.float32)
            scores = jnp.einsum('bhqd,bhkd->bhqk', q, k) / math.sqrt(HEAD_DIM)
            scores = jnp.tanh(scores / SOFTCAP) * SOFTCAP
            scores = scores + _alibi_bias(HEADS, t)[None] + amask
            attn = jax.nn.softmax(scores, axis=-1)
            y = jnp.einsum('bhqk,bhkd->bhqd', attn, v)
            gate = jax.nn.sigmoid(jnp.einsum('bhtd,hde->bhte', y, gate_w) + gate_b[None, :, None, :])
            y = (y * gate).transpose(0, 2, 1, 3).reshape(b, t, HEADS * HEAD_DIM)
            return y @ w_o + b_o
        return _forward(x, w_q, b_q, w_down, b_down, w_up, b_up, w_o, b_o, qn_w, kn_w, gate_w, gate_b)

    def _L1_ffn_ref(hidden_states, router_w, e_bias, W_gate, W_up, W_down, shared_gate, shared_up, shared_down):
        import math
        import jax, jax.numpy as jnp
        import numpy as np
        from jax import lax
        D = 256
        I = 128
        E = 32
        K = 4
        NG = 8
        TKG = 3
        NSH = 2
        SCALE = 2.5
        CF = 1.25
        B, S = (2, 256)

        def _router(x, router_w, e_bias):
            scores = jax.nn.sigmoid(x @ router_w.T)
            sc = scores + e_bias[None, :]
            T = x.shape[0]
            gs = sc.reshape(T, NG, E // NG)
            group_scores = lax.top_k(gs, 2)[0].sum(-1)
            _, gidx = lax.top_k(group_scores, TKG)
            gmask = jnp.zeros((T, NG), sc.dtype).at[jnp.arange(T)[:, None], gidx].set(1.0)
            smask = jnp.repeat(gmask, E // NG, axis=1)
            masked = jnp.where(smask > 0, sc, 0.0)
            _, topk_idx = lax.top_k(masked, K)
            topk_w = jnp.take_along_axis(scores, topk_idx, axis=1)
            topk_w = topk_w / (topk_w.sum(-1, keepdims=True) + 1e-20)
            topk_w = topk_w * SCALE
            return (topk_idx.astype(jnp.int32), topk_w)

        def _moe_forward(hidden_states, router_w, e_bias, W_gate, W_up, W_down, shared_gate, shared_up, shared_down):
            b, s, d = hidden_states.shape
            T = b * s
            C = int(math.ceil(CF * T / E))
            EC = E * C
            x = hidden_states.reshape(T, d)
            topk_idx, topk_w = _router(x, router_w, e_bias)
            expert_flat = topk_idx.reshape(-1)
            w_flat = topk_w.reshape(-1)
            tok_flat = jnp.repeat(jnp.arange(T, dtype=jnp.int32), K)
            sort_ix = jnp.argsort(expert_flat)
            e_sorted = expert_flat[sort_ix]
            tok_s = tok_flat[sort_ix]
            w_s = w_flat[sort_ix]
            counts = jnp.zeros(E, jnp.int32).at[e_sorted].add(1)
            group_start = jnp.concatenate([jnp.zeros(1, jnp.int32), jnp.cumsum(counts)[:-1].astype(jnp.int32)])
            pos = jnp.arange(T * K, dtype=jnp.int32) - group_start[e_sorted]
            valid = pos < C
            dest = e_sorted * C + jnp.where(valid, pos, 0)
            slots_token = jnp.zeros(EC, jnp.int32).at[dest].add(jnp.where(valid, tok_s, 0))
            slots_w = jnp.zeros(EC, w_s.dtype).at[dest].add(jnp.where(valid, w_s, 0.0))
            Xp = x[slots_token].reshape(E, C, d)
            G = jnp.einsum('ecd,edi->eci', Xp, W_gate)
            U = jnp.einsum('ecd,edi->eci', Xp, W_up)
            Y = jnp.einsum('eci,eid->ecd', jax.nn.silu(G) * U, W_down)
            Yf = Y.reshape(EC, d) * slots_w[:, None]
            out = jnp.zeros((T, d), x.dtype).at[slots_token].add(Yf)
            shared = jax.nn.silu(x @ shared_gate.T) * (x @ shared_up.T) @ shared_down.T
            return (out + shared).reshape(b, s, d)
        return _moe_forward(hidden_states, router_w, e_bias, W_gate, W_up, W_down, shared_gate, shared_up, shared_down)
    x = L0_attn_hidden_states
    x = _layernorm(x + _L0_attn_ref(x, L0_attn_in_proj_w, L0_attn_conv_w, L0_attn_conv_b, L0_attn_A_log, L0_attn_D, L0_attn_dt_bias, L0_attn_norm_w, L0_attn_out_proj_w), axis=-1)
    x = _layernorm(x + _L0_ffn_ref(x, L0_ffn_A, L0_ffn_Bw, L0_ffn_Wg), axis=-1)
    x = _layernorm(x + _L1_attn_ref(x, L1_attn_w_q, L1_attn_b_q, L1_attn_w_down, L1_attn_b_down, L1_attn_w_up, L1_attn_b_up, L1_attn_w_o, L1_attn_b_o, L1_attn_qn_w, L1_attn_kn_w, L1_attn_gate_w, L1_attn_gate_b), axis=-1)
    x = _layernorm(x + _L1_ffn_ref(x, L1_ffn_router_w, L1_ffn_e_bias, L1_ffn_W_gate, L1_ffn_W_up, L1_ffn_W_down, L1_ffn_shared_gate, L1_ffn_shared_up, L1_ffn_shared_down), axis=-1)
    return x

_drawn_inputs = setup_inputs


def setup_inputs(seed=0):
    import zlib

    import numpy as np

    out = dict(_drawn_inputs(seed))
    spreads = {'L0_attn_conv_b': (0.0, 0.415),
     'L0_attn_D': (1.0, 0.6),
     'L0_attn_norm_w': (1.0, 0.6),
     'L1_attn_b_q': (0.0, 0.8),
     'L1_attn_b_down': (0.0, 0.8),
     'L1_attn_b_up': (0.0, 0.1),
     'L1_attn_b_o': (0.0, 0.1),
     'L1_attn_qn_w': (1.0, 0.6),
     'L1_attn_kn_w': (1.0, 0.6),
     'L1_attn_gate_b': (0.0, 0.8),
     'L1_ffn_e_bias': (0.0, 0.8)}
    factors = {'L0_attn_in_proj_w': 2.896,
     'L0_attn_conv_w': 5.17,
     'L0_attn_A_log': 8.0,
     'L0_attn_dt_bias': 8.0,
     'L0_attn_out_proj_w': 2.908,
     'L1_attn_w_q': 7.983,
     'L1_attn_w_down': 4.082,
     'L1_attn_w_up': 3.508,
     'L1_attn_gate_w': 8.0,
     'L1_ffn_router_w': 7.89,
     'L1_ffn_W_gate': 7.534,
     'L1_ffn_W_up': 7.4,
     'L1_ffn_W_down': 7.438,
     'L1_ffn_shared_gate': 3.397,
     'L1_ffn_shared_up': 3.362,
     'L1_ffn_shared_down': 3.366}
    for name, (base, spread) in spreads.items():
        noise = np.random.default_rng([zlib.crc32(name.encode()), seed]).standard_normal(out[name].shape)
        drawn = base * np.exp(spread * noise) if base else spread * noise
        out[name] = jnp.asarray(drawn.astype(out[name].dtype))
    for name, factor in factors.items():
        out[name] = (out[name] * factor).astype(out[name].dtype)
    return out
```

```python
from contextlib import ExitStack

import numpy as np

import concourse.bass as bass
from concourse import mybir

F32 = mybir.dt.float32
U32 = mybir.dt.uint32
ALU = mybir.AluOpType
ACT = mybir.ActivationFunctionType
AX = mybir.AxisListType

P = 128
BATCH, SEQ, DM = 2, 512, 256
NT = BATCH * SEQ
TILES = NT // P
HALVES = NT // 512
KD = DM // P
TPH = TILES // HALVES

INTER, HEADS, PDIM, NSTATE, KCONV = 512, 64, 8, 128, 4
CONV = INTER + 2 * NSTATE
CT = CONV // P
PROJ = 2 * INTER + 2 * NSTATE + HEADS
Q = 32
G = P // Q
CHUNKS = SEQ // Q
HQ = 16
RING = 8

LE, LR, LSCALE = 8, 64, 64.0 / 16.0

AH, HD, NKV, LATENT = 16, 128, 4, 64
KVG = AH // NKV
QKH = AH + NKV
SEL_TOPK, SEL_DIM = 64, 64
SOFTCAP = 30.0
SLOPE = [2.0 ** (-8.0 * (h + 1) / AH) for h in range(AH)]
KEY_COL = [0, 512, 1024, 896]
NCOL = 1280
VW = HD + 1
LATER, TAKEN, FAR = -1e30, -3e38, -1e30

NE, NG, TKG, TOPK, MSCALE = 32, 8, 3, 4, 2.5
CAP = -(-5 * NT // (4 * NE))
SLOTS = NE * CAP
ST = SLOTS // P
EG = 8
EI = 128

LN_EPS = 1e-5
SEMAPHORES = 256


class Signal:

    def __init__(self, ctx, nc, name):
        self.sem = ctx.enter_context(nc.semaphore(name))
        self.n = 0

    def by(self, ins):
        ins.then_inc(self.sem, 1)
        self.n += 1

    def then_wait(self, eng, ins):
        self.by(ins)
        eng.wait_ge(self.sem, self.n)


def spread(ap, axis, n):
    a = ap.unsqueeze(axis)
    shape = list(a.shape)
    shape[axis] = n
    return a.broadcast_to(shape)


class Memory:
    pass


class Space:

    def __init__(self, ap):
        self.ap, self.at = ap, 0

    def take(self, parts, *shape):
        n = int(np.prod(shape))
        assert self.at + n <= self.ap.shape[1], (self.at, n)
        piece = self.ap[0:parts, self.at:self.at + n]
        self.at += n
        names = "abcd"[:len(shape)]
        if len(shape) > 1:
            piece = piece.rearrange(f"p ({' '.join(names)}) -> p {' '.join(names)}",
                                    **{k: v for k, v in zip(names[1:], shape[1:])})
        return piece


def rows(dram):
    return dram.rearrange("(i p) d -> p i d", p=P)


def k_tiles(dram):
    return dram.rearrange("(k p) n -> p k n", p=P)


def transpose_rows(pe, nc, m, bank, ready, done):
    for h in range(HALVES):
        for k in range(KD):
            for j in range(TPH):
                i = h * TPH + j
                ready(i)
                last = nc.tensor.transpose(m.ps[:, bank + h * KD + k, P * j:P * (j + 1)],
                                           m.x[:, i, P * k:P * (k + 1)], m.ident[:, :])
            done.by(last)


def copy_transposed(eng, copy, m, bank, transposed, copied):
    for h in range(HALVES):
        for k in range(KD):
            n = h * KD + k
            eng.wait_ge(transposed.sem, n + 1)
            copied.by(copy(m.xT[:, k, 512 * h:512 * (h + 1)], m.ps[:, bank + n, :]))


def project_and_convolve(nc, m, a):
    with ExitStack() as ctx:
        sig = lambda name: Signal(ctx, nc, "proj_" + name)
        sb = lambda name, shape: ctx.enter_context(nc.sbuf_tensor("proj_" + name, shape, F32))
        raw = sb("raw", [P, CT, BATCH, KCONV - 1 + SEQ])
        acc = sb("acc", [P, 2, NT])
        lin = sb("lin", [P, 2, NT])
        th = sb("th", [P, 2, NT])
        hb = sb("hb", [P, CT])
        al = sb("al", [HEADS, 2])
        dtb = sb("dtb", [HEADS, 1])
        u = sb("u", [HEADS, NT])
        e = sb("e", [HEADS, NT])
        w = sb("w", [HEADS, NT])
        lw = sb("lw", [HEADS, NT])
        d1 = sb("d1", [HEADS, NT])
        eq = sb("eq", [HEADS, NT])

        x_in, w_in, ct_in = sig("x_in"), sig("w_in"), sig("ct_in")
        small_in = m.small_in
        xt_ps, xt_sb = sig("xt_ps"), sig("xt_sb")
        proj_ps, raw_sb, dt_sb = sig("proj_ps"), sig("raw_sb"), sig("dt_sb")
        pad_zero, dve, act = sig("pad_zero"), sig("dve1"), sig("act1")
        e_ready, w_ready, lw_ready, dt_ready, da_ready = (sig(n) for n in
                                                          ("e_ready", "w_ready", "lw_ready", "dt_ready", "da_ready"))
        daz_ready, daz_out, dac_in = sig("daz_ready"), sig("daz_out"), sig("dac_in")
        a_ready, conv_done, lin_th, silu_done, hb_ready = (sig(n) for n in
                                                           ("a_ready", "conv_done", "lin_th", "silu_done", "hb_ready"))
        order = [4, 5, 0, 1, 2, 3]
        W_DT = PROJ - HEADS

        with nc.Block() as block:
            @block.sync
            def _(sp):
                sp.dma_start(m.ident[:, :], a["c_ident"]).then_inc(x_in.sem, 16)
                for h in range(HALVES):
                    sp.dma_start(m.x[:, TPH * h:TPH * (h + 1), :],
                                 rows(a["x"])[:, TPH * h:TPH * (h + 1), :]).then_inc(x_in.sem, 16)
                sp.dma_start(m.w_in[:, :, INTER:PROJ], k_tiles(a["L0_attn_in_proj_w"])[:, :, INTER:PROJ]
                             ).then_inc(w_in.sem, 16)
                sp.dma_start(m.w_in[:, :, 0:INTER], k_tiles(a["L0_attn_in_proj_w"])[:, :, 0:INTER]
                             ).then_inc(m.wz_in.sem, 16)
                sp.dma_start(m.w_out[:, :, :], k_tiles(a["L0_attn_out_proj_w"])).then_inc(m.late_in.sem, 16)
                sp.dma_start(m.norm_w[:, :], a["L0_attn_norm_w"].rearrange("(k p) -> p k", p=P),
                             allow_slow_non_contiguous=True).then_inc(m.late_in.sem, 16)
                load_lora(nc, m, a, sp)
                sp.wait_ge(daz_ready.sem, 1)
                sp.dma_start(m.da_dram, w[:, :]).then_inc(daz_out.sem, 16)
                sp.wait_ge(daz_out.sem, 16)
                sp.dma_start(m.da_chunk[:, :, :], m.da_dram.rearrange("h (c t) -> c h t", t=Q),
                             allow_slow_non_contiguous=True).then_inc(dac_in.sem, 16)
                sp.wait_ge(dac_in.sem, 16)

            @block.gpsimd
            def _(pool):
                pool.dma_start(m.conv_w[:, :, :], a["L0_attn_conv_w"].rearrange("(c p) k -> p c k", p=P),
                               allow_slow_non_contiguous=True).then_inc(small_in.sem, 16)
                pool.dma_start(m.conv_b[:, :], a["L0_attn_conv_b"].rearrange("(c p) -> p c", p=P),
                               allow_slow_non_contiguous=True).then_inc(small_in.sem, 16)
                pool.dma_start(al[:, 0:1], a["L0_attn_A_log"].unsqueeze(1),
                               allow_slow_non_contiguous=True).then_inc(small_in.sem, 16)
                pool.dma_start(dtb[:, :], a["L0_attn_dt_bias"].unsqueeze(1),
                               allow_slow_non_contiguous=True).then_inc(small_in.sem, 16)
                pool.dma_start(m.d_row[:, :], a["L0_attn_D"].partition_broadcast(P)).then_inc(m.const_in.sem, 16)
                for t, name in ((m.eye_q[:, :], "c_eye_q"), (m.sel_last[:, :, :], "c_sel_last"),
                                (m.in_chunk[:, :], "c_in_chunk"), (m.sel_chunk[:, :, :], "c_sel_chunk")):
                    pool.dma_start(t, a[name]).then_inc(m.const_in.sem, 16)
                pad_zero.by(nc.gpsimd.memset(raw[:, :, :, 0:KCONV - 1], 0.0))
                pad_zero.by(nc.gpsimd.memset(m.half[:, :], -0.5))
                pad_zero.by(nc.gpsimd.memset(d1[:, :], 0.0))

            @block.tensor
            def _(pe):
                pe.wait_ge(x_in.sem, 48)
                transpose_rows(pe, nc, m, 0, lambda i: None, xt_ps)
                pe.wait_ge(w_in.sem, 16)
                pe.wait_ge(xt_sb.sem, 4)
                n = 0
                for h in range(HALVES):
                    for k in range(KD):
                        last = nc.tensor.matmul(m.ps[0:HEADS, 4 + n, :], m.w_in[:, k, W_DT:PROJ],
                                                m.xT[:, k, 512 * h:512 * (h + 1)], start=k == 0, stop=k == KD - 1)
                    proj_ps.by(last)
                    n += 1
                for ct in order:
                    for h in range(HALVES):
                        if n >= 8:
                            if n < 10:
                                pe.wait_ge(dt_sb.sem, n - 7)
                            else:
                                pe.wait_ge(raw_sb.sem, n - 9)
                        for k in range(KD):
                            last = nc.tensor.matmul(m.ps[:, (4 + n) % 8, :],
                                                    m.w_in[:, k, INTER + P * ct:INTER + P * (ct + 1)],
                                                    m.xT[:, k, 512 * h:512 * (h + 1)], start=k == 0, stop=k == KD - 1)
                        proj_ps.by(last)
                        n += 1

            @block.scalar
            def _(sc):
                sc.wait_ge(small_in.sem, 64)
                act.then_wait(sc, nc.scalar.activation(al[:, 1:2], al[:, 0:1], ACT.Exp))
                a_ready.by(nc.scalar.mul(al[:, 0:1], al[:, 1:2], -1.0))
                hb_ready.by(nc.scalar.mul(hb[:, :], m.conv_b[:, :], 0.5))
                sc.wait_ge(dt_sb.sem, 2)
                act.then_wait(sc, nc.scalar.activation(e[:, :], u[:, :], ACT.Abs))
                e_ready.by(nc.scalar.activation(e[:, :], e[:, :], ACT.Exp, scale=-1.0))
                sc.wait_ge(pad_zero.sem, 1)

                def copy_raw(n):
                    ct, h = order[n // 2], n % 2
                    sc.wait_ge(proj_ps.sem, n + 3)
                    raw_sb.by(nc.scalar.activation(raw[:, ct, h, KCONV - 1:], m.ps[:, (6 + n) % 8, :],
                                                   ACT.Copy, scale=0.5))

                for n in range(4):
                    copy_raw(n)
                sc.wait_ge(w_ready.sem, 1)
                lw_ready.by(nc.scalar.activation(lw[:, :], w[:, :], ACT.Ln))
                for n in range(4, 12):
                    copy_raw(n)
                sc.wait_ge(dt_ready.sem, 1)
                sc.wait_ge(a_ready.sem, 1)
                da_ready.by(nc.scalar.activation(w[:, :], m.dtT[:, :], ACT.Exp, scale=al[:, 0:1]))
                sc.wait_ge(hb_ready.sem, 1)
                for n, ct in enumerate(order):
                    sc.wait_ge(conv_done.sem, n + 1)
                    if n >= 2:
                        sc.wait_ge(silu_done.sem, n - 1)
                    nc.scalar.activation(lin[:, n % 2, :], acc[:, n % 2, :], ACT.Identity, scale=0.5,
                                         bias=hb[:, ct:ct + 1])
                    lin_th.by(nc.scalar.activation(th[:, n % 2, :], acc[:, n % 2, :], ACT.Tanh, scale=0.5,
                                                   bias=hb[:, ct:ct + 1]))

            @block.vector
            def _(v):
                copy_transposed(v, nc.vector.tensor_copy, m, 0, xt_ps, xt_sb)
                v.wait_ge(small_in.sem, 64)
                for h in range(HALVES):
                    v.wait_ge(proj_ps.sem, h + 1)
                    dt_sb.by(nc.vector.tensor_scalar(u[:, 512 * h:512 * (h + 1)], m.ps[0:HEADS, 4 + h, :],
                                                     dtb[:, 0:1], None, ALU.add))
                v.wait_ge(e_ready.sem, 1)
                w_ready.then_wait(v, nc.vector.tensor_scalar(w[:, :], e[:, :], 1.0, None, ALU.add))
                v.wait_ge(pad_zero.sem, 3)

                def convolve(n):
                    ct = order[n]
                    v.wait_ge(raw_sb.sem, 2 * n + 2)
                    out = acc[:, n % 2, :].rearrange("p (b t) -> p b t", b=BATCH)
                    if n >= 2:
                        v.wait_ge(lin_th.sem, n - 1)
                    dve.then_wait(v, nc.vector.tensor_scalar(out, raw[:, ct, :, 0:SEQ], m.conv_w[:, ct, 0:1], None,
                                                             ALU.mult))
                    for k in range(1, KCONV):
                        last = nc.vector.scalar_tensor_tensor(out, raw[:, ct, :, k:k + SEQ], m.conv_w[:, ct, k:k + 1],
                                                              out, ALU.mult, ALU.add)
                        (conv_done if k == KCONV - 1 else dve).then_wait(v, last)

                def finish_silu(n):
                    v.wait_ge(lin_th.sem, n + 1)
                    silu_done.by(nc.vector.scalar_tensor_tensor(m.xc[:, order[n], :], th[:, n % 2, :], 1.0,
                                                                lin[:, n % 2, :], ALU.add, ALU.mult))

                convolve(0)
                v.wait_ge(lw_ready.sem, 1)
                dve.then_wait(v, nc.vector.tensor_scalar(w[:, :], w[:, :], -1.0, None, ALU.add))
                dve.then_wait(v, nc.vector.tensor_scalar(eq[:, :], w[:, :], 0.0, None, ALU.is_equal))
                nc.vector.tensor_tensor(lw[:, :], lw[:, :], eq[:, :], ALU.add).then_inc(dve.sem, 1)
                dve.n += 1
                dve.then_wait(v, nc.vector.tensor_tensor(w[:, :], w[:, :], eq[:, :], ALU.add))
                dve.then_wait(v, nc.vector.reciprocal(w[:, :], w[:, :]))
                dve.then_wait(v, nc.vector.tensor_tensor(lw[:, :], lw[:, :], w[:, :], ALU.mult))
                dve.then_wait(v, nc.vector.tensor_tensor(lw[:, :], lw[:, :], e[:, :], ALU.mult))
                dt_ready.by(nc.vector.scalar_tensor_tensor(m.dtT[:, :], u[:, :], 0.0, lw[:, :], ALU.max, ALU.add))
                convolve(1)
                v.wait_ge(da_ready.sem, 1)
                starts = lambda t: t[:, :].rearrange("h (c t) -> h c t", t=Q)[:, :, 0:1]
                dve.then_wait(v, nc.vector.tensor_copy(starts(d1), starts(w)))
                daz_ready.then_wait(v, nc.vector.memset(starts(w), 0.0))
                dve.by(nc.vector.tensor_tensor_scan(m.sinceT[:, :], w[:, :], d1[:, :], 0.0, ALU.mult, ALU.add))
                for n in range(2, CT):
                    finish_silu(n - 2)
                    convolve(n)
                finish_silu(CT - 2)
                finish_silu(CT - 1)


def within_chunks(nc, m, a):
    with ExitStack() as ctx:
        sig = lambda name: Signal(ctx, nc, "chunk_" + name)
        sb = lambda name, shape: ctx.enter_context(nc.sbuf_tensor("chunk_" + name, shape, F32))
        eye = sb("eye", [P, HQ, Q])
        gram = sb("gram", [P, 2, Q])
        dec = sb("dec", [P, 2, HEADS, Q])
        mix = sb("mix", [P, 2, HEADS, Q])
        dtx = sb("dtx", [P, 2, HEADS, PDIM])
        dtd = sb("dtd", [P, 2, HEADS, G, PDIM])
        dt_row = sb("dt_row", [P, TILES, HEADS])

        b_ps, b_sb, row_ps, row_sb = sig("b_ps"), sig("b_sb"), sig("row_ps"), sig("row_sb")
        x_ps, x_sb, gram_ps, gram_sb = sig("x_ps"), sig("x_sb"), sig("gram_ps"), sig("gram_sb")
        da_ps, scanned, mixed, dtx_ready, spreaded = (sig(n) for n in ("da_ps", "scanned", "mixed", "dtx_ready",
                                                                       "spreaded"))
        intra_ps, intra_sb, dtf_ready, eye_ready = (sig(n) for n in ("intra_ps", "intra_sb", "dtf_ready", "eye_ready"))
        NQ = HEADS // HQ
        with nc.Block() as block:
            @block.tensor
            def _(pe):
                for i in range(TILES):
                    last = nc.tensor.transpose(m.ps[:, 4 + i // 4, P * (i % 4):P * (i % 4 + 1)],
                                               m.xc[:, 4, P * i:P * (i + 1)], m.ident[:, :])
                b_ps.by(last)
                for bank, src in ((6, m.dtT), (7, m.sinceT)):
                    for i in range(TILES):
                        last = nc.tensor.transpose(m.ps[:, bank, HEADS * i:HEADS * (i + 1)],
                                                   src[:, P * i:P * (i + 1)], m.ident[0:HEADS, 0:HEADS])
                row_ps.by(last)
                pe.wait_ge(m.const_in.sem, 16 * 5)

                def feed(i):
                    if i >= 1:
                        pe.wait_ge(x_sb.sem, i)
                        pe.wait_ge(gram_sb.sem, i)
                    for c in range(4):
                        last = nc.tensor.transpose(m.ps[:, 2, P * c:P * (c + 1)], m.xc[:, c, P * i:P * (i + 1)],
                                                   m.ident[:, :])
                    x_ps.by(last)
                    t = slice(P * i, P * (i + 1))
                    gram_ps.by(nc.tensor.matmul(m.ps[:, 3, 0:P], m.xc[:, 4, t], m.xc[:, 5, t], start=True, stop=True))
                    for q in range(NQ):
                        n = NQ * i + q
                        if n >= 2:
                            pe.wait_ge(scanned.sem, n - 1)
                        da_ps.by(nc.tensor.matmul(m.ps[:, n % 2, :], m.sel_chunk[:, i, :],
                                                  m.da_chunk[:, HQ * q:HQ * (q + 1), :].rearrange("c h t -> c (h t)"),
                                                  start=True, stop=True))

                feed(0)
                pe.wait_ge(b_sb.sem, 2)
                pe.wait_ge(row_sb.sem, 2)
                for i in range(TILES):
                    if i + 1 < TILES:
                        feed(i + 1)
                    pe.wait_ge(mixed.sem, i + 1)
                    pe.wait_ge(spreaded.sem, i + 1)
                    if i >= 1:
                        pe.wait_ge(intra_sb.sem, G * i)
                    for h in range(HEADS):
                        last = nc.tensor.matmul(m.ps[0:Q, 4 + h // HQ, (G * PDIM) * (h % HQ):(G * PDIM) * (h % HQ + 1)],
                                                mix[:, i % 2, h, :],
                                                dtd[:, i % 2, h, :, :].rearrange("p g d -> p (g d)"),
                                                start=True, stop=True)
                    intra_ps.by(last)

            @block.scalar
            def _(sc):
                sc.wait_ge(b_ps.sem, 1)
                for j in range(2):
                    b_sb.by(nc.scalar.copy(m.b_row[:, 4 * j:4 * j + 4, :].rearrange("p i n -> p (i n)"),
                                           m.ps[:, 4 + j, :]))
                sc.wait_ge(row_ps.sem, 1)
                row_sb.by(nc.scalar.copy(dt_row[:, :, :].rearrange("p i h -> p (i h)"), m.ps[:, 6, :]))
                row_sb.by(nc.scalar.copy(m.since_row[:, :, :].rearrange("p i h -> p (i h)"), m.ps[:, 7, :]))

                def intra_out(i):
                    sc.wait_ge(intra_ps.sem, i + 1)
                    src = m.ps[0:Q, 4:8, :].rearrange("t b (h g d) -> t b h g d", g=G, d=PDIM)
                    for g in range(G):
                        dst = m.xc[Q * g:Q * (g + 1), 0:4, P * i:P * (i + 1)]
                        intra_sb.by(nc.scalar.copy(dst.rearrange("t b (h d) -> t b h d", d=PDIM), src[:, :, :, g, :]))

                for i in range(TILES):
                    sc.wait_ge(x_ps.sem, i + 1)
                    x_sb.by(nc.scalar.copy(m.x_row[:, i, :], m.ps[:, 2, :]))
                    sc.wait_ge(gram_ps.sem, i + 1)
                    if i >= 2:
                        sc.wait_ge(mixed.sem, i - 1)
                    for g in range(G):
                        last = nc.scalar.copy(gram[Q * g:Q * (g + 1), i % 2, :],
                                              m.ps[Q * g:Q * (g + 1), 3, Q * g:Q * (g + 1)])
                    gram_sb.by(last)
                    if i >= 1:
                        intra_out(i - 1)
                intra_out(TILES - 1)

            @block.vector
            def _(v):
                v.wait_ge(m.const_in.sem, 16 * 5)
                eye_ready.then_wait(v, nc.vector.tensor_copy(eye[:, :, :], spread(m.eye_q[:, :], 1, HQ)))
                v.wait_ge(row_sb.sem, 2)
                for i in range(TILES):
                    v.wait_ge(x_sb.sem, i + 1)
                    if i >= 2:
                        v.wait_ge(spreaded.sem, i - 1)
                    dtx_ready.by(nc.vector.tensor_tensor(
                        dtx[:, i % 2, :, :], m.x_row[:, i, :].rearrange("p (h d) -> p h d", d=PDIM),
                        spread(dt_row[:, i, :], 2, PDIM), ALU.mult))
                    if i >= 2:
                        v.wait_ge(mixed.sem, i - 1)
                    for q in range(NQ):
                        v.wait_ge(da_ps.sem, NQ * i + q + 1)
                        scanned.by(nc.vector.tensor_tensor_scan(
                            dec[:, i % 2, HQ * q:HQ * (q + 1), :].rearrange("p h t -> p (h t)"),
                            m.ps[:, (NQ * i + q) % 2, :], eye[:, :, :].rearrange("p h t -> p (h t)"),
                            0.0, ALU.mult, ALU.add))
                    v.wait_ge(scanned.sem, NQ * (i + 1))
                    dtf_ready.by(nc.vector.tensor_tensor(m.dt_end[:, i, :, :], dtx[:, i % 2, :, :],
                                                         spread(dec[:, i % 2, :, Q - 1], 2, PDIM), ALU.mult))

            @block.gpsimd
            def _(pool):
                for i in range(TILES):
                    pool.wait_ge(dtx_ready.sem, i + 1)
                    if i >= 2:
                        pool.wait_ge(intra_ps.sem, i - 1)
                    for g in range(G):
                        last = nc.gpsimd.tensor_scalar(dtd[:, i % 2, :, g, :], dtx[:, i % 2, :, :],
                                                       m.in_chunk[:, g:g + 1], None, ALU.mult)
                    spreaded.by(last)
                    pool.wait_ge(scanned.sem, NQ * (i + 1))
                    pool.wait_ge(gram_sb.sem, i + 1)
                    mixed.by(nc.gpsimd.tensor_tensor(mix[:, i % 2, :, :], dec[:, i % 2, :, :],
                                                     spread(gram[:, i % 2, :], 1, HEADS), ALU.mult))


def carry_states(nc, m, a):
    with ExitStack() as ctx:
        sig = lambda name: Signal(ctx, nc, "state_" + name)
        sb = lambda name, shape: ctx.enter_context(nc.sbuf_tensor("state_" + name, shape, F32))
        st = sb("st", [P, BATCH, RING, HEADS, PDIM])
        tmp = sb("tmp", [P, 2, HEADS, PDIM])
        y = sb("y", [P, 2, HEADS, PDIM])
        xd = sb("xd", [P, 2, HEADS, PDIM])
        th = sb("thz", [P, 2, INTER])
        zs = sb("zs", [P, 2, INTER])
        sq = sb("sq", [P, INTER])
        ss = sb("ss", [P, TILES])
        rms = sb("rms", [P, TILES])
        gt = sb("gt", [P, 2, INTER])
        r = sb("r", [P, 2, DM])
        bs = sb("bs", [P, 2, 6])
        mv = sb("mv", [P, 2, 2])
        rs = sb("rs", [P, 2, 1])

        zero, decay_ps, new_ps, carried, inter_ps = (sig(n) for n in ("zero", "decay_ps", "new_ps", "carried",
                                                                      "inter_ps"))
        y1, y2, xd_ready, z_ps, th_ready, zs_ready = (sig(n) for n in ("y1", "y2", "xd_ready", "z_ps", "th_ready",
                                                                       "zs_ready"))
        ss_ready, gated, gt_ps, gt_sb, out_ps, rms_ready = (sig(n) for n in ("ss_ready", "gated", "gt_ps", "gt_sb",
                                                                             "out_ps", "rms_ready"))
        dve, pl, wn, mv_ready, rs_ready, resid = (sig(n) for n in ("dve3", "pool3", "wn", "mv_ready", "rs_ready",
                                                                  "resid"))
        tiles = [i // 2 + TPH * (i % 2) for i in range(TILES)]
        with nc.Block() as block:
            @block.tensor
            def _(pe):
                pe.wait_ge(m.wz_in.sem, 16)
                pe.wait_ge(zero.sem, 1)

                def finish(n):
                    i = tiles[n]
                    pe.wait_ge(gated.sem, n + 1)
                    if n >= 1:
                        pe.wait_ge(gt_sb.sem, n)
                    for c in range(4):
                        last = nc.tensor.transpose(m.ps[:, 6, P * c:P * (c + 1)], th[:, n % 2, P * c:P * (c + 1)],
                                                   m.ident[:, :])
                    gt_ps.by(last)
                    pe.wait_ge(gt_sb.sem, n + 1)
                    pe.wait_ge(wn.sem, 4)
                    if n >= 1:
                        pe.wait_ge(mv_ready.sem, n)
                    for c in range(4):
                        last = nc.tensor.matmul(m.ps[:, 7, 0:DM], gt[:, n % 2, P * c:P * (c + 1)], m.w_out[:, c, :],
                                                start=c == 0, stop=c == 3)
                    out_ps.by(last)

                for n, i in enumerate(tiles):
                    b = i // TPH
                    if n >= 1:
                        pe.wait_ge(carried.sem, G * n)
                    for g in range(G):
                        last = nc.tensor.matmul(m.ps[:, 0, HEADS * g:HEADS * (g + 1)], m.sel_last[:, g, :],
                                                m.since_row[:, i, :], start=True, stop=True)
                    decay_ps.by(last)
                    for g in range(G):
                        k = G * n + g
                        if k >= 2:
                            pe.wait_ge(carried.sem, k - 1)
                        new_ps.by(nc.tensor.matmul(m.ps[:, 1 + k % 2, :], m.b_row[Q * g:Q * (g + 1), i, :],
                                                   m.dt_end[Q * g:Q * (g + 1), i, :, :].rearrange("p h d -> p (h d)"),
                                                   start=True, stop=True))
                    if n >= 1:
                        pe.wait_ge(zs_ready.sem, n)
                    for k in range(KD):
                        last = nc.tensor.matmul(m.ps[:, 5, :], m.xT[:, k, P * i:P * (i + 1)], m.w_in[:, k, 0:INTER],
                                                start=k == 0, stop=k == KD - 1)
                    z_ps.by(last)
                    if n >= 1:
                        pe.wait_ge(y1.sem, n)
                    for g in range(G):
                        c = G * (i % TPH) + g
                        pe.wait_ge(carried.sem, G * n + g)
                        last = nc.tensor.matmul(m.ps[Q * g:Q * (g + 1), 3, :],
                                                m.xc[:, 5, P * i + Q * g:P * i + Q * (g + 1)],
                                                st[:, b, c % RING, :, :].rearrange("p h d -> p (h d)"),
                                                start=True, stop=True)
                    inter_ps.by(last)
                    if n >= 1:
                        finish(n - 1)
                finish(TILES - 1)

            @block.scalar
            def _(sc):
                for n, i in enumerate(tiles):
                    sc.wait_ge(z_ps.sem, n + 1)
                    if n >= 2:
                        sc.wait_ge(gt_ps.sem, n - 1)
                    th_ready.by(nc.scalar.activation(th[:, n % 2, :], m.ps[:, 5, :], ACT.Tanh, scale=0.125))
                    sc.wait_ge(y2.sem, n + 1)
                    ss_ready.by(nc.scalar.activation(sq[:, :], y[:, n % 2, :, :].rearrange("p h d -> p (h d)"),
                                                     ACT.Square, accum_out=ss[:, n:n + 1]))
                    sc.wait_ge(gt_ps.sem, n + 1)
                    gt_sb.by(nc.scalar.copy(gt[:, n % 2, :], m.ps[:, 6, :]))

            @block.vector
            def _(v):
                for b in range(BATCH):
                    zero.by(nc.vector.memset(st[:, b, 0, :, :], 0.0))
                v.wait_ge(m.late_in.sem, 16 * 2)
                for c in range(4):
                    wn.by(nc.vector.tensor_scalar(m.w_out[:, c, :], m.w_out[:, c, :], m.norm_w[:, c:c + 1], None,
                                                  ALU.mult))

                def tail(n):
                    i = tiles[n]
                    v.wait_ge(out_ps.sem, n + 1)
                    v.wait_ge(rms_ready.sem, n + 1)
                    dve.then_wait(v, nc.vector.scalar_tensor_tensor(r[:, n % 2, :], m.ps[:, 7, 0:DM],
                                                                    rms[:, n:n + 1], m.x[:, i, :], ALU.mult, ALU.add))
                    dve.then_wait(v, nc.vector.bn_stats(bs[:, n % 2, :], r[:, n % 2, :]))
                    mv_ready.by(nc.vector.bn_aggr(mv[:, n % 2, :], bs[:, n % 2, :]))

                def normalise(n):
                    i = tiles[n]
                    v.wait_ge(rs_ready.sem, n + 1)
                    v.wait_ge(mv_ready.sem, n + 1)
                    resid.by(nc.vector.tensor_scalar(m.x[:, i, :], r[:, n % 2, :], mv[:, n % 2, 0:1],
                                                     rs[:, n % 2, 0:1], ALU.subtract, ALU.mult))

                for n, i in enumerate(tiles):
                    b = i // TPH
                    v.wait_ge(decay_ps.sem, n + 1)
                    for g in range(G):
                        c, k = G * (i % TPH) + g, G * n + g
                        if k:
                            v.wait_ge(carried.sem, k)
                        if n >= 4:
                            v.wait_ge(inter_ps.sem, n - 3)
                        dve.then_wait(v, nc.vector.tensor_tensor(
                            tmp[:, k % 2, :, :], st[:, b, c % RING, :, :],
                            spread(m.ps[:, 0, HEADS * g:HEADS * (g + 1)], 2, PDIM), ALU.mult))
                        v.wait_ge(new_ps.sem, k + 1)
                        carried.by(nc.vector.tensor_tensor(
                            st[:, b, (c + 1) % RING, :, :], tmp[:, k % 2, :, :],
                            m.ps[:, 1 + k % 2, :].rearrange("p (h d) -> p h d", d=PDIM), ALU.add))
                    v.wait_ge(th_ready.sem, n + 1)
                    if n >= 2:
                        v.wait_ge(gated.sem, n - 1)
                    zs_ready.by(nc.vector.scalar_tensor_tensor(zs[:, n % 2, :], th[:, n % 2, :], 1.0, m.ps[:, 5, :],
                                                               ALU.add, ALU.mult))
                    v.wait_ge(inter_ps.sem, n + 1)
                    if n >= 2:
                        v.wait_ge(ss_ready.sem, n - 1)
                    y1.by(nc.vector.tensor_tensor(y[:, n % 2, :, :],
                                                  m.ps[:, 3, :].rearrange("p (h d) -> p h d", d=PDIM),
                                                  spread(m.since_row[:, i, :], 2, PDIM), ALU.mult))
                    if n >= 1:
                        tail(n - 1)
                        normalise(n - 1)
                tail(TILES - 1)
                normalise(TILES - 1)

            @block.gpsimd
            def _(pool):
                pool.wait_ge(m.const_in.sem, 16 * 5)

                def row_scales(n):
                    pool.wait_ge(ss_ready.sem, n + 1)
                    pl.then_wait(pool, nc.gpsimd.tensor_scalar(rms[:, n:n + 1], ss[:, n:n + 1], 1.0 / INTER, 1e-5,
                                                               ALU.mult, ALU.add))
                    pl.then_wait(pool, nc.gpsimd.tensor_tensor(rms[:, n:n + 1], rms[:, n:n + 1], m.half[:, :],
                                                               ALU.pow))
                    rms_ready.by(nc.gpsimd.tensor_scalar(rms[:, n:n + 1], rms[:, n:n + 1], 0.125, None, ALU.mult))

                def ln_scale(n):
                    pool.wait_ge(mv_ready.sem, n + 1)
                    pl.then_wait(pool, nc.gpsimd.tensor_scalar(rs[:, n % 2, :], mv[:, n % 2, 1:2], LN_EPS, None,
                                                               ALU.add))
                    rs_ready.by(nc.gpsimd.tensor_tensor(rs[:, n % 2, :], rs[:, n % 2, :], m.half[:, :], ALU.pow))

                for n, i in enumerate(tiles):
                    xd_ready.then_wait(pool, nc.gpsimd.tensor_tensor(
                        xd[:, n % 2, :, :], m.x_row[:, i, :].rearrange("p (h d) -> p h d", d=PDIM),
                        spread(m.d_row[:, :], 2, PDIM), ALU.mult))
                    xd4 = xd[:, n % 2, :, :].rearrange("p (c h) d -> p c (h d)", c=4)
                    pl.then_wait(pool, nc.gpsimd.tensor_tensor(xd4, xd4, m.xc[:, 0:4, P * i:P * (i + 1)], ALU.add))
                    pool.wait_ge(y1.sem, n + 1)
                    y2.then_wait(pool, nc.gpsimd.tensor_tensor(y[:, n % 2, :, :], y[:, n % 2, :, :], xd[:, n % 2, :, :],
                                                               ALU.add))
                    pool.wait_ge(zs_ready.sem, n + 1)
                    gated.by(nc.gpsimd.tensor_tensor(th[:, n % 2, :], y[:, n % 2, :, :].rearrange("p h d -> p (h d)"),
                                                     zs[:, n % 2, :], ALU.mult))
                    row_scales(n)
                    if n >= 1:
                        ln_scale(n - 1)
                ln_scale(TILES - 1)


def ln_stats(nc, v, work, n, step, mv_ready):
    step.then_wait(v, nc.vector.bn_stats(work.bs[:, n % 2, :], work.r[:, n % 2, :]))
    mv_ready.by(nc.vector.bn_aggr(work.mv[:, n % 2, :], work.bs[:, n % 2, :]))


def ln_scale(nc, pool, m, work, n, step, mv_ready, rs_ready):
    pool.wait_ge(mv_ready.sem, n + 1)
    step.then_wait(pool, nc.gpsimd.tensor_scalar(work.rs[:, n % 2, :], work.mv[:, n % 2, 1:2], LN_EPS, None, ALU.add))
    rs_ready.by(nc.gpsimd.tensor_tensor(work.rs[:, n % 2, :], work.rs[:, n % 2, :], m.half[:, :], ALU.pow))


def ln_apply(nc, v, m, work, n, i, rs_ready, x_ready):
    v.wait_ge(rs_ready.sem, n + 1)
    x_ready.by(nc.vector.tensor_scalar(m.x[:, i, :], work.r[:, n % 2, :], work.mv[:, n % 2, 0:1],
                                       work.rs[:, n % 2, 0:1], ALU.subtract, ALU.mult))


def ln_work(sb):
    w = Memory()
    w.r, w.bs, w.mv, w.rs = sb("r", [P, 2, DM]), sb("bs", [P, 2, 6]), sb("mv", [P, 2, 2]), sb("rs", [P, 2, 1])
    return w


def load_lora(nc, m, a, sp):
    sp.dma_start(m.lw_a[:, :, :], a["L0_ffn_A"].rearrange("e r d -> (e r) d").rearrange("(j p) d -> p j d", p=P)
                 ).then_inc(m.lora_in.sem, 16)
    for h in range(KD):
        sp.dma_start(m.lw_b[:, h, :, :], a["L0_ffn_Bw"][:, P * h:P * (h + 1), :].rearrange("e p r -> p e r")
                     ).then_inc(m.lora_in.sem, 16)
    sp.dma_start(m.lw_g[:, :], a["L0_ffn_Wg"]).then_inc(m.lora_in.sem, 16)
    sp.dma_start(m.first8[:, :], a["c_first8"]).then_inc(m.lora_in.sem, 16)


def lora_experts(nc, m, a):
    with ExitStack() as ctx:
        sig = lambda name: Signal(ctx, nc, "lora_" + name)
        sb = lambda name, shape: ctx.enter_context(nc.sbuf_tensor("lora_" + name, shape, F32))
        aT = sb("aT", [P, KD, LE * LR])
        bT = sb("bT", [P, LE * LR // P, DM])
        gT = sb("gT", [P, KD, LE])
        lg = sb("lg", [P, TILES, LE])
        ex = sb("ex", [P, TILES, LE])
        hot = sb("hot", [P, TILES, LE])
        mx = sb("mx", [P, TILES])
        sm = sb("sm", [P, TILES])
        hm = sb("hm", [P, 2, LE, LR])
        hT = sb("hT", [P, 2, LE * LR])
        work = ln_work(sb)
        xt_ps, xt_sb, wt_ps, wt_sb = sig("xt_ps"), sig("xt_sb"), sig("wt_ps"), sig("wt_sb")
        lg_ps, ex_in, ex_out, h_ps, h_sb = (sig(n) for n in ("lg_ps", "ex_in", "ex_out", "h_ps", "h_sb"))
        hT_ps, hT_sb, y_ps, dve, pl = (sig(n) for n in ("hT_ps", "hT_sb", "y_ps", "dve4", "pool4"))
        mv_ready, rs_ready, x_ready = sig("mv_ready"), sig("rs_ready"), sig("x_ready")
        NJ = LE * LR // P
        with nc.Block() as block:
            @block.tensor
            def _(pe):
                pe.wait_ge(m.lora_in.sem, 16 * 5)
                for k in range(KD):
                    last = nc.tensor.transpose(m.ps[:, 4, LE * k:LE * (k + 1)], m.lw_g[:, P * k:P * (k + 1)],
                                               m.ident[0:LE, 0:LE])
                wt_ps.by(last)
                for k in range(KD):
                    for j in range(NJ):
                        last = nc.tensor.transpose(m.ps[:, 5 + k, P * j:P * (j + 1)], m.lw_a[:, j, P * k:P * (k + 1)],
                                                   m.ident[:, :])
                    wt_ps.by(last)
                for jj in range(2):
                    if jj == 1:
                        pe.wait_ge(wt_sb.sem, 1)
                    for j in (2 * jj, 2 * jj + 1):
                        for h in range(KD):
                            last = nc.tensor.transpose(
                                m.ps[:, 7 if jj == 0 else 4, DM * (j % 2) + P * h:DM * (j % 2) + P * (h + 1)],
                                m.lw_b[:, h, 2 * j:2 * j + 2, :].rearrange("p e r -> p (e r)"), m.ident[:, :])
                    wt_ps.by(last)
                transpose_rows(pe, nc, m, 0, lambda i: None, xt_ps)
                pe.wait_ge(xt_sb.sem, 4)
                pe.wait_ge(wt_sb.sem, 5)
                for i in range(TILES):
                    for k in range(KD):
                        last = nc.tensor.matmul(m.ps[:, 0, LE * i:LE * (i + 1)], m.xT[:, k, P * i:P * (i + 1)],
                                                gT[:, k, :], start=k == 0, stop=k == KD - 1)
                lg_ps.by(last)

                def down(i):
                    pe.wait_ge(h_sb.sem, i + 1)
                    for j in range(NJ):
                        last = nc.tensor.transpose(m.ps[:, 1 + i % 2, P * j:P * (j + 1)],
                                                   hm[:, i % 2, 2 * j:2 * j + 2, :].rearrange("p e r -> p (e r)"),
                                                   m.ident[:, :])
                    hT_ps.by(last)
                    pe.wait_ge(hT_sb.sem, i + 1)
                    if i >= 2:
                        pe.wait_ge(mv_ready.sem, i - 1)
                    for j in range(NJ):
                        last = nc.tensor.matmul(m.ps[:, 3 + 4 * (i % 2), 0:DM], hT[:, i % 2, P * j:P * (j + 1)],
                                                bT[:, j, :], start=j == 0, stop=j == NJ - 1)
                    y_ps.by(last)

                for i in range(TILES):
                    if i >= 2:
                        pe.wait_ge(h_sb.sem, i - 1)
                    for k in range(KD):
                        last = nc.tensor.matmul(m.ps[:, 5 + i % 2, :], m.xT[:, k, P * i:P * (i + 1)], aT[:, k, :],
                                                start=k == 0, stop=k == KD - 1)
                    h_ps.by(last)
                    if i >= 1:
                        down(i - 1)
                down(TILES - 1)

            @block.scalar
            def _(sc):
                for n, (bank, dst) in enumerate(((4, gT[:, :, :].rearrange("p k e -> p (k e)")),
                                                 (5, aT[:, 0, :]), (6, aT[:, 1, :]),
                                                 (7, bT[:, 0:2, :].rearrange("p j o -> p (j o)")),
                                                 (4, bT[:, 2:4, :].rearrange("p j o -> p (j o)")))):
                    sc.wait_ge(wt_ps.sem, n + 1)
                    wt_sb.by(nc.scalar.copy(dst, m.ps[:, bank, 0:dst.shape[1]]))
                sc.wait_ge(ex_in.sem, 1)
                ex_out.by(nc.scalar.activation(ex[:, :, :], lg[:, :, :], ACT.Exp))
                for i in range(TILES):
                    sc.wait_ge(hT_ps.sem, i + 1)
                    if i >= 2:
                        sc.wait_ge(y_ps.sem, i - 1)
                    hT_sb.by(nc.scalar.copy(hT[:, i % 2, :], m.ps[:, 1 + i % 2, :]))

            @block.vector
            def _(v):
                copy_transposed(v, nc.vector.tensor_copy, m, 0, xt_ps, xt_sb)
                v.wait_ge(lg_ps.sem, 1)
                lps = m.ps[:, 0, 0:TILES * LE].rearrange("p (i e) -> p i e", e=LE)
                dve.then_wait(v, nc.vector.tensor_reduce(mx[:, :], lps, AX.X, ALU.max))
                ex_in.then_wait(v, nc.vector.tensor_tensor(lg[:, :, :], lps, spread(mx[:, :], 2, LE), ALU.subtract))
                dve.then_wait(v, nc.vector.tensor_scalar(hot[:, :, :], lg[:, :, :], 0.0, None, ALU.is_equal))
                dve.then_wait(v, nc.vector.tensor_tensor(hot[:, :, :], hot[:, :, :], spread(m.first8[:, :], 1, TILES),
                                                         ALU.mult))
                dve.then_wait(v, nc.vector.tensor_reduce(mx[:, :], hot[:, :, :], AX.X, ALU.max))
                dve.then_wait(v, nc.vector.tensor_tensor(hot[:, :, :], hot[:, :, :], spread(mx[:, :], 2, LE),
                                                         ALU.is_equal))
                v.wait_ge(ex_out.sem, 1)
                dve.then_wait(v, nc.vector.tensor_reduce(sm[:, :], ex[:, :, :], AX.X, ALU.add))
                dve.then_wait(v, nc.vector.reciprocal(sm[:, :], sm[:, :]))
                dve.then_wait(v, nc.vector.scalar_tensor_tensor(hot[:, :, :], hot[:, :, :], LSCALE,
                                                                spread(sm[:, :], 2, LE), ALU.mult, ALU.mult))

                def tail(i):
                    v.wait_ge(y_ps.sem, i + 1)
                    if i >= 2:
                        v.wait_ge(x_ready.sem, i - 1)
                    dve.then_wait(v, nc.vector.tensor_tensor(work.r[:, i % 2, :], m.ps[:, 3 + 4 * (i % 2), 0:DM],
                                                             m.x[:, i, :], ALU.add))
                    ln_stats(nc, v, work, i, dve, mv_ready)

                for i in range(TILES):
                    v.wait_ge(h_ps.sem, i + 1)
                    if i >= 2:
                        v.wait_ge(hT_ps.sem, i - 1)
                    h_sb.by(nc.vector.tensor_tensor(hm[:, i % 2, :, :],
                                                    m.ps[:, 5 + i % 2, :].rearrange("p (e r) -> p e r", r=LR),
                                                    spread(hot[:, i, :], 2, LR), ALU.mult))
                    if i >= 1:
                        tail(i - 1)
                    if i >= 2:
                        ln_apply(nc, v, m, work, i - 2, i - 2, rs_ready, x_ready)
                tail(TILES - 1)
                for i in (TILES - 2, TILES - 1):
                    ln_apply(nc, v, m, work, i, i, rs_ready, x_ready)

            @block.gpsimd
            def _(pool):
                for i in range(TILES):
                    ln_scale(nc, pool, m, work, i, pl, mv_ready, rs_ready)


def load_qkv(nc, m, a, sp):
    sp.dma_start(m.w_down[:, :, :], k_tiles(a["L1_attn_w_down"])).then_inc(m.qkv_in.sem, 16)
    sp.dma_start(m.b_down[:, :], a["L1_attn_b_down"].unsqueeze(1), allow_slow_non_contiguous=True
                 ).then_inc(m.qkv_in.sem, 16)
    sp.dma_start(m.w_up[:, :], a["L1_attn_w_up"]).then_inc(m.qkv_in.sem, 16)
    sp.dma_start(m.b_up[:, :], a["L1_attn_b_up"].partition_broadcast(P)).then_inc(m.qkv_in.sem, 16)
    sp.dma_start(m.b_q[:, :], a["L1_attn_b_q"].partition_broadcast(P)).then_inc(m.qkv_in.sem, 16)
    for k, name in enumerate(("L1_attn_qn_w", "L1_attn_kn_w")):
        sp.dma_start(m.norm_qk[:, k, :], a[name].partition_broadcast(P)).then_inc(m.qkv_in.sem, 16)
    sp.dma_start(m.dist, a["c_dist"]).then_inc(m.qkv_in.sem, 16)
    sp.dma_start(m.cos_row[:, :, :], a["c_cos"]).then_inc(m.qkv_in.sem, 16)
    sp.dma_start(m.sin_row[:, :, :], a["c_sin"]).then_inc(m.qkv_in.sem, 16)
    sp.dma_start(m.w_q[:, :, :], k_tiles(a["L1_attn_w_q"])).then_inc(m.qkv_in.sem, 16)
QKV_LOADS = 11


class Selection:

    def __init__(self, sig, first, s, top, later, not_self):
        self.first, self.s, self.top, self.later, self.not_self = first, s, top, later, not_self
        self.masks, self.s_ps, self.s_sb, self.kept, self.s_turned, self.biased, self.dve = (sig(n) for n in (
            "masks", "sel_ps", "sel_sb", "kept", "sel_turned", "sel_biased", "sel_dve"))

    def buffer(self, i):
        j = i % TPH
        return self.s[:, i % 2, 0:P * (j + 1)], self.s[:, i % 2, P * j:P * (j + 1)]


def form_masks(nc, pool, q):
    q.masks.by(nc.gpsimd.memset(q.later, 0.0))
    q.masks.then_wait(pool, nc.gpsimd.memset(q.not_self, 1.0))
    q.masks.by(nc.gpsimd.affine_select(q.later, q.later, [[-1, P]], ALU.is_ge, LATER, base=0, channel_multiplier=1))
    q.masks.by(nc.gpsimd.affine_select(q.not_self, q.not_self, [[-1, P]], ALU.not_equal, 0.0, base=0,
                                       channel_multiplier=1))


def select_scores(nc, pe, m, q, i):
    b, j = i // TPH, i % TPH
    if i > q.first:
        pe.wait_ge(q.biased.sem, i - q.first)
    q.s_ps.by(nc.tensor.matmul(m.ps[:, 7, 0:P * (j + 1)], m.qT[0:SEL_DIM, 0, P * i:P * (i + 1)],
                               m.kT[0:SEL_DIM, 0, SEQ * b:SEQ * b + P * (j + 1)], start=True, stop=True))


def select_copy(nc, sc, m, q, i):
    n = i - q.first
    sc.wait_ge(q.s_ps.sem, n + 1)
    if n >= 2:
        sc.wait_ge(q.s_turned.sem, n - 1)
    s, own = q.buffer(i)
    q.s_sb.by(nc.scalar.copy(s, m.ps[:, 7, 0:s.shape[1]]))


def select_rounds(nc, v, q, i, lo, hi):
    s, own = q.buffer(i)
    if lo == 0:
        v.wait_ge(q.s_sb.sem, i - q.first + 1)
        v.wait_ge(q.masks.sem, 4)
        q.dve.then_wait(v, nc.vector.tensor_tensor(own, own, q.later, ALU.add))
    for _ in range(lo, hi):
        q.dve.then_wait(v, nc.vector.max(q.top, s))
        q.dve.then_wait(v, nc.vector.match_replace(s, q.top, s, TAKEN))
    if hi == SEL_TOPK // 8:
        q.dve.then_wait(v, nc.vector.tensor_scalar(s, s, TAKEN / 2, None, ALU.is_gt))
        q.kept.by(nc.vector.tensor_tensor(own, own, q.not_self, ALU.mult))


def select_turn(nc, pe, m, q, i):
    pe.wait_ge(q.kept.sem, i - q.first + 1)
    for k in range(i % TPH + 1):
        last = nc.tensor.transpose(m.ps[:, 7, P * k:P * (k + 1)], q.s[:, i % 2, P * k:P * (k + 1)], m.ident[:, :])
    q.s_turned.by(last)


def select_bias(nc, v, m, q, i):
    b, j = i // TPH, i % TPH
    v.wait_ge(q.s_turned.sem, i - q.first + 1)
    for k in range(j + 1):
        c = KEY_COL[k] + P * (j - k)
        last = nc.vector.scalar_tensor_tensor(m.bias[b][:, c:c + P], m.ps[:, 7, P * k:P * (k + 1)], FAR,
                                              m.dist[:, c:c + P], ALU.mult, ALU.add)
    q.biased.by(last)


def prepare_attention(nc, m, a):
    with ExitStack() as ctx:
        sig = lambda name: Signal(ctx, nc, "qkv_" + name)
        sb = lambda name, shape: ctx.enter_context(nc.sbuf_tensor("qkv_" + name, shape, F32))
        latT = sb("latT", [LATENT, NT])
        cw = sb("cw", [P, 2, TPH, HD])
        sw = sb("sw", [P, 2, TPH, HD])
        qb = sb("qb", [P, 2, QKH, HD])
        t1 = sb("t1", [P, QKH, HD])
        sq = m.cos_row
        ss = sb("ss5", [P, 2, QKH])
        half20 = sb("half20", [P, QKH])
        s = sb("s", [P, 2, SEQ])
        top = sb("top", [P, 8])
        xt_ps, xt_sb, lat_ps, lat_sb, tab = (sig(n) for n in ("xt_ps", "xt_sb", "lat_ps", "lat_sb", "tab"))
        q_ps, kv_ps, qb_ready, v_ready, squared = (sig(n) for n in ("q_ps", "kv_ps", "qb_ready", "v_ready",
                                                                   "squared"))
        rs_ready, cos_ready, sin_ready, rot, normed = (sig(n) for n in ("rs_ready", "cos_ready", "sin_ready", "rot",
                                                                       "normed"))
        turned, qk_sb, pl, ones = (sig(n) for n in ("turned", "qk_sb", "pool5", "ones"))
        NG = QKH // 4
        TURN, SELECT = 2, 5
        KEYS = NG - 1
        q = Selection(sig, 0, s, top[:, :], m.sin_row[:, 0, :], m.sin_row[:, 1, :])
        with nc.Block() as block:
            @block.sync
            def _(sp):
                load_qkv(nc, m, a, sp)

            @block.tensor
            def _(pe):
                pe.wait_ge(m.qkv_in.sem, 16 * QKV_LOADS)
                transpose_rows(pe, nc, m, 0, lambda i: None, xt_ps)
                pe.wait_ge(xt_sb.sem, 4)
                for h in range(HALVES):
                    for k in range(KD):
                        last = nc.tensor.matmul(m.ps[0:LATENT, 4 + h, :], m.w_down[:, k, :],
                                                m.xT[:, k, 512 * h:512 * (h + 1)], start=k == 0, stop=k == KD - 1)
                    lat_ps.by(last)
                pe.wait_ge(lat_sb.sem, 2)

                def project_kv(i):
                    if i >= 1:
                        pe.wait_ge(qb_ready.sem, 3 * i - 2)
                        pe.wait_ge(v_ready.sem, i)
                    for c in range(2):
                        last = nc.tensor.matmul(m.ps[:, 4 + c, :], latT[:, P * i:P * (i + 1)],
                                                m.w_up[:, 512 * c:512 * (c + 1)], start=True, stop=True)
                    kv_ps.by(last)

                def project_q(i, c):
                    if i >= 1 and c % 2 == 0:
                        pe.wait_ge(qb_ready.sem, 3 * i - 1 + c // 2)
                    for k in range(KD):
                        last = nc.tensor.matmul(m.ps[:, c, :], m.xT[:, k, P * i:P * (i + 1)],
                                                m.w_q[:, k, 512 * c:512 * (c + 1)], start=k == 0, stop=k == KD - 1)
                    if c % 2 == 1:
                        q_ps.by(last)

                def turn(i, g):
                    if g == KEYS:
                        pe.wait_ge(normed.sem, i + 1)
                    if turned.n >= 1:
                        pe.wait_ge(qk_sb.sem, turned.n)
                    for j in range(4):
                        last = nc.tensor.transpose(m.ps[:, 6, P * j:P * (j + 1)], qb[:, i % 2, 4 * g + j, :],
                                                   m.ident[:, :])
                    turned.by(last)

                for i in range(TILES + TURN):
                    now, turning = i < TILES, i >= TURN
                    n = i - SELECT
                    if now:
                        project_kv(i)
                    if 0 <= n < TPH:
                        pe.wait_ge(qk_sb.sem, NG * (n + 1))
                        select_scores(nc, pe, m, q, n)
                    if now:
                        project_q(i, 0)
                        project_q(i, 1)
                    if turning:
                        for g in (KEYS, 0, 1):
                            turn(i - TURN, g)
                    if now:
                        project_q(i, 2)
                    if turning:
                        turn(i - TURN, 2)
                    if 0 <= n < TPH - 1:
                        select_turn(nc, pe, m, q, n)
                    if now:
                        project_q(i, 3)
                    if turning:
                        turn(i - TURN, 3)
                select_turn(nc, pe, m, q, TPH - 1)

            @block.scalar
            def _(sc):
                for h in range(HALVES):
                    sc.wait_ge(lat_ps.sem, h + 1)
                    lat_sb.by(nc.scalar.activation(latT[:, 512 * h:512 * (h + 1)], m.ps[0:LATENT, 4 + h, :],
                                                   ACT.Identity, bias=m.b_down[:, 0:1]))

                def copy_turned(i, g):
                    sc.wait_ge(turned.sem, qk_sb.n + 1)
                    dst = (m.kT[:, :, P * i:P * (i + 1)] if g == KEYS else
                           m.qT[:, 4 * g:4 * g + 4, P * i:P * (i + 1)])
                    qk_sb.by(nc.scalar.copy(dst, m.ps[:, 6, :].rearrange("p (j t) -> p j t", t=P)))

                def square(i, heads, added):
                    sc.wait_ge(qb_ready.sem, 3 * i + added)
                    for h in heads:
                        if squared.n >= TPH:
                            sc.wait_ge(squared.sem, squared.n - TPH + 1)
                        squared.by(nc.scalar.activation(sq[:, squared.n % TPH, :], qb[:, i % 2, h, :], ACT.Square,
                                                        accum_out=ss[:, i % 2, h:h + 1]))

                for i in range(TILES + TURN):
                    turning = i >= TURN
                    if 0 <= i - SELECT < TPH:
                        select_copy(nc, sc, m, q, i - SELECT)
                    if turning:
                        for g in (KEYS, 0, 1):
                            copy_turned(i - TURN, g)
                    if turning:
                        copy_turned(i - TURN, 2)
                    if i < TILES:
                        if turning:
                            sc.wait_ge(normed.sem, i - TURN + 1)
                        square(i, range(16, 20), 1)
                        square(i, range(0, 8), 2)
                    if turning:
                        copy_turned(i - TURN, 3)
                    if i < TILES:
                        square(i, range(8, 16), 3)

            @block.vector
            def _(v):
                v.wait_ge(m.qkv_in.sem, 16 * QKV_LOADS)
                copy_transposed(v, nc.vector.tensor_copy, m, 0, xt_ps, xt_sb)
                for n in range(2):
                    nc.vector.tensor_tensor(cw[:, n, :, :], m.cos_row[:, :, :], spread(m.norm_qk[:, n, :], 1, TPH),
                                            ALU.mult)
                    for o in range(2):
                        last = nc.vector.tensor_tensor(sw[:, n, :, o::2], m.sin_row[:, :, o::2],
                                                       spread(m.norm_qk[:, n, 1 - o::2], 1, TPH), ALU.mult)
                    tab.by(last)
                v.wait_ge(tab.sem, 2)

                def turned_before(i, groups):
                    if i >= 2:
                        v.wait_ge(turned.sem, NG * (i - 2) + groups)

                def add_kv(i):
                    turned_before(i, 1)
                    v.wait_ge(kv_ps.sem, i + 1)
                    qb_ready.by(nc.vector.tensor_tensor(qb[:, i % 2, 16:20, :].rearrange("p h d -> p (h d)"),
                                                        m.ps[:, 4, :], m.b_up[:, 0:512], ALU.add))
                    v_ready.by(nc.vector.tensor_tensor(m.v[:, i, :, 0:HD],
                                                       m.ps[:, 5, :].rearrange("p (g d) -> p g d", d=HD),
                                                       m.b_up[:, 512:1024].rearrange("p (g d) -> p g d", d=HD),
                                                       ALU.add))

                def add_q(i, half):
                    turned_before(i, 3 + 2 * half)
                    v.wait_ge(q_ps.sem, 2 * i + half + 1)
                    qb_ready.by(nc.vector.tensor_tensor(
                        qb[:, i % 2, 8 * half:8 * half + 8, :].rearrange("p h d -> p (h d)"),
                        m.ps[:, 2 * half:2 * half + 2, :].rearrange("p b n -> p (b n)"),
                        m.b_q[:, 1024 * half:1024 * (half + 1)], ALU.add))

                def sin_part(i):
                    b, j = qb[:, i % 2, :, :], i % TPH
                    v.wait_ge(qb_ready.sem, 3 * i + 3)
                    if i >= 1:
                        v.wait_ge(rot.sem, i)
                    for n, h0, h1 in ((0, 0, 16), (1, 16, 20)):
                        for o in range(2):
                            last = nc.vector.tensor_tensor(t1[:, h0:h1, o::2], b[:, h0:h1, 1 - o::2],
                                                           spread(sw[:, n, j, o::2], 1, h1 - h0), ALU.mult)
                    sin_ready.by(last)

                def normalise(i):
                    v.wait_ge(rot.sem, i + 1)
                    v.wait_ge(rs_ready.sem, i + 1)
                    normed.by(nc.vector.tensor_tensor(qb[:, i % 2, :, :], qb[:, i % 2, :, :],
                                                      spread(ss[:, i % 2, :], 2, HD), ALU.mult))

                for i in range(TILES):
                    n = i - SELECT
                    add_kv(i)
                    add_q(i, 0)
                    add_q(i, 1)
                    if 0 <= n < TPH:
                        select_bias(nc, v, m, q, n)
                    sin_part(i)
                    if i >= 1:
                        normalise(i - 1)
                    if 0 <= n + 1 < TPH:
                        select_rounds(nc, v, q, n + 1, 0, SEL_TOPK // 8)
                normalise(TILES - 1)
                select_bias(nc, v, m, q, TPH - 1)

            @block.gpsimd
            def _(pool):
                ones.by(nc.gpsimd.memset(m.v[:, :, :, HD:HD + 1], 1.0))
                ones.then_wait(pool, nc.gpsimd.memset(half20[:, :], -0.5))
                pool.wait_ge(tab.sem, 2)
                form_masks(nc, pool, q)
                for i in range(TILES):
                    j = i % TPH
                    b = qb[:, i % 2, :, :]
                    pool.wait_ge(sin_ready.sem, i + 1)
                    pool.wait_ge(squared.sem, QKH * (i + 1))
                    for of_k, h0, h1 in ((0, 0, 16), (1, 16, 20)):
                        last = nc.gpsimd.tensor_tensor(b[:, h0:h1, :], b[:, h0:h1, :],
                                                       spread(cw[:, of_k, j, :], 1, h1 - h0), ALU.mult)
                    cos_ready.then_wait(pool, last)
                    rot.by(nc.gpsimd.tensor_tensor(b, b, t1[:, :, :], ALU.add))
                    pl.then_wait(pool, nc.gpsimd.tensor_scalar(ss[:, i % 2, :], ss[:, i % 2, :], 1.0 / HD, 1e-6,
                                                               ALU.mult, ALU.add))
                    rs_ready.by(nc.gpsimd.tensor_tensor(ss[:, i % 2, :], ss[:, i % 2, :], half20[:, :], ALU.pow))


def load_attention(nc, m, a, sp):
    sp.dma_start(m.gate_b[:, :], a["L1_attn_gate_b"].rearrange("h e -> e h"), allow_slow_non_contiguous=True
                 ).then_inc(m.attn_in.sem, 16)
    for h in range(2):
        sp.dma_start(m.gate_w[:, 8 * h:8 * h + 8, :],
                     a["L1_attn_gate_w"][8 * h:8 * h + 8, :, :].rearrange("h d e -> d h e")).then_inc(m.attn_in.sem, 16)
    sp.dma_start(m.w_o[:, :, :], a["L1_attn_w_o"].rearrange("(h d) n -> d h n", d=P)).then_inc(m.wo_in.sem, 16)
    sp.dma_start(m.b_o[:, :], a["L1_attn_b_o"].partition_broadcast(P)).then_inc(m.wo_in.sem, 16)
ATTN_LOADS = 3


def attend(nc, m, a):
    with ExitStack() as ctx:
        sig = lambda name: Signal(ctx, nc, "att_" + name)
        sb = lambda name, shape: ctx.enter_context(nc.sbuf_tensor("att_" + name, shape, F32))
        rd = sb("rd", [P, 2, TPH])
        c = 0
        parts = []
        for n in (NCOL, NCOL, SEQ, SEQ, SEQ):
            parts.append(m.rows[:, c:c + 2 * n].rearrange("p (u n) -> p u n", u=2))
            c += 2 * n
        t, p, yn, yT, tg = parts
        yn = yn.rearrange("p u (j d) -> p u j d", d=HD)
        gb = sb("gb", [P, AH])
        top = sb("top", [P, 8])
        late = Space(m.weights[:, 2 * NE * DM - 2 * SEQ - 2 * P:])
        q = Selection(sig, TPH, late.take(P, 2, SEQ), top[:, :], late.take(P, P), late.take(P, P))
        s_ps, capped, biased, p_ready, y_ps, y_sb = (sig(n) for n in ("s_ps", "capped", "biased", "p_ready", "y_ps",
                                                                     "y_sb"))
        yT_ps, yT_sb, g_ps, g_sb, z_ready, gb_ready, dve = (sig(n) for n in (
            "yT_ps", "yT_sb", "g_ps", "g_sb", "z_ready", "gb_ready", "dve7"))
        todo = [(b, h) for b in range(BATCH) for h in range(AH)]
        N = len(todo)
        flat = m.ps[:, 0:3, :].rearrange("p b n -> p (b n)")
        ROUNDS = [0, 3, 6, 8]
        TURN = len(ROUNDS) - 1

        def tile_step(n):
            return (TPH + n // (TURN + 1), n % (TURN + 1)) if n < TPH * (TURN + 1) else (None, -1)

        with nc.Block() as block:
            @block.sync
            def _(sp):
                load_attention(nc, m, a, sp)
                load_gate(nc, m, a, sp, 0)
                sp.wait_ge(q.biased.sem, TPH)
                load_gate(nc, m, a, sp, 1)

            @block.gpsimd
            def _(pool):
                form_masks(nc, pool, q)

            @block.tensor
            def _(pe):
                def scores(n):
                    b, h = todo[n]
                    if n >= 1:
                        pe.wait_ge(capped.sem, n)
                    for i in range(TPH):
                        w = SEQ - P * i
                        last = nc.tensor.matmul(flat[:, KEY_COL[i]:KEY_COL[i] + w],
                                                m.kT[:, h // KVG, SEQ * b + P * i:SEQ * b + P * (i + 1)],
                                                m.qT[:, h, SEQ * b + P * i:SEQ * (b + 1)], start=True, stop=True)
                    s_ps.by(last)

                def values(n):
                    b, h = todo[n]
                    pe.wait_ge(p_ready.sem, n + 1)
                    if n >= 1:
                        pe.wait_ge(y_sb.sem, n)
                    for j in range(TPH):
                        out = m.ps[:, 3, VW * j:VW * (j + 1)] if j < 3 else m.ps[:, 4, 0:VW]
                        for i in range(j + 1):
                            c = KEY_COL[i] + P * (j - i)
                            last = nc.tensor.matmul(out, p[:, n % 2, c:c + P], m.v[:, TPH * b + i, h // KVG, :],
                                                    start=i == 0, stop=i == j)
                    y_ps.by(last)

                def turn(n):
                    pe.wait_ge(y_sb.sem, n + 1)
                    if n >= 1:
                        pe.wait_ge(yT_sb.sem, n)
                    for j in range(TPH):
                        last = nc.tensor.transpose(m.ps[:, 5, P * j:P * (j + 1)], yn[:, n % 2, j, :], m.ident[:, :])
                    yT_ps.by(last)

                def gate(n):
                    if n == 0:
                        pe.wait_ge(m.attn_in.sem, 16 * ATTN_LOADS)
                    pe.wait_ge(yT_sb.sem, n + 1)
                    if n >= 1:
                        pe.wait_ge(g_sb.sem, n)
                    g_ps.by(nc.tensor.matmul(m.ps[:, 6, :], m.gate_w[:, todo[n][1], :], yT[:, n % 2, :], start=True,
                                             stop=True))

                scores(0)
                for n in range(N):
                    i, step = tile_step(n)
                    if step == 0:
                        select_scores(nc, pe, m, q, i)
                    if step == TURN:
                        select_turn(nc, pe, m, q, i)
                    if n + 1 < N:
                        scores(n + 1)
                    if n >= 1:
                        turn(n - 1)
                    values(n)
                    if n >= 1:
                        gate(n - 1)
                turn(N - 1)
                gate(N - 1)

            @block.scalar
            def _(sc):
                def cap(n):
                    sc.wait_ge(s_ps.sem, n + 1)
                    if n >= 2:
                        sc.wait_ge(p_ready.sem, n - 1)
                    capped.by(nc.scalar.activation(t[:, n % 2, :], flat[:, 0:NCOL], ACT.Tanh,
                                                   scale=1.0 / (HD ** 0.5 * SOFTCAP)))

                def gating(n):
                    if n == 0:
                        sc.wait_ge(gb_ready.sem, 1)
                    sc.wait_ge(yT_ps.sem, n + 1)
                    if n >= 2:
                        sc.wait_ge(z_ready.sem, n - 1)
                    yT_sb.by(nc.scalar.copy(yT[:, n % 2, :], m.ps[:, 5, :]))
                    sc.wait_ge(g_ps.sem, n + 1)
                    g_sb.by(nc.scalar.activation(tg[:, n % 2, :], m.ps[:, 6, :], ACT.Tanh,
                                                 bias=gb[:, todo[n][1]:todo[n][1] + 1]))

                cap(0)
                for n in range(N):
                    i, step = tile_step(n)
                    if step == 0:
                        select_copy(nc, sc, m, q, i)
                    sc.wait_ge(biased.sem, n + 1)
                    if n >= 2:
                        sc.wait_ge(y_ps.sem, n - 1)
                    p_ready.by(nc.scalar.activation(p[:, n % 2, :], t[:, n % 2, :], ACT.Exp, scale=SOFTCAP))
                    if n + 1 < N:
                        cap(n + 1)
                    if n >= 1:
                        gating(n - 1)
                gating(N - 1)

            def normalise(v, n):
                v.wait_ge(y_ps.sem, n + 1)
                if n >= 2:
                    v.wait_ge(yT_ps.sem, n - 1)
                y3 = m.ps[:, 3, 0:3 * VW].rearrange("p (j d) -> p j d", d=VW)
                nc.vector.reciprocal(rd[:, n % 2, 0:3], y3[:, :, HD])
                dve.then_wait(v, nc.vector.reciprocal(rd[:, n % 2, 3:4], m.ps[:, 4, HD:HD + 1]))
                nc.vector.scalar_tensor_tensor(yn[:, n % 2, 0:3, :], y3[:, :, 0:HD], 0.5,
                                               spread(rd[:, n % 2, 0:3], 2, HD), ALU.mult, ALU.mult)
                y_sb.by(nc.vector.tensor_scalar(yn[:, n % 2, 3, :], m.ps[:, 4, 0:HD], rd[:, n % 2, 3:4], 0.5,
                                                ALU.mult, ALU.mult))

            @block.vector
            def _(v):

                def finish(n):
                    b, h = todo[n]
                    v.wait_ge(g_sb.sem, n + 1)
                    z_ready.by(nc.vector.scalar_tensor_tensor(m.qT[:, h, SEQ * b:SEQ * (b + 1)], tg[:, n % 2, :], 1.0,
                                                              yT[:, n % 2, :], ALU.add, ALU.mult))

                for n in range(N):
                    b, h = todo[n]
                    v.wait_ge(capped.sem, n + 1)
                    if n == AH:
                        v.wait_ge(q.biased.sem, TPH)
                    if n == 1:
                        v.wait_ge(m.attn_in.sem, 16 * ATTN_LOADS)
                        gb_ready.by(nc.vector.tensor_scalar(gb[:, :], m.gate_b[:, :], 0.5, None, ALU.mult))
                    biased.by(nc.vector.scalar_tensor_tensor(t[:, n % 2, :], m.bias[b], SLOPE[h] / SOFTCAP,
                                                             t[:, n % 2, :], ALU.mult, ALU.add))
                    if n >= 2:
                        finish(n - 2)
                    if n >= 1:
                        normalise(v, n - 1)
                    i, step = tile_step(n)
                    if 0 <= step < TURN:
                        select_rounds(nc, v, q, i, ROUNDS[step], ROUNDS[step + 1])
                    if step == TURN:
                        select_bias(nc, v, m, q, i)
                normalise(v, N - 1)
                finish(N - 2)
                finish(N - 1)


def attention_output(nc, m, a):
    with ExitStack() as ctx:
        sig = lambda name: Signal(ctx, nc, "out_" + name)
        sb = lambda name, shape: ctx.enter_context(nc.sbuf_tensor("out_" + name, shape, F32))
        work = ln_work(sb)
        o_ps, mv_ready, rs_ready, x_ready, xb, dve, pl = (sig(n) for n in ("o_ps", "mv_ready", "rs_ready", "x_ready",
                                                                          "xb", "dve8", "pool8"))
        with nc.Block() as block:
            @block.sync
            def _(sp):
                load_up_down(nc, m, a, sp)

            @block.tensor
            def _(pe):
                pe.wait_ge(m.wo_in.sem, 32)
                for i in range(TILES):
                    if i >= 2:
                        pe.wait_ge(mv_ready.sem, i - 1)
                    for h in range(AH):
                        last = nc.tensor.matmul(m.ps[:, i % 2, 0:DM], m.qT[:, h, P * i:P * (i + 1)], m.w_o[:, h, :],
                                                start=h == 0, stop=h == AH - 1)
                    o_ps.by(last)

            @block.vector
            def _(v):
                v.wait_ge(m.wo_in.sem, 32)
                for i in range(TILES):
                    xb.by(nc.vector.tensor_tensor(m.x[:, i, :], m.x[:, i, :], m.b_o[:, :], ALU.add))
                    v.wait_ge(o_ps.sem, i + 1)
                    v.wait_ge(xb.sem, i + 1)
                    if i >= 2:
                        v.wait_ge(x_ready.sem, i - 1)
                    dve.then_wait(v, nc.vector.tensor_tensor(work.r[:, i % 2, :], m.ps[:, i % 2, 0:DM], m.x[:, i, :],
                                                             ALU.add))
                    ln_stats(nc, v, work, i, dve, mv_ready)
                    ln_apply(nc, v, m, work, i, i, rs_ready, x_ready)

            @block.gpsimd
            def _(pool):
                for i in range(TILES):
                    ln_scale(nc, pool, m, work, i, pl, mv_ready, rs_ready)


def load_up_down(nc, m, a, sp):
    for h in range(2):
        e = slice(16 * h, 16 * h + 16)
        for k in range(KD):
            sp.dma_start(m.w_up_e[:, e, k, :], a["L1_ffn_W_up"][e, P * k:P * (k + 1), :].rearrange("e p i -> p e i")
                         ).then_inc(m.up_in.sem, 16)
    for h in range(2):
        e = slice(16 * h, 16 * h + 16)
        sp.dma_start(m.w_down_e[:, e, :], a["L1_ffn_W_down"][e, :, :].rearrange("e i d -> i e d")
                     ).then_inc(m.down_in.sem, 16)


def load_gate(nc, m, a, sp, half):
    e = slice(16 * half, 16 * half + 16)
    for k in range(KD):
        sp.dma_start(m.w_gate_e[:, e, k, :], a["L1_ffn_W_gate"][e, P * k:P * (k + 1), :].rearrange("e p i -> p e i")
                     ).then_inc(m.gate_in.sem, 16)


def route_and_run_experts(nc, m, a):
    with ExitStack() as ctx:
        sig = lambda name: Signal(ctx, nc, "moe_" + name)
        space = Space(m.free)
        sb = lambda name, shape: space.take(*shape)
        rw = sb("rw", [NE, DM])
        rT = sb("rT", [P, KD, NE])
        eb = sb("eb", [P, NE])
        before = sb("before", [P, P])
        every = sb("every", [P, P])
        lower = sb("lower", [P, NG, NG])
        iota = sb("iota", [P, CAP])
        own = sb("own", [P, ST, NE])
        restart = sb("restart", [P, TILES, NE])
        score = sb("score", [P, TILES, NE])
        info = sb("info", [P, TILES, 1 + NE])
        mk = sb("mk", [P, TILES, NE])
        pre = sb("pre", [P, TILES, NE])
        top = sb("top", [P, TILES, 8])
        gs = sb("gs", [P, 4, TILES * NG])
        cmp_ = sb("cmp", [P, 2, TILES, NG, NG])
        gm = sb("gm", [P, TILES * NG])
        cnt = sb("cnt", [P, TILES])
        pos = sb("pos", [P, TILES, NE])
        hot = sb("hot", [P, 2, NE, CAP])
        xp = sb("xp", [P, KD, SLOTS])
        sg = sb("sg", [P, 2, EG * CAP])
        hT = sb("hT", [P, SLOTS])
        sw = sb("sw", [P, ST, NE])
        c_in, xt_ps, xt_sb, rw_ps, rw_sb = (sig(n) for n in ("c_in", "xt_ps", "xt_sb", "rw_ps", "rw_sb"))
        l_ps, sc_ready, ready, dve, chosen, before_ps, info_ready = (sig(n) for n in (
            "l_ps", "sc_ready", "ready", "dve9", "chosen", "before_ps", "info_ready"))
        hot_ready, used, xp_sb = (sig(n) for n in ("hot_ready", "used", "xp_sb"))
        gu_ps, sg_ready, h_ready, yT_ps, yT_sb = (sig(n) for n in ("gu_ps", "sg_ready", "h_ready", "yT_ps", "yT_sb"))
        NGR = NE // EG
        with nc.Block() as block:
            @block.sync
            def _(sp):
                sp.dma_start(rw[:, :], a["L1_ffn_router_w"]).then_inc(c_in.sem, 16)
                sp.dma_start(eb[:, :], a["L1_ffn_e_bias"].partition_broadcast(P)).then_inc(c_in.sem, 16)
                sp.dma_start(before[:, :], a["c_before"]).then_inc(c_in.sem, 16)
                sp.dma_start(lower[:, :, :], a["c_lower"]).then_inc(c_in.sem, 16)
                sp.dma_start(iota[:, :], a["c_iota"][:, 0:CAP]).then_inc(c_in.sem, 16)
                sp.dma_start(own[:, :, :], a["c_own"]).then_inc(c_in.sem, 16)
                sp.dma_start(info[:, :, 0:1], a["c_token"], allow_slow_non_contiguous=True).then_inc(c_in.sem, 16)

            @block.tensor
            def _(pe):
                pe.wait_ge(c_in.sem, 16 * 7)
                transpose_rows(pe, nc, m, 0, lambda i: None, xt_ps)
                for k in range(KD):
                    last = nc.tensor.transpose(m.ps[:, 4, NE * k:NE * (k + 1)], rw[:, P * k:P * (k + 1)],
                                               m.ident[0:NE, 0:NE])
                rw_ps.by(last)
                pe.wait_ge(xt_sb.sem, 4)
                pe.wait_ge(rw_sb.sem, 1)
                for i in range(TILES):
                    for k in range(KD):
                        last = nc.tensor.matmul(m.ps[:, 5, NE * i:NE * (i + 1)], m.xT[:, k, P * i:P * (i + 1)],
                                                rT[:, k, :], start=k == 0, stop=k == KD - 1)
                l_ps.by(last)
                pe.wait_ge(chosen.sem, 1)
                pe.wait_ge(ready.sem, 1)
                for i in range(TILES):
                    for j in range(i + 1):
                        last = nc.tensor.matmul(m.ps[:, 4, NE * i:NE * (i + 1)], (before if j == i else every)[:, :],
                                                pre[:, j, :], start=j == 0, stop=j == i)
                before_ps.by(last)
                pe.wait_ge(info_ready.sem, 1)
                for i in range(TILES):
                    pe.wait_ge(hot_ready.sem, i + 1)
                    flat = hot[:, i % 2, :, :].rearrange("p e c -> p (e c)")
                    for k in range(KD):
                        for c in range(3):
                            w = min(512, SLOTS - 512 * c)
                            nc.tensor.matmul(m.ps[:, 3 * k + c, 0:w], m.x[:, i, P * k:P * (k + 1)],
                                             flat[:, 512 * c:512 * c + w], start=i == 0, stop=i == TILES - 1)
                    for s in range(ST):
                        last = nc.tensor.matmul(m.ps[:, 6, (1 + NE) * s:(1 + NE) * (s + 1)],
                                                flat[:, P * s:P * (s + 1)], info[:, i, :], start=i == 0 and s == 0,
                                                stop=i == TILES - 1, skip_group_check=True)
                    used.by(last)
                pe.wait_ge(xp_sb.sem, KD)
                pe.wait_ge(m.gate_in.sem, 16 * 2 * KD)
                pe.wait_ge(m.up_in.sem, 16 * 2 * KD)

                def down(g):
                    pe.wait_ge(h_ready.sem, g + 1)
                    if g == 0:
                        pe.wait_ge(m.down_in.sem, 32)
                    if g >= 1:
                        pe.wait_ge(yT_sb.sem, KD * g)
                    for k in range(KD):
                        for e in range(EG * g, EG * (g + 1)):
                            c = CAP * (e - EG * g)
                            last = nc.tensor.matmul(m.ps[:, 4 + k, c:c + CAP], m.w_down_e[:, e, P * k:P * (k + 1)],
                                                    hT[:, CAP * e:CAP * (e + 1)], start=True, stop=True)
                        yT_ps.by(last)

                for g in range(NGR):
                    if g >= 2:
                        pe.wait_ge(h_ready.sem, g - 1)
                    for n, wts in enumerate((m.w_gate_e, m.w_up_e)):
                        for e in range(EG * g, EG * (g + 1)):
                            c = CAP * (e - EG * g)
                            for k in range(KD):
                                last = nc.tensor.matmul(m.ps[:, 2 * (g % 2) + n, c:c + CAP], wts[:, e, k, :],
                                                        xp[:, k, CAP * e:CAP * (e + 1)], start=k == 0,
                                                        stop=k == KD - 1)
                        gu_ps.by(last)
                    if g >= 1:
                        down(g - 1)
                down(NGR - 1)

            def copy_down(sc, g):
                for k in range(KD):
                    sc.wait_ge(yT_ps.sem, KD * g + k + 1)
                    yT_sb.by(nc.scalar.copy(m.yT[:, k, EG * CAP * g:EG * CAP * (g + 1)], m.ps[:, 4 + k, 0:EG * CAP]))

            @block.scalar
            def _(sc):
                sc.wait_ge(rw_ps.sem, 1)
                rw_sb.by(nc.scalar.copy(rT[:, :, :].rearrange("p k e -> p (k e)"), m.ps[:, 4, 0:KD * NE]))
                sc.wait_ge(l_ps.sem, 1)
                sc_ready.by(nc.scalar.activation(score[:, :, :].rearrange("p i e -> p (i e)"),
                                                 m.ps[:, 5, 0:TILES * NE], ACT.Sigmoid))
                sc.wait_ge(used.sem, TILES)
                flat = m.ps[:, 0:6, :].rearrange("p (k b) n -> p k (b n)", k=KD)
                xp_sb.by(nc.scalar.copy(xp[:, 0, :], flat[:, 0, 0:SLOTS]))
                for g in range(NGR):
                    sc.wait_ge(gu_ps.sem, 2 * g + 1)
                    if g >= 2:
                        sc.wait_ge(h_ready.sem, g - 1)
                    sg_ready.by(nc.scalar.activation(sg[:, g % 2, :], m.ps[:, 2 * (g % 2), 0:EG * CAP], ACT.Sigmoid))
                    if g >= 1:
                        copy_down(sc, g - 1)
                copy_down(sc, NGR - 1)

            @block.gpsimd
            def _(pool):
                nc.gpsimd.memset(restart[:, :, 1:], 1.0)
                nc.gpsimd.memset(restart[:, :, 0:1], 0.0)
                ready.by(nc.gpsimd.memset(every[:, :], 1.0))

            @block.vector
            def _(v):
                step = lambda ins: dve.then_wait(v, ins)
                tt, ts, stt = nc.vector.tensor_tensor, nc.vector.tensor_scalar, nc.vector.scalar_tensor_tensor
                copy_transposed(v, nc.vector.tensor_copy, m, 0, xt_ps, xt_sb)
                v.wait_ge(c_in.sem, 16 * 7)
                v.wait_ge(sc_ready.sem, 1)
                step(tt(mk[:, :, :], score[:, :, :], spread(eb[:, :], 1, TILES), ALU.add))
                q = mk[:, :, :].rearrange("p i (g j) -> p (i g) j", j=NE // NG)
                nc.vector.tensor_tensor(gs[:, 0, :], q[:, :, 0], q[:, :, 1], ALU.max)
                nc.vector.tensor_tensor(gs[:, 1, :], q[:, :, 0], q[:, :, 1], ALU.min)
                nc.vector.tensor_tensor(gs[:, 2, :], q[:, :, 2], q[:, :, 3], ALU.max)
                step(tt(gs[:, 3, :], q[:, :, 2], q[:, :, 3], ALU.min))
                step(tt(gs[:, 3, :], gs[:, 1, :], gs[:, 3, :], ALU.max))
                step(tt(gs[:, 1, :], gs[:, 0, :], gs[:, 2, :], ALU.min))
                step(tt(gs[:, 1, :], gs[:, 1, :], gs[:, 3, :], ALU.max))
                step(tt(gs[:, 0, :], gs[:, 0, :], gs[:, 2, :], ALU.max))
                step(tt(gs[:, 0, :], gs[:, 0, :], gs[:, 1, :], ALU.add))
                g3 = gs[:, 0, :].rearrange("p (i g) -> p i g", g=NG)
                for i in range(TILES):
                    others, mine = spread(g3[:, i, :], 1, NG), spread(g3[:, i, :], 2, NG)
                    nc.vector.tensor_tensor(cmp_[:, 0, i, :, :], others, mine, ALU.is_gt)
                    last = nc.vector.tensor_tensor(cmp_[:, 1, i, :, :], others, mine, ALU.is_equal)
                step(last)
                c3 = lambda n: cmp_[:, n, :, :, :].rearrange("p i g h -> p i (g h)")
                step(tt(c3(1), c3(1), spread(lower[:, :, :].rearrange("p g h -> p (g h)"), 1, TILES), ALU.mult))
                step(tt(c3(0), c3(0), c3(1), ALU.add))
                step(nc.vector.tensor_reduce(gm[:, :], cmp_[:, 0, :, :, :].rearrange("p i g h -> p (i g) h"), AX.X,
                                             ALU.add))
                step(ts(gm[:, :], gm[:, :], TKG - 0.5, None, ALU.is_lt))
                step(tt(q, q, spread(gm[:, :], 2, NE // NG), ALU.mult))
                for i in range(TILES):
                    last = nc.vector.max(top[:, i, :], mk[:, i, :])
                step(last)
                fourth = spread(top[:, :, TOPK - 1], 2, NE)
                step(tt(pos[:, :, :], mk[:, :, :], fourth, ALU.is_gt))
                step(tt(mk[:, :, :], mk[:, :, :], fourth, ALU.is_equal))
                step(nc.vector.tensor_reduce(cnt[:, :], pos[:, :, :], AX.X, ALU.add))
                step(ts(cnt[:, :], cnt[:, :], -1.0, TOPK + 0.5, ALU.mult, ALU.add))
                v.wait_ge(ready.sem, 1)
                flat = lambda t: t[:, :, :].rearrange("p i e -> p (i e)")
                step(nc.vector.tensor_tensor_scan(flat(pre), flat(restart), flat(mk), 0.0, ALU.mult, ALU.add))
                step(tt(pre[:, :, :], pre[:, :, :], spread(cnt[:, :], 2, NE), ALU.is_lt))
                step(tt(pre[:, :, :], pre[:, :, :], mk[:, :, :], ALU.mult))
                chosen.then_wait(v, tt(pre[:, :, :], pre[:, :, :], pos[:, :, :], ALU.add))
                step(tt(mk[:, :, :], score[:, :, :], pre[:, :, :], ALU.mult))
                step(nc.vector.tensor_reduce(cnt[:, :], mk[:, :, :], AX.X, ALU.add))
                step(ts(cnt[:, :], cnt[:, :], 1e-20, None, ALU.add))
                step(nc.vector.reciprocal(cnt[:, :], cnt[:, :]))
                info_ready.then_wait(v, stt(info[:, :, 1:], mk[:, :, :], MSCALE, spread(cnt[:, :], 2, NE), ALU.mult,
                                            ALU.mult))
                v.wait_ge(before_ps.sem, 1)
                step(stt(flat(pos), m.ps[:, 4, 0:TILES * NE], 1.0, flat(pre), ALU.add, ALU.mult))
                step(ts(pos[:, :, :], pos[:, :, :], -1.0, None, ALU.add))
                for i in range(TILES):
                    if i >= 2:
                        v.wait_ge(used.sem, i - 1)
                    hot_ready.by(tt(hot[:, i % 2, :, :], spread(iota[:, :], 1, NE), spread(pos[:, i, :], 2, CAP),
                                    ALU.is_equal))
                v.wait_ge(used.sem, TILES)
                facts = m.ps[:, 6, 0:ST * (1 + NE)].rearrange("p (s e) -> p s e", e=1 + NE)
                ps3 = m.ps[:, 0:6, :].rearrange("p (k b) n -> p k (b n)", k=KD)
                xp_sb.by(nc.vector.tensor_copy(xp[:, 1, :], ps3[:, 1, 0:SLOTS]))
                m.slots_ready.by(nc.vector.tensor_copy(m.slot_token[:, :], facts[:, :, 0]))
                step(tt(sw[:, :, :], facts[:, :, 1:], own[:, :, :], ALU.mult))
                m.slots_ready.by(nc.vector.tensor_reduce(m.slot_weight[:, :], sw[:, :, :], AX.X, ALU.add))
                for g in range(NGR):
                    v.wait_ge(sg_ready.sem, g + 1)
                    step(tt(sg[:, g % 2, :], m.ps[:, 2 * (g % 2), 0:EG * CAP], sg[:, g % 2, :], ALU.mult))
                    v.wait_ge(gu_ps.sem, 2 * g + 2)
                    h_ready.by(tt(hT[:, EG * CAP * g:EG * CAP * (g + 1)], sg[:, g % 2, :],
                                  m.ps[:, 2 * (g % 2) + 1, 0:EG * CAP], ALU.mult))


def combine_and_store(nc, m, a, out):
    with ExitStack() as ctx:
        sig = lambda name: Signal(ctx, nc, "end_" + name)
        spaces = [Space(m.free), Space(m.weights), Space(m.kv)]
        sb = lambda name, shape: next(s for s in spaces if s.at + int(np.prod(shape[1:])) <= s.ap.shape[1]).take(*shape)
        w_row = sb("w_row", [P, 3, KD, DM])
        wT = sb("wT", [P, 3, KD, DM])
        token = sb("token", [P, NT])
        back = sb("back", [P, ST, NT])
        y = sb("y", [P, ST, DM])
        sg = sb("sg", [P, 2, 512])
        hs = sb("hs", [P, KD, NT])
        work = ln_work(sb)
        c_in, w_ps, w_sb, y_ps, y_sb, back_ready = (sig(n) for n in ("c_in", "w_ps", "w_sb", "y_ps", "y_sb",
                                                                    "back_ready"))
        gu_ps, sg_ready, gated, h_ready, o_ps = (sig(n) for n in ("gu_ps", "sg_ready", "gated", "h_ready", "o_ps"))
        mv_ready, rs_ready, x_ready, dve, pl = (sig(n) for n in ("mv_ready", "rs_ready", "x_ready", "dve10", "pool10"))
        with nc.Block() as block:
            @block.sync
            def _(sp):
                for n, name in enumerate(("gate", "up", "down")):
                    sp.dma_start(w_row[:, n, :, :], k_tiles(a["L1_ffn_shared_" + name])).then_inc(c_in.sem, 16)
                sp.dma_start(token[:, :], a["c_iota"]).then_inc(c_in.sem, 16)
                for i in range(TILES):
                    sp.wait_ge(x_ready.sem, i + 1)
                    sp.dma_start(rows(out)[:, i, :], m.x[:, i, :]).then_inc(m.stored.sem, 16)
                sp.wait_ge(m.stored.sem, 16 * TILES)

            @block.tensor
            def _(pe):
                for s in range(ST // 2):
                    for t in (2 * s, 2 * s + 1):
                        for k in range(KD):
                            c = DM * (t % 2) + P * k
                            last = nc.tensor.transpose(m.ps[:, s, c:c + P], m.yT[:, k, P * t:P * (t + 1)],
                                                       m.ident[:, :])
                    y_ps.by(last)
                pe.wait_ge(c_in.sem, 64)
                for n in range(3):
                    for j in range(KD):
                        for k in range(KD):
                            c = DM * k + P * j
                            last = nc.tensor.transpose(m.ps[:, 5 + n, c:c + P], w_row[:, n, j, P * k:P * (k + 1)],
                                                       m.ident[:, :])
                    w_ps.by(last)
                pe.wait_ge(w_sb.sem, 3)
                pe.wait_ge(y_sb.sem, ST // 2)
                for n in range(KD * HALVES):
                    j, h = n // HALVES, n % HALVES
                    if n >= 2:
                        pe.wait_ge(h_ready.sem, n - 1)
                    for u in range(2):
                        for k in range(KD):
                            last = nc.tensor.matmul(m.ps[:, 2 * (n % 2) + u, :], wT[:, u, k, P * j:P * (j + 1)],
                                                    m.xT[:, k, 512 * h:512 * (h + 1)], start=k == 0, stop=k == KD - 1)
                    gu_ps.by(last)
                pe.wait_ge(back_ready.sem, ST)
                for i in range(TILES):
                    if i == 0:
                        pe.wait_ge(h_ready.sem, KD * HALVES)
                    if i >= 2:
                        pe.wait_ge(mv_ready.sem, i - 1)
                    dst = m.ps[:, 4 + i % 2, 0:DM]
                    for s in range(ST):
                        nc.tensor.matmul(dst, back[:, s, P * i:P * (i + 1)], y[:, s, :], start=s == 0, stop=False)
                    for k in range(KD):
                        last = nc.tensor.matmul(dst, hs[:, k, P * i:P * (i + 1)], wT[:, 2, k, :], start=False,
                                                stop=k == KD - 1)
                    o_ps.by(last)

            @block.scalar
            def _(sc):
                for s in range(ST // 2):
                    sc.wait_ge(y_ps.sem, s + 1)
                    y_sb.by(nc.scalar.copy(y[:, 2 * s:2 * s + 2, :].rearrange("p s d -> p (s d)"), m.ps[:, s, :]))
                for n in range(3):
                    sc.wait_ge(w_ps.sem, n + 1)
                    w_sb.by(nc.scalar.copy(wT[:, n, :, :].rearrange("p k d -> p (k d)"), m.ps[:, 5 + n, :]))
                for n in range(KD * HALVES):
                    sc.wait_ge(gu_ps.sem, n + 1)
                    if n >= 2:
                        sc.wait_ge(h_ready.sem, n - 1)
                    sg_ready.by(nc.scalar.activation(sg[:, n % 2, :], m.ps[:, 2 * (n % 2), :], ACT.Sigmoid))

            @block.vector
            def _(v):
                v.wait_ge(c_in.sem, 64)
                for s in range(ST):
                    back_ready.by(nc.vector.tensor_scalar(back[:, s, :], token[:, :], m.slot_token[:, s:s + 1],
                                                          m.slot_weight[:, s:s + 1], ALU.is_equal, ALU.mult))
                for n in range(KD * HALVES):
                    j, h = n // HALVES, n % HALVES
                    v.wait_ge(sg_ready.sem, n + 1)
                    gated.then_wait(v, nc.vector.tensor_tensor(sg[:, n % 2, :], m.ps[:, 2 * (n % 2), :],
                                                               sg[:, n % 2, :], ALU.mult))
                    h_ready.by(nc.vector.tensor_tensor(hs[:, j, 512 * h:512 * (h + 1)], sg[:, n % 2, :],
                                                       m.ps[:, 2 * (n % 2) + 1, :], ALU.mult))
                for i in range(TILES):
                    v.wait_ge(o_ps.sem, i + 1)
                    if i >= 2:
                        v.wait_ge(x_ready.sem, i - 1)
                    dve.then_wait(v, nc.vector.tensor_tensor(work.r[:, i % 2, :], m.ps[:, 4 + i % 2, 0:DM],
                                                             m.x[:, i, :], ALU.add))
                    ln_stats(nc, v, work, i, dve, mv_ready)
                    ln_apply(nc, v, m, work, i, i, rs_ready, x_ready)

            @block.gpsimd
            def _(pool):
                for i in range(TILES):
                    ln_scale(nc, pool, m, work, i, pl, mv_ready, rs_ready)


def constants():
    p = np.arange(P)
    f = lambda x: np.ascontiguousarray(x, dtype=np.float32)
    c = {
        "c_ident": f(np.eye(P)),
        "c_eye_q": f(p[:, None] % Q == np.arange(Q)[None, :]),
        "c_sel_last": f(np.broadcast_to((p[:, None] == Q * np.arange(G)[None, :] + Q - 1)[:, :, None], (P, G, P))),
        "c_in_chunk": f(p[:, None] // Q == np.arange(G)[None, :]),
        "c_sel_chunk": f(np.arange(BATCH * CHUNKS)[:, None, None]
                         == G * np.arange(TILES)[None, :, None] + p[None, None, :] // Q),
        "c_first8": f(np.broadcast_to(LE - np.arange(LE), (P, LE))),
    }
    c["c_before"] = f(p[:, None] < p[None, :])
    c["c_lower"] = f(np.broadcast_to(np.arange(NG)[None, :] < np.arange(NG)[:, None], (P, NG, NG)))
    c["c_iota"] = f(np.broadcast_to(np.arange(NT), (P, NT)))
    c["c_token"] = f(p[:, None, None] + P * np.arange(TILES)[None, :, None])
    slot = p[:, None] + P * np.arange(ST)[None, :]
    c["c_own"] = f(slot[:, :, None] // CAP == np.arange(NE)[None, None, :])
    pos = np.arange(SEQ, dtype=np.float32)
    inv = (1.0 / np.power(np.float32(10000.0), np.arange(0, HD, 2, dtype=np.float32) / np.float32(HD))).astype(np.float32)
    ang = (pos[:, None] * np.concatenate([inv, inv])[None, 0::2]).astype(np.float32)
    cos, sin = np.repeat(np.cos(ang), 2, axis=1), np.repeat(np.sin(ang), 2, axis=1)
    sin = sin * np.where(np.arange(HD) % 2 == 0, -1.0, 1.0)
    c["c_cos"] = f(cos.reshape(TPH, P, HD).transpose(1, 0, 2))
    c["c_sin"] = f(sin.reshape(TPH, P, HD).transpose(1, 0, 2))
    dist = np.zeros((P, NCOL))
    for k in range(TPH):
        q = np.arange(P * k, SEQ)[None, :]
        key = P * k + p[:, None]
        dist[:, KEY_COL[k]:KEY_COL[k] + SEQ - P * k] = np.where(q >= key, -(q - key), LATER)
    c["c_dist"] = f(dist)
    return c


def build(nc, a, out, upto=99):
    ctx = ExitStack()
    with ctx:
        m = Memory()
        sb = lambda name, shape, dt=F32: ctx.enter_context(nc.sbuf_tensor(name, shape, dt))
        m.ps = ctx.enter_context(nc.psum_tensor("ps", [P, 8, 512], F32))
        m.x = sb("x", [P, TILES, DM])
        m.xT = sb("xT", [P, KD, NT])
        m.ident = sb("ident", [P, P])
        m.half = sb("half", [P, 1])
        m.wz_in, m.late_in, m.const_in, m.small_in = (Signal(ctx, nc, n) for n in ("wz_in", "late_in", "const_in",
                                                                                   "small_in"))
        m.lora_in, m.qkv_in, m.attn_in = (Signal(ctx, nc, n) for n in ("lora_in", "qkv_in", "attn_in"))
        m.wo_in, m.gate_in, m.up_in, m.down_in, m.stored, m.slots_ready = (Signal(ctx, nc, n) for n in (
            "wo_in", "gate_in", "up_in", "down_in", "stored", "slots_ready"))
        with ExitStack() as attention:
            sba = lambda name, shape: attention.enter_context(nc.sbuf_tensor(name, shape, F32))
            m.w_down = sba("w_down", [P, KD, LATENT])
            m.b_down = sba("b_down", [LATENT, 1])
            m.b_o = sba("b_o", [P, DM])
            m.gate_b = sba("gate_b", [P, AH])
            m.w_q = sba("w_q", [P, KD, AH * HD])
            first_layer(nc, m, a, upto)
            if upto < 5:
                return store(nc, m, out)
            m.qT = sba("qT", [P, AH, NT])
            m.kv = sba("kv", [P, NKV * NT + TILES * NKV * VW])
            m.kT = m.kv[:, 0:NKV * NT].rearrange("p (g t) -> p g t", t=NT)
            m.v = m.kv[:, NKV * NT:].rearrange("p (i g d) -> p i g d", g=NKV, d=VW)
            bias = sba("bias", [P, BATCH, NCOL])
            m.bias = [bias[:, b, :] for b in range(BATCH)]
            m.dist = m.bias[1]
            with ExitStack() as once:
                sbo = lambda name, shape: once.enter_context(nc.sbuf_tensor(name, shape, F32))
                m.w_up = sbo("w_up", [LATENT, 2 * NKV * HD])
                m.b_up = sbo("b_up", [P, 2 * NKV * HD])
                m.b_q = sbo("b_q", [P, AH * HD])
                m.norm_qk = sbo("norm_qk", [P, 2, HD])
                m.cos_row = sbo("cos_row", [P, TPH, HD])
                m.sin_row = sbo("sin_row", [P, TPH, HD])
                prepare_attention(nc, m, a)
            m.w_o = m.w_q[:, :, :].rearrange("p k (h n) -> p (k h) n", n=DM)
            m.gate_w = m.xT[:, :, :].rearrange("p k (h e) -> p (k h) e", e=HD)
            m.weights = sba("weights", [P, 2 * NE * DM])
            m.rows = m.weights[:, 0:NE * DM]
            m.w_gate_e = m.weights[:, NE * DM:].rearrange("p (e k i) -> p e k i", k=KD, i=EI)
            m.w_up_e = m.kv[:, 0:NE * KD * EI].rearrange("p (e k i) -> p e k i", k=KD, i=EI)
            m.w_down_e = m.rows.rearrange("p (e d) -> p e d", d=DM)
            attend(nc, m, a)
            attention_output(nc, m, a)
            nc.all_engine_barrier(sems_to_clear=range(m.slots_ready.sem.num + 1, SEMAPHORES))
            spare = m.qT[:, :, :].rearrange("p h t -> p (h t)")
            m.yT = spare[:, 0:KD * SLOTS].rearrange("p (k s) -> p k s", k=KD)
            m.free = spare[:, KD * SLOTS:]
            m.slot_token = sba("slot_token", [P, ST])
            m.slot_weight = sba("slot_weight", [P, ST])
            route_and_run_experts(nc, m, a)
            combine_and_store(nc, m, a, out)


def first_layer(nc, m, a, upto):
        with ExitStack() as lora:
            sbl = lambda name, shape: lora.enter_context(nc.sbuf_tensor(name, shape, F32))
            m.lw_a = sbl("lw_a", [P, LE * LR // P, DM])
            m.lw_b = sbl("lw_b", [P, KD, LE, LR])
            m.lw_g = sbl("lw_g", [LE, DM])
            m.first8 = sbl("first8", [P, LE])
            mixer_layer(nc, m, a, upto)
            if upto >= 4:
                lora_experts(nc, m, a)


def mixer_layer(nc, m, a, upto):
        with ExitStack() as mixer:
            sbm = lambda name, shape: mixer.enter_context(nc.sbuf_tensor(name, shape, F32))
            m.w_in = sbm("w_in", [P, KD, PROJ])
            m.w_out = sbm("w_out", [P, INTER // P, DM])
            m.norm_w = sbm("norm_w", [P, INTER // P])
            m.conv_w = sbm("conv_w", [P, CT, KCONV])
            m.conv_b = sbm("conv_b", [P, CT])
            m.d_row = sbm("d_row", [P, HEADS])
            m.eye_q = sbm("eye_q", [P, Q])
            m.sel_last = sbm("sel_last", [P, G, P])
            m.in_chunk = sbm("in_chunk", [P, G])
            m.sel_chunk = sbm("sel_chunk", [BATCH * CHUNKS, TILES, P])
            m.xc = sbm("xc", [P, CT, NT])
            m.dtT = sbm("dtT", [HEADS, NT])
            m.sinceT = sbm("sinceT", [HEADS, NT])
            m.da_chunk = sbm("da_chunk", [BATCH * CHUNKS, HEADS, Q])
            m.x_row = sbm("x_row", [P, TILES, INTER])
            m.b_row = sbm("b_row", [P, TILES, NSTATE])
            m.since_row = sbm("since_row", [P, TILES, HEADS])
            m.da_dram = nc.dram_tensor("da_dram", (HEADS, NT), F32, kind="Internal").ap()
            project_and_convolve(nc, m, a)
            with ExitStack() as pair:
                m.dt_end = pair.enter_context(nc.sbuf_tensor("dt_end", [P, TILES, HEADS, PDIM], F32))
                if upto >= 2:
                    within_chunks(nc, m, a)
                if upto >= 3:
                    carry_states(nc, m, a)


def store(nc, m, out):
    with ExitStack() as ctx:
        stored = Signal(ctx, nc, "stored")
        with nc.Block() as block:
            @block.sync
            def _(sp):
                sp.dma_start(rows(out), m.x[:, :, :]).then_inc(stored.sem, 16)
                sp.wait_ge(stored.sem, 16)


def kernel(**inputs):
    import concourse.bacc as bacc
    from concourse.bass_utils import run_bass_kernel_spmd

    nc = bacc.Bacc("TRN2", target_bir_lowering=False, num_devices=1)
    arrays, a = {}, {}
    for name, value in {**inputs, **constants()}.items():
        value = np.ascontiguousarray(value)
        arrays[f"in_{name}"] = value
        a[name] = nc.dram_tensor(f"in_{name}", value.shape, mybir.dt.from_np(value.dtype), kind="ExternalInput").ap()
    a["x"] = a["L0_attn_hidden_states"].rearrange("b t d -> (b t) d")
    out = nc.dram_tensor("out_0", (BATCH, SEQ, DM), F32, kind="ExternalOutput").ap()
    build(nc, a, out.rearrange("b t d -> (b t) d"))
    results = run_bass_kernel_spmd(nc, [arrays], core_ids=[0]).results
    return results[0]["out_0"]
```

```python
from contextlib import ExitStack

import numpy as np

import concourse.bass as bass
from concourse import mybir

F32 = mybir.dt.float32
U32 = mybir.dt.uint32
ALU = mybir.AluOpType
ACT = mybir.ActivationFunctionType
AX = mybir.AxisListType

P = 128
BATCH, SEQ, DM = 2, 512, 256
NT = BATCH * SEQ
TILES = NT // P
HALVES = NT // 512
KD = DM // P
TPH = TILES // HALVES

INTER, HEADS, PDIM, NSTATE, KCONV = 512, 64, 8, 128, 4
CONV = INTER + 2 * NSTATE
CT = CONV // P
PROJ = 2 * INTER + 2 * NSTATE + HEADS
Q = 32
G = P // Q
CHUNKS = SEQ // Q
HQ = 16
RING = 8

LE, LR, LSCALE = 8, 64, 64.0 / 16.0

AH, HD, NKV, LATENT = 16, 128, 4, 64
KVG = AH // NKV
QKH = AH + NKV
SEL_TOPK, SEL_DIM = 64, 64
SOFTCAP = 30.0
SLOPE = [2.0 ** (-8.0 * (h + 1) / AH) for h in range(AH)]
KEY_COL = [0, 512, 1024, 896]
NCOL = 1280
VW = HD + 1
LATER, TAKEN, FAR = -1e30, -3e38, -1e30

NE, NG, TKG, TOPK, MSCALE = 32, 8, 3, 4, 2.5
CAP = -(-5 * NT // (4 * NE))
SLOTS = NE * CAP
ST = SLOTS // P
EI = 128
PAIR_ROWS = P // 2

LN_EPS = 1e-5
SEMAPHORES = 256


class Signal:

    def __init__(self, ctx, nc, name):
        self.sem = ctx.enter_context(nc.semaphore(name))
        self.n = 0

    def by(self, ins):
        ins.then_inc(self.sem, 1)
        self.n += 1

    def then_wait(self, eng, ins):
        self.by(ins)
        eng.wait_ge(self.sem, self.n)


def spread(ap, axis, n):
    a = ap.unsqueeze(axis)
    shape = list(a.shape)
    shape[axis] = n
    return a.broadcast_to(shape)


class Memory:
    pass


class Space:

    def __init__(self, ap):
        self.ap, self.at = ap, 0

    def fits(self, shape):
        return self.at + int(np.prod(shape[1:])) <= self.ap.shape[1]

    def take(self, parts, *shape):
        n = int(np.prod(shape))
        assert self.at + n <= self.ap.shape[1], (self.at, n)
        piece = self.ap[0:parts, self.at:self.at + n]
        self.at += n
        names = "abcd"[:len(shape)]
        if len(shape) > 1:
            piece = piece.rearrange(f"p ({' '.join(names)}) -> p {' '.join(names)}",
                                    **{k: v for k, v in zip(names[1:], shape[1:])})
        return piece


def rows(dram):
    return dram.rearrange("(i p) d -> p i d", p=P)


def k_tiles(dram):
    return dram.rearrange("(k p) n -> p k n", p=P)


def transpose_rows(pe, nc, m, bank, ready, done):
    for h in range(HALVES):
        for k in range(KD):
            for j in range(TPH):
                i = h * TPH + j
                ready(i)
                last = nc.tensor.transpose(m.ps[:, bank + h * KD + k, P * j:P * (j + 1)],
                                           m.x[:, i, P * k:P * (k + 1)], m.ident[:, :])
            done.by(last)


def copy_transposed(eng, copy, m, bank, transposed, copied):
    for h in range(HALVES):
        for k in range(KD):
            n = h * KD + k
            eng.wait_ge(transposed.sem, n + 1)
            copied.by(copy(m.xT[:, k, 512 * h:512 * (h + 1)], m.ps[:, bank + n, :]))


def load_decay(nc, m, sp, i):
    for g in range(G):
        sp.dma_start(m.decay[Q * g:Q * (g + 1), i % 2, :, :].rearrange("p h t -> p (h t)"),
                     m.da_dram[G * i + g, :, :].rearrange("h t -> (h t)").partition_broadcast(Q)
                     ).then_inc(m.decay_in[i % 2].sem, 16)


def project_and_convolve(nc, m, a):
    with ExitStack() as ctx:
        sig = lambda name: Signal(ctx, nc, "proj_" + name)
        sb = lambda name, shape: ctx.enter_context(nc.sbuf_tensor("proj_" + name, shape, F32))
        raw = sb("raw", [P, CT, BATCH, KCONV - 1 + SEQ])
        acc = sb("acc", [P, 4, NT])
        th = sb("th", [P, 2, NT])
        hb = sb("hb", [P, CT])
        al = sb("al", [P, 2])
        dtb = sb("dtb", [P, 1])
        u = sb("u", [P, SEQ])
        e = sb("e", [P, SEQ])
        w = sb("w", [P, SEQ])
        lw = sb("lw", [P, SEQ])
        d1 = sb("d1", [P, SEQ])
        eq = sb("eq", [P, SEQ])

        x_in, w_in, ct_in = sig("x_in"), sig("w_in"), sig("ct_in")
        small_in, dt_in = m.small_in, m.dt_in
        xt_ps, xt_sb = sig("xt_ps"), sig("xt_sb")
        proj_ps, raw_sb, dt_sb = sig("proj_ps"), sig("raw_sb"), sig("dt_sb")
        pad_zero, dve, act = sig("pad_zero"), sig("dve1"), sig("act1")
        e_ready, w_ready, lw_ready, dt_ready, da_ready = (sig(n) for n in
                                                          ("e_ready", "w_ready", "lw_ready", "dt_ready", "da_ready"))
        daz_ready, daz_out = sig("daz_ready"), sig("daz_out")
        a_ready, conv_done, tapped, th_ready, silu_done, hb_ready = (sig(n) for n in
                                                           ("a_ready", "conv_done", "tapped", "th_ready",
                                                            "silu_done", "hb_ready"))
        order = [4, 5, 0, 1, 2, 3]
        W_DT = PROJ - HEADS

        with nc.Block() as block:
            @block.sync
            def _(sp):
                sp.dma_start(m.ident[:, :], a["c_ident"]).then_inc(x_in.sem, 16)
                for h in range(HALVES):
                    sp.dma_start(m.x[:, TPH * h:TPH * (h + 1), :],
                                 rows(a["x"])[:, TPH * h:TPH * (h + 1), :]).then_inc(x_in.sem, 16)
                sp.dma_start(m.w_in[:, :, INTER:PROJ], k_tiles(a["L0_attn_in_proj_w"])[:, :, INTER:PROJ]
                             ).then_inc(w_in.sem, 16)
                sp.dma_start(m.w_in[:, :, 0:INTER], k_tiles(a["L0_attn_in_proj_w"])[:, :, 0:INTER]
                             ).then_inc(m.wz_in.sem, 16)
                sp.dma_start(m.w_out[:, :, :], k_tiles(a["L0_attn_out_proj_w"])).then_inc(m.late_in.sem, 16)
                sp.dma_start(m.norm_w[:, :], a["L0_attn_norm_w"].rearrange("(k p) -> p k", p=P),
                             allow_slow_non_contiguous=True).then_inc(m.late_in.sem, 16)
                load_lora(nc, m, a, sp)
                sp.wait_ge(daz_ready.sem, 1)
                for b in range(BATCH):
                    sp.dma_start(m.da_dram[CHUNKS * b:CHUNKS * (b + 1), :, :].rearrange("c h t -> h c t"),
                                 w[HEADS * b:HEADS * (b + 1), :].rearrange("h (c t) -> h c t", t=Q),
                                 allow_slow_non_contiguous=True).then_inc(daz_out.sem, 16)
                sp.wait_ge(daz_out.sem, 32)
                for i in range(2):
                    load_decay(nc, m, sp, i)

            @block.gpsimd
            def _(pool):
                for b in range(BATCH):
                    own = slice(HEADS * b, HEADS * (b + 1))
                    pool.dma_start(al[own, 0:1], a["L0_attn_A_log"].unsqueeze(1),
                                   allow_slow_non_contiguous=True).then_inc(dt_in.sem, 16)
                    pool.dma_start(dtb[own, :], a["L0_attn_dt_bias"].unsqueeze(1),
                                   allow_slow_non_contiguous=True).then_inc(dt_in.sem, 16)
                pool.dma_start(m.conv_w[:, :, :], a["L0_attn_conv_w"].rearrange("(c p) k -> p c k", p=P),
                               allow_slow_non_contiguous=True).then_inc(small_in.sem, 16)
                pool.dma_start(m.conv_b[:, :], a["L0_attn_conv_b"].rearrange("(c p) -> p c", p=P),
                               allow_slow_non_contiguous=True).then_inc(small_in.sem, 16)
                pool.dma_start(m.d_row[:, :], a["L0_attn_D"].partition_broadcast(P)).then_inc(m.const_in.sem, 16)
                for t, name in ((m.eye_q[:, :], "c_eye_q"), (m.sel_last[:, :, :], "c_sel_last"),
                                (m.in_chunk[:, :], "c_in_chunk")):
                    pool.dma_start(t, a[name]).then_inc(m.const_in.sem, 16)
                pad_zero.by(nc.gpsimd.memset(raw[:, :, :, 0:KCONV - 1], 0.0))
                pad_zero.by(nc.gpsimd.memset(m.half[:, :], -0.5))
                pad_zero.by(nc.gpsimd.memset(d1[:, :], 0.0))

            @block.tensor
            def _(pe):
                pe.wait_ge(x_in.sem, 48)
                transpose_rows(pe, nc, m, 0, lambda i: None, xt_ps)
                pe.wait_ge(w_in.sem, 16)
                pe.wait_ge(xt_sb.sem, 4)
                n = 0
                for h in range(HALVES):
                    for k in range(KD):
                        last = nc.tensor.matmul(m.ps[HEADS * h:HEADS * (h + 1), 4 + n, :], m.w_in[:, k, W_DT:PROJ],
                                                m.xT[:, k, 512 * h:512 * (h + 1)], start=k == 0, stop=k == KD - 1)
                    proj_ps.by(last)
                    n += 1
                for ct in order:
                    for h in range(HALVES):
                        if n >= 8:
                            if n < 10:
                                pe.wait_ge(dt_sb.sem, n - 7)
                            else:
                                pe.wait_ge(raw_sb.sem, n - 9)
                        for k in range(KD):
                            last = nc.tensor.matmul(m.ps[:, (4 + n) % 8, :],
                                                    m.w_in[:, k, INTER + P * ct:INTER + P * (ct + 1)],
                                                    m.xT[:, k, 512 * h:512 * (h + 1)], start=k == 0, stop=k == KD - 1)
                        proj_ps.by(last)
                        n += 1

            @block.scalar
            def _(sc):
                sc.wait_ge(dt_in.sem, 64)
                act.then_wait(sc, nc.scalar.activation(al[:, 1:2], al[:, 0:1], ACT.Exp))
                a_ready.by(nc.scalar.mul(al[:, 0:1], al[:, 1:2], -1.0))
                sc.wait_ge(dt_sb.sem, 2)
                act.then_wait(sc, nc.scalar.activation(e[:, :], u[:, :], ACT.Abs))
                e_ready.by(nc.scalar.activation(e[:, :], e[:, :], ACT.Exp, scale=-1.0))
                sc.wait_ge(pad_zero.sem, 1)

                def copy_raw(n):
                    ct, h = order[n // 2], n % 2
                    sc.wait_ge(proj_ps.sem, n + 3)
                    raw_sb.by(nc.scalar.activation(raw[:, ct, h, KCONV - 1:], m.ps[:, (6 + n) % 8, :],
                                                   ACT.Copy, scale=0.25))

                def first_tap(n):
                    ct = order[n]
                    if n >= 4:
                        sc.wait_ge(silu_done.sem, n - 3)
                    tapped.by(nc.scalar.activation(acc[:, n % 4, :].rearrange("p (b t) -> p b t", b=BATCH),
                                                   raw[:, ct, :, 0:SEQ], ACT.Identity, scale=m.conv_w[:, ct, 0:1],
                                                   bias=hb[:, ct:ct + 1]))

                for n in range(4):
                    copy_raw(n)
                sc.wait_ge(raw_sb.sem, 4)
                sc.wait_ge(small_in.sem, 32)
                hb_ready.then_wait(sc, nc.scalar.mul(hb[:, :], m.conv_b[:, :], 0.5))
                first_tap(0)
                first_tap(1)
                sc.wait_ge(w_ready.sem, 1)
                lw_ready.by(nc.scalar.activation(lw[:, :], w[:, :], ACT.Ln))
                for n in range(4, 12):
                    copy_raw(n)
                sc.wait_ge(raw_sb.sem, 12)
                first_tap(2)
                first_tap(3)
                sc.wait_ge(dt_ready.sem, 1)
                sc.wait_ge(a_ready.sem, 1)
                da_ready.by(nc.scalar.activation(w[:, :], m.dtT[:, :], ACT.Exp, scale=al[:, 0:1]))
                for n, ct in enumerate(order):
                    sc.wait_ge(conv_done.sem, n + 1)
                    if n >= 2:
                        sc.wait_ge(silu_done.sem, n - 1)
                    th_ready.by(nc.scalar.activation(th[:, n % 2, :], acc[:, n % 4, :], ACT.Tanh))
                    if n + 4 < CT:
                        first_tap(n + 4)

            @block.vector
            def _(v):
                copy_transposed(v, nc.vector.tensor_copy, m, 0, xt_ps, xt_sb)
                v.wait_ge(dt_in.sem, 64)
                for h in range(HALVES):
                    v.wait_ge(proj_ps.sem, h + 1)
                    own = slice(HEADS * h, HEADS * (h + 1))
                    dt_sb.by(nc.vector.tensor_scalar(u[own, :], m.ps[own, 4 + h, :], dtb[own, 0:1], None, ALU.add))
                v.wait_ge(e_ready.sem, 1)
                w_ready.then_wait(v, nc.vector.tensor_scalar(w[:, :], e[:, :], 1.0, None, ALU.add))
                v.wait_ge(pad_zero.sem, 3)

                def convolve(n):
                    ct = order[n]
                    v.wait_ge(raw_sb.sem, 2 * n + 2)
                    out = acc[:, n % 4, :].rearrange("p (b t) -> p b t", b=BATCH)
                    v.wait_ge(tapped.sem, n + 1)
                    for k in range(1, KCONV):
                        last = nc.vector.scalar_tensor_tensor(out, raw[:, ct, :, k:k + SEQ], m.conv_w[:, ct, k:k + 1],
                                                              out, ALU.mult, ALU.add)
                        (conv_done if k == KCONV - 1 else dve).then_wait(v, last)

                def finish_silu(n):
                    v.wait_ge(th_ready.sem, n + 1)
                    silu_done.by(nc.vector.scalar_tensor_tensor(m.xc[:, order[n], :], th[:, n % 2, :], 1.0,
                                                                acc[:, n % 4, :], ALU.add, ALU.mult))

                v.wait_ge(small_in.sem, 32)
                convolve(0)
                v.wait_ge(lw_ready.sem, 1)
                dve.then_wait(v, nc.vector.tensor_scalar(w[:, :], w[:, :], -1.0, None, ALU.add))
                dve.then_wait(v, nc.vector.tensor_scalar(eq[:, :], w[:, :], 0.0, None, ALU.is_equal))
                nc.vector.tensor_tensor(lw[:, :], lw[:, :], eq[:, :], ALU.add).then_inc(dve.sem, 1)
                dve.n += 1
                dve.then_wait(v, nc.vector.tensor_tensor(w[:, :], w[:, :], eq[:, :], ALU.add))
                dve.then_wait(v, nc.vector.reciprocal(w[:, :], w[:, :]))
                dve.then_wait(v, nc.vector.tensor_tensor(lw[:, :], lw[:, :], w[:, :], ALU.mult))
                dve.then_wait(v, nc.vector.tensor_tensor(lw[:, :], lw[:, :], e[:, :], ALU.mult))
                dt_ready.by(nc.vector.scalar_tensor_tensor(m.dtT[:, :], u[:, :], 0.0, lw[:, :], ALU.max, ALU.add))
                convolve(1)
                v.wait_ge(da_ready.sem, 1)
                starts = lambda t: t[:, :].rearrange("h (c t) -> h c t", t=Q)[:, :, 0:1]
                dve.then_wait(v, nc.vector.tensor_copy(starts(d1), starts(w)))
                daz_ready.then_wait(v, nc.vector.memset(starts(w), 0.0))
                dve.by(nc.vector.tensor_tensor_scan(m.sinceT[:, :], w[:, :], d1[:, :], 0.0, ALU.mult, ALU.add))
                for n in range(2, CT):
                    finish_silu(n - 2)
                    convolve(n)
                finish_silu(CT - 2)
                finish_silu(CT - 1)


def within_chunks(nc, m, a):
    with ExitStack() as ctx:
        sig = lambda name: Signal(ctx, nc, "chunk_" + name)
        sb = lambda name, shape: ctx.enter_context(nc.sbuf_tensor("chunk_" + name, shape, F32))
        eye = sb("eye", [P, HQ, Q])
        gram = sb("gram", [P, 2, Q])
        dec = sb("dec", [P, 2, HEADS, Q])
        mix = sb("mix", [P, 2, HEADS, Q])
        dtx = sb("dtx", [P, 2, HEADS, PDIM])
        dtd = sb("dtd", [P, 2, HEADS, G, PDIM])
        dt_row = sb("dt_row", [P, TILES, HEADS])

        b_ps, b_sb, row_ps, row_sb = sig("b_ps"), sig("b_sb"), sig("row_ps"), sig("row_sb")
        x_ps, x_sb, gram_ps, gram_sb = sig("x_ps"), sig("x_sb"), sig("gram_ps"), sig("gram_sb")
        scanned, mixed, dtx_ready, spreaded = (sig(n) for n in ("scanned", "mixed", "dtx_ready", "spreaded"))
        intra_ps, intra_sb, dtf_ready, eye_ready = (sig(n) for n in ("intra_ps", "intra_sb", "dtf_ready", "eye_ready"))
        NQ = HEADS // HQ
        with nc.Block() as block:
            @block.sync
            def _(sp):
                for i in range(2, TILES):
                    sp.wait_ge(scanned.sem, NQ * (i - 1))
                    load_decay(nc, m, sp, i)

            @block.tensor
            def _(pe):
                for i in range(TILES):
                    last = nc.tensor.transpose(m.ps[:, 4 + i // 4, P * (i % 4):P * (i % 4 + 1)],
                                               m.xc[:, 4, P * i:P * (i + 1)], m.ident[:, :])
                b_ps.by(last)
                for bank, src in ((6, m.dtT), (7, m.sinceT)):
                    by_tile = m.ps[:, bank, :].rearrange("p (b j h) -> p j b h", b=BATCH, j=TPH)
                    for j in range(TPH):
                        last = nc.tensor.transpose(by_tile[:, j, :, :], src[:, P * j:P * (j + 1)], m.ident[:, :])
                row_ps.by(last)
                pe.wait_ge(m.const_in.sem, 16 * 4)

                def feed(i):
                    if i >= 1:
                        pe.wait_ge(x_sb.sem, i)
                        pe.wait_ge(gram_sb.sem, i)
                    for c in range(4):
                        last = nc.tensor.transpose(m.ps[:, 2, P * c:P * (c + 1)], m.xc[:, c, P * i:P * (i + 1)],
                                                   m.ident[:, :])
                    x_ps.by(last)
                    t = slice(P * i, P * (i + 1))
                    gram_ps.by(nc.tensor.matmul(m.ps[:, 3, 0:P], m.xc[:, 4, t], m.xc[:, 5, t], start=True, stop=True))
                feed(0)
                pe.wait_ge(b_sb.sem, 2)
                pe.wait_ge(row_sb.sem, 2)
                for i in range(TILES):
                    if i + 1 < TILES:
                        feed(i + 1)
                    pe.wait_ge(mixed.sem, i + 1)
                    pe.wait_ge(spreaded.sem, i + 1)
                    if i >= 2:
                        pe.wait_ge(intra_sb.sem, G * (i - 1))
                    own = slice(Q * (i % 2), Q * (i % 2 + 1))
                    for h in range(HEADS):
                        last = nc.tensor.matmul(m.ps[own, 4 + h // HQ, (G * PDIM) * (h % HQ):(G * PDIM) * (h % HQ + 1)],
                                                mix[:, i % 2, h, :],
                                                dtd[:, i % 2, h, :, :].rearrange("p g d -> p (g d)"),
                                                start=True, stop=True)
                    intra_ps.by(last)

            @block.scalar
            def _(sc):
                sc.wait_ge(b_ps.sem, 1)
                for j in range(2):
                    b_sb.by(nc.scalar.copy(m.b_row[:, 4 * j:4 * j + 4, :].rearrange("p i n -> p (i n)"),
                                           m.ps[:, 4 + j, :]))
                sc.wait_ge(row_ps.sem, 1)
                row_sb.by(nc.scalar.copy(dt_row[:, :, :].rearrange("p i h -> p (i h)"), m.ps[:, 6, :]))
                row_sb.by(nc.scalar.copy(m.since_row[:, :, :].rearrange("p i h -> p (i h)"), m.ps[:, 7, :]))

                def intra_out(i):
                    sc.wait_ge(intra_ps.sem, i + 1)
                    src = m.ps[Q * (i % 2):Q * (i % 2 + 1), 4:8, :].rearrange("t b (h g d) -> t b h g d", g=G, d=PDIM)
                    for g in range(G):
                        dst = m.xc[Q * g:Q * (g + 1), 0:4, P * i:P * (i + 1)]
                        intra_sb.by(nc.scalar.copy(dst.rearrange("t b (h d) -> t b h d", d=PDIM), src[:, :, :, g, :]))

                def feed_out(i):
                    sc.wait_ge(x_ps.sem, i + 1)
                    x_sb.by(nc.scalar.copy(m.x_row[:, i, :], m.ps[:, 2, :]))
                    sc.wait_ge(gram_ps.sem, i + 1)
                    if i >= 2:
                        sc.wait_ge(mixed.sem, i - 1)
                    for g in range(G):
                        last = nc.scalar.copy(gram[Q * g:Q * (g + 1), i % 2, :],
                                              m.ps[Q * g:Q * (g + 1), 3, Q * g:Q * (g + 1)])
                    gram_sb.by(last)

                feed_out(0)
                for i in range(TILES):
                    sc.wait_ge(dtx_ready.sem, i + 1)
                    if i >= 2:
                        sc.wait_ge(intra_ps.sem, i - 1)
                    for g in range(G):
                        last = nc.scalar.activation(dtd[:, i % 2, :, g, :], dtx[:, i % 2, :, :], ACT.Copy,
                                                    scale=m.in_chunk[:, g:g + 1])
                    spreaded.by(last)
                    if i + 1 < TILES:
                        feed_out(i + 1)
                    if i >= 1:
                        intra_out(i - 1)
                intra_out(TILES - 1)

            @block.vector
            def _(v):
                v.wait_ge(m.const_in.sem, 16 * 4)
                eye_ready.then_wait(v, nc.vector.tensor_copy(eye[:, :, :], spread(m.eye_q[:, :], 1, HQ)))
                v.wait_ge(row_sb.sem, 2)
                for i in range(TILES):
                    v.wait_ge(x_sb.sem, i + 1)
                    if i >= 2:
                        v.wait_ge(spreaded.sem, i - 1)
                    dtx_ready.by(nc.vector.tensor_tensor(
                        dtx[:, i % 2, :, :], m.x_row[:, i, :].rearrange("p (h d) -> p h d", d=PDIM),
                        spread(dt_row[:, i, :], 2, PDIM), ALU.mult))
                    if i >= 2:
                        v.wait_ge(mixed.sem, i - 1)
                    v.wait_ge(m.decay_in[i % 2].sem, 16 * G * (i // 2 + 1))
                    for q in range(NQ):
                        scanned.by(nc.vector.tensor_tensor_scan(
                            dec[:, i % 2, HQ * q:HQ * (q + 1), :].rearrange("p h t -> p (h t)"),
                            m.decay[:, i % 2, HQ * q:HQ * (q + 1), :].rearrange("p h t -> p (h t)"), eye[:, :, :].rearrange("p h t -> p (h t)"),
                            0.0, ALU.mult, ALU.add))
                    v.wait_ge(scanned.sem, NQ * (i + 1))
                    dtf_ready.by(nc.vector.tensor_tensor(m.dt_end[:, i, :, :], dtx[:, i % 2, :, :],
                                                         spread(dec[:, i % 2, :, Q - 1], 2, PDIM), ALU.mult))

            @block.gpsimd
            def _(pool):
                for i in range(TILES):
                    if i >= 2:
                        pool.wait_ge(intra_ps.sem, i - 1)
                    pool.wait_ge(scanned.sem, NQ * (i + 1))
                    pool.wait_ge(gram_sb.sem, i + 1)
                    mixed.by(nc.gpsimd.tensor_tensor(mix[:, i % 2, :, :], dec[:, i % 2, :, :],
                                                     spread(gram[:, i % 2, :], 1, HEADS), ALU.mult))


def carry_states(nc, m, a):
    with ExitStack() as ctx:
        sig = lambda name: Signal(ctx, nc, "state_" + name)
        sb = lambda name, shape: ctx.enter_context(nc.sbuf_tensor("state_" + name, shape, F32))
        st = sb("st", [P, BATCH, RING, HEADS, PDIM])
        tmp = sb("tmp", [P, 2, HEADS, PDIM])
        y = sb("y", [P, 2, HEADS, PDIM])
        xd = sb("xd", [P, 2, HEADS, PDIM])
        th = sb("thz", [P, 2, INTER])
        zs = sb("zs", [P, 2, INTER])
        sq = sb("sq", [P, INTER])
        ss = sb("ss", [P, TILES])
        rms = sb("rms", [P, TILES])
        gt = sb("gt", [P, 2, INTER])
        r = sb("r", [P, 2, DM])
        bs = sb("bs", [P, 2, 6])
        mv = sb("mv", [P, 2, 2])
        rs = sb("rs", [P, 2, 1])

        zero, decay_ps, new_ps, carried, inter_ps = (sig(n) for n in ("zero", "decay_ps", "new_ps", "carried",
                                                                      "inter_ps"))
        y1, y2, xd_ready, z_ps, th_ready, zs_ready = (sig(n) for n in ("y1", "y2", "xd_ready", "z_ps", "th_ready",
                                                                       "zs_ready"))
        ss_ready, gated, gt_ps, gt_sb, out_ps, rms_ready = (sig(n) for n in ("ss_ready", "gated", "gt_ps", "gt_sb",
                                                                             "out_ps", "rms_ready"))
        dve, pl, wn, mv_ready, rs_ready, resid = (sig(n) for n in ("dve3", "pool3", "wn", "mv_ready", "rs_ready",
                                                                  "resid"))
        tiles = [i // 2 + TPH * (i % 2) for i in range(TILES)]
        LAG = 2
        with nc.Block() as block:
            @block.tensor
            def _(pe):
                pe.wait_ge(m.wz_in.sem, 16)
                pe.wait_ge(zero.sem, 1)

                def finish(n):
                    i = tiles[n]
                    pe.wait_ge(gated.sem, n + 1)
                    if n >= 1:
                        pe.wait_ge(gt_sb.sem, n)
                    for c in range(4):
                        last = nc.tensor.transpose(m.ps[:, 6, P * c:P * (c + 1)], th[:, n % 2, P * c:P * (c + 1)],
                                                   m.ident[:, :])
                    gt_ps.by(last)
                    pe.wait_ge(gt_sb.sem, n + 1)
                    pe.wait_ge(wn.sem, 4)
                    if n >= 1:
                        pe.wait_ge(mv_ready.sem, n)
                    for c in range(4):
                        last = nc.tensor.matmul(m.ps[:, 7, 0:DM], gt[:, n % 2, P * c:P * (c + 1)], m.w_out[:, c, :],
                                                start=c == 0, stop=c == 3)
                    out_ps.by(last)

                for n, i in enumerate(tiles):
                    b = i // TPH
                    if n >= 1:
                        pe.wait_ge(carried.sem, G * n)
                    for g in range(G):
                        last = nc.tensor.matmul(m.ps[:, 0, HEADS * g:HEADS * (g + 1)], m.sel_last[:, g, :],
                                                m.since_row[:, i, :], start=True, stop=True)
                    decay_ps.by(last)
                    for g in range(G):
                        k = G * n + g
                        if k >= 2:
                            pe.wait_ge(carried.sem, k - 1)
                        new_ps.by(nc.tensor.matmul(m.ps[:, 1 + k % 2, :], m.b_row[Q * g:Q * (g + 1), i, :],
                                                   m.dt_end[Q * g:Q * (g + 1), i, :, :].rearrange("p h d -> p (h d)"),
                                                   start=True, stop=True))
                    if n >= 1:
                        pe.wait_ge(zs_ready.sem, n)
                    for k in range(KD):
                        last = nc.tensor.matmul(m.ps[:, 5, :], m.xT[:, k, P * i:P * (i + 1)], m.w_in[:, k, 0:INTER],
                                                start=k == 0, stop=k == KD - 1)
                    z_ps.by(last)
                    if n >= LAG:
                        finish(n - LAG)
                    if n >= 1:
                        pe.wait_ge(y1.sem, n)
                    for g in range(G):
                        c = G * (i % TPH) + g
                        pe.wait_ge(carried.sem, G * n + g)
                        last = nc.tensor.matmul(m.ps[Q * g:Q * (g + 1), 3, :],
                                                m.xc[:, 5, P * i + Q * g:P * i + Q * (g + 1)],
                                                st[:, b, c % RING, :, :].rearrange("p h d -> p (h d)"),
                                                start=True, stop=True)
                    inter_ps.by(last)
                for n in range(TILES - LAG, TILES):
                    finish(n)

            @block.scalar
            def _(sc):
                def copy_gated(n):
                    sc.wait_ge(gt_ps.sem, n + 1)
                    if n >= 2:
                        sc.wait_ge(out_ps.sem, n - 1)
                    gt_sb.by(nc.scalar.copy(gt[:, n % 2, :], m.ps[:, 6, :]))

                for n, i in enumerate(tiles):
                    if n >= LAG:
                        copy_gated(n - LAG)
                    sc.wait_ge(z_ps.sem, n + 1)
                    if n >= 2:
                        sc.wait_ge(gt_ps.sem, n - 1)
                    th_ready.by(nc.scalar.activation(th[:, n % 2, :], m.ps[:, 5, :], ACT.Tanh, scale=0.125))
                    sc.wait_ge(y2.sem, n + 1)
                    ss_ready.by(nc.scalar.activation(sq[:, :], y[:, n % 2, :, :].rearrange("p h d -> p (h d)"),
                                                     ACT.Square, accum_out=ss[:, n:n + 1]))
                for n in range(TILES - LAG, TILES):
                    copy_gated(n)

            @block.vector
            def _(v):
                for b in range(BATCH):
                    zero.by(nc.vector.memset(st[:, b, 0, :, :], 0.0))
                v.wait_ge(m.late_in.sem, 16 * 2)
                for c in range(4):
                    wn.by(nc.vector.tensor_scalar(m.w_out[:, c, :], m.w_out[:, c, :], m.norm_w[:, c:c + 1], None,
                                                  ALU.mult))

                def tail(n):
                    i = tiles[n]
                    v.wait_ge(out_ps.sem, n + 1)
                    v.wait_ge(rms_ready.sem, n + 1)
                    dve.then_wait(v, nc.vector.scalar_tensor_tensor(r[:, n % 2, :], m.ps[:, 7, 0:DM],
                                                                    rms[:, n:n + 1], m.x[:, i, :], ALU.mult, ALU.add))
                    dve.then_wait(v, nc.vector.bn_stats(bs[:, n % 2, :], r[:, n % 2, :]))
                    mv_ready.by(nc.vector.bn_aggr(mv[:, n % 2, :], bs[:, n % 2, :]))

                def normalise(n):
                    i = tiles[n]
                    v.wait_ge(rs_ready.sem, n + 1)
                    v.wait_ge(mv_ready.sem, n + 1)
                    resid.by(nc.vector.tensor_scalar(m.x[:, i, :], r[:, n % 2, :], mv[:, n % 2, 0:1],
                                                     rs[:, n % 2, 0:1], ALU.subtract, ALU.mult))

                for n, i in enumerate(tiles):
                    b = i // TPH
                    v.wait_ge(decay_ps.sem, n + 1)
                    for g in range(G):
                        c, k = G * (i % TPH) + g, G * n + g
                        if k:
                            v.wait_ge(carried.sem, k)
                        if n >= 4:
                            v.wait_ge(inter_ps.sem, n - 3)
                        dve.then_wait(v, nc.vector.tensor_tensor(
                            tmp[:, k % 2, :, :], st[:, b, c % RING, :, :],
                            spread(m.ps[:, 0, HEADS * g:HEADS * (g + 1)], 2, PDIM), ALU.mult))
                        v.wait_ge(new_ps.sem, k + 1)
                        carried.by(nc.vector.tensor_tensor(
                            st[:, b, (c + 1) % RING, :, :], tmp[:, k % 2, :, :],
                            m.ps[:, 1 + k % 2, :].rearrange("p (h d) -> p h d", d=PDIM), ALU.add))
                    if n >= LAG:
                        tail(n - LAG)
                    v.wait_ge(th_ready.sem, n + 1)
                    if n >= 2:
                        v.wait_ge(gated.sem, n - 1)
                    zs_ready.by(nc.vector.scalar_tensor_tensor(zs[:, n % 2, :], th[:, n % 2, :], 1.0, m.ps[:, 5, :],
                                                               ALU.add, ALU.mult))
                    v.wait_ge(inter_ps.sem, n + 1)
                    if n >= 2:
                        v.wait_ge(ss_ready.sem, n - 1)
                    y1.by(nc.vector.tensor_tensor(y[:, n % 2, :, :],
                                                  m.ps[:, 3, :].rearrange("p (h d) -> p h d", d=PDIM),
                                                  spread(m.since_row[:, i, :], 2, PDIM), ALU.mult))
                    if n >= LAG:
                        normalise(n - LAG)
                for n in range(TILES - LAG, TILES):
                    tail(n)
                    normalise(n)

            @block.gpsimd
            def _(pool):
                pool.wait_ge(m.const_in.sem, 16 * 4)

                def row_scales(n):
                    pool.wait_ge(ss_ready.sem, n + 1)
                    pl.then_wait(pool, nc.gpsimd.tensor_scalar(rms[:, n:n + 1], ss[:, n:n + 1], 1.0 / INTER, 1e-5,
                                                               ALU.mult, ALU.add))
                    pl.then_wait(pool, nc.gpsimd.tensor_tensor(rms[:, n:n + 1], rms[:, n:n + 1], m.half[:, :],
                                                               ALU.pow))
                    rms_ready.by(nc.gpsimd.tensor_scalar(rms[:, n:n + 1], rms[:, n:n + 1], 0.125, None, ALU.mult))

                def ln_scale(n):
                    pool.wait_ge(mv_ready.sem, n + 1)
                    pl.then_wait(pool, nc.gpsimd.tensor_scalar(rs[:, n % 2, :], mv[:, n % 2, 1:2], LN_EPS, None,
                                                               ALU.add))
                    rs_ready.by(nc.gpsimd.tensor_tensor(rs[:, n % 2, :], rs[:, n % 2, :], m.half[:, :], ALU.pow))

                for n, i in enumerate(tiles):
                    xd_ready.then_wait(pool, nc.gpsimd.tensor_tensor(
                        xd[:, n % 2, :, :], m.x_row[:, i, :].rearrange("p (h d) -> p h d", d=PDIM),
                        spread(m.d_row[:, :], 2, PDIM), ALU.mult))
                    xd4 = xd[:, n % 2, :, :].rearrange("p (c h) d -> p c (h d)", c=4)
                    pl.then_wait(pool, nc.gpsimd.tensor_tensor(xd4, xd4, m.xc[:, 0:4, P * i:P * (i + 1)], ALU.add))
                    if n >= LAG:
                        ln_scale(n - LAG)
                    pool.wait_ge(y1.sem, n + 1)
                    y2.then_wait(pool, nc.gpsimd.tensor_tensor(y[:, n % 2, :, :], y[:, n % 2, :, :], xd[:, n % 2, :, :],
                                                               ALU.add))
                    pool.wait_ge(zs_ready.sem, n + 1)
                    gated.by(nc.gpsimd.tensor_tensor(th[:, n % 2, :], y[:, n % 2, :, :].rearrange("p h d -> p (h d)"),
                                                     zs[:, n % 2, :], ALU.mult))
                    row_scales(n)
                for n in range(TILES - LAG, TILES):
                    ln_scale(n)


def ln_stats(nc, v, work, n, step, mv_ready):
    step.then_wait(v, nc.vector.bn_stats(work.bs[:, n % 2, :], work.r[:, n % 2, :]))
    mv_ready.by(nc.vector.bn_aggr(work.mv[:, n % 2, :], work.bs[:, n % 2, :]))


def ln_scale(nc, pool, m, work, n, step, mv_ready, rs_ready):
    pool.wait_ge(mv_ready.sem, n + 1)
    step.then_wait(pool, nc.gpsimd.tensor_scalar(work.rs[:, n % 2, :], work.mv[:, n % 2, 1:2], LN_EPS, None, ALU.add))
    rs_ready.by(nc.gpsimd.tensor_tensor(work.rs[:, n % 2, :], work.rs[:, n % 2, :], m.half[:, :], ALU.pow))


def ln_apply(nc, v, m, work, n, i, rs_ready, x_ready):
    v.wait_ge(rs_ready.sem, n + 1)
    x_ready.by(nc.vector.tensor_scalar(m.x[:, i, :], work.r[:, n % 2, :], work.mv[:, n % 2, 0:1],
                                       work.rs[:, n % 2, 0:1], ALU.subtract, ALU.mult))


def ln_work(sb):
    w = Memory()
    w.r, w.bs, w.mv, w.rs = sb("r", [P, 2, DM]), sb("bs", [P, 2, 6]), sb("mv", [P, 2, 2]), sb("rs", [P, 2, 1])
    return w


def load_lora(nc, m, a, sp):
    sp.dma_start(m.lw_a[:, :, :], a["L0_ffn_A"].rearrange("e r d -> (e r) d").rearrange("(j p) d -> p j d", p=P)
                 ).then_inc(m.lora_in.sem, 16)
    for h in range(KD):
        sp.dma_start(m.lw_b[:, h, :, :], a["L0_ffn_Bw"][:, P * h:P * (h + 1), :].rearrange("e p r -> p e r")
                     ).then_inc(m.lora_in.sem, 16)
    sp.dma_start(m.lw_g[:, :], a["L0_ffn_Wg"]).then_inc(m.lora_in.sem, 16)
    sp.dma_start(m.first8[:, :], a["c_first8"]).then_inc(m.lora_in.sem, 16)


def lora_experts(nc, m, a):
    with ExitStack() as ctx:
        sig = lambda name: Signal(ctx, nc, "lora_" + name)
        sb = lambda name, shape: ctx.enter_context(nc.sbuf_tensor("lora_" + name, shape, F32))
        aT = sb("aT", [P, KD, LE * LR])
        bT = sb("bT", [P, LE * LR // P, DM])
        gT = sb("gT", [P, KD, LE])
        lg = sb("lg", [P, TILES, LE])
        ex = sb("ex", [P, TILES, LE])
        hot = sb("hot", [P, TILES, LE])
        mx = sb("mx", [P, TILES])
        sm = sb("sm", [P, TILES])
        hm = sb("hm", [P, 2, LE, LR])
        hT = sb("hT", [P, 2, LE * LR])
        work = ln_work(sb)
        xt_ps, xt_sb, wt_ps, wt_sb = sig("xt_ps"), sig("xt_sb"), sig("wt_ps"), sig("wt_sb")
        lg_ps, ex_in, ex_out, h_ps, h_sb = (sig(n) for n in ("lg_ps", "ex_in", "ex_out", "h_ps", "h_sb"))
        hT_ps, hT_sb, y_ps, dve, pl = (sig(n) for n in ("hT_ps", "hT_sb", "y_ps", "dve4", "pool4"))
        mv_ready, rs_ready, x_ready = sig("mv_ready"), sig("rs_ready"), sig("x_ready")
        NJ = LE * LR // P
        with nc.Block() as block:
            @block.tensor
            def _(pe):
                pe.wait_ge(m.lora_in.sem, 16 * 5)
                for k in range(KD):
                    last = nc.tensor.transpose(m.ps[:, 4, LE * k:LE * (k + 1)], m.lw_g[:, P * k:P * (k + 1)],
                                               m.ident[0:LE, 0:LE])
                wt_ps.by(last)
                for k in range(KD):
                    for j in range(NJ):
                        last = nc.tensor.transpose(m.ps[:, 5 + k, P * j:P * (j + 1)], m.lw_a[:, j, P * k:P * (k + 1)],
                                                   m.ident[:, :])
                    wt_ps.by(last)
                for jj in range(2):
                    if jj == 1:
                        pe.wait_ge(wt_sb.sem, 1)
                    for j in (2 * jj, 2 * jj + 1):
                        for h in range(KD):
                            last = nc.tensor.transpose(
                                m.ps[:, 7 if jj == 0 else 4, DM * (j % 2) + P * h:DM * (j % 2) + P * (h + 1)],
                                m.lw_b[:, h, 2 * j:2 * j + 2, :].rearrange("p e r -> p (e r)"), m.ident[:, :])
                    wt_ps.by(last)
                transpose_rows(pe, nc, m, 0, lambda i: None, xt_ps)
                pe.wait_ge(xt_sb.sem, 4)
                pe.wait_ge(wt_sb.sem, 5)
                for i in range(TILES):
                    for k in range(KD):
                        last = nc.tensor.matmul(m.ps[:, 0, LE * i:LE * (i + 1)], m.xT[:, k, P * i:P * (i + 1)],
                                                gT[:, k, :], start=k == 0, stop=k == KD - 1)
                lg_ps.by(last)

                def down(i):
                    pe.wait_ge(h_sb.sem, i + 1)
                    for j in range(NJ):
                        last = nc.tensor.transpose(m.ps[:, 1 + i % 2, P * j:P * (j + 1)],
                                                   hm[:, i % 2, 2 * j:2 * j + 2, :].rearrange("p e r -> p (e r)"),
                                                   m.ident[:, :])
                    hT_ps.by(last)
                    pe.wait_ge(hT_sb.sem, i + 1)
                    if i >= 2:
                        pe.wait_ge(mv_ready.sem, i - 1)
                    for j in range(NJ):
                        last = nc.tensor.matmul(m.ps[:, 3 + 4 * (i % 2), 0:DM], hT[:, i % 2, P * j:P * (j + 1)],
                                                bT[:, j, :], start=j == 0, stop=j == NJ - 1)
                    y_ps.by(last)

                for i in range(TILES):
                    if i >= 2:
                        pe.wait_ge(h_sb.sem, i - 1)
                    for k in range(KD):
                        last = nc.tensor.matmul(m.ps[:, 5 + i % 2, :], m.xT[:, k, P * i:P * (i + 1)], aT[:, k, :],
                                                start=k == 0, stop=k == KD - 1)
                    h_ps.by(last)
                    if i >= 1:
                        down(i - 1)
                down(TILES - 1)

            @block.scalar
            def _(sc):
                for n, (bank, dst) in enumerate(((4, gT[:, :, :].rearrange("p k e -> p (k e)")),
                                                 (5, aT[:, 0, :]), (6, aT[:, 1, :]),
                                                 (7, bT[:, 0:2, :].rearrange("p j o -> p (j o)")),
                                                 (4, bT[:, 2:4, :].rearrange("p j o -> p (j o)")))):
                    sc.wait_ge(wt_ps.sem, n + 1)
                    wt_sb.by(nc.scalar.copy(dst, m.ps[:, bank, 0:dst.shape[1]]))
                sc.wait_ge(ex_in.sem, 1)
                ex_out.by(nc.scalar.activation(ex[:, :, :], lg[:, :, :], ACT.Exp))
                for i in range(TILES):
                    sc.wait_ge(hT_ps.sem, i + 1)
                    if i >= 2:
                        sc.wait_ge(y_ps.sem, i - 1)
                    hT_sb.by(nc.scalar.copy(hT[:, i % 2, :], m.ps[:, 1 + i % 2, :]))

            @block.vector
            def _(v):
                copy_transposed(v, nc.vector.tensor_copy, m, 0, xt_ps, xt_sb)
                v.wait_ge(lg_ps.sem, 1)
                lps = m.ps[:, 0, 0:TILES * LE].rearrange("p (i e) -> p i e", e=LE)
                dve.then_wait(v, nc.vector.tensor_reduce(mx[:, :], lps, AX.X, ALU.max))
                ex_in.then_wait(v, nc.vector.tensor_tensor(lg[:, :, :], lps, spread(mx[:, :], 2, LE), ALU.subtract))
                dve.then_wait(v, nc.vector.tensor_scalar(hot[:, :, :], lg[:, :, :], 0.0, None, ALU.is_equal))
                dve.then_wait(v, nc.vector.tensor_tensor(hot[:, :, :], hot[:, :, :], spread(m.first8[:, :], 1, TILES),
                                                         ALU.mult))
                dve.then_wait(v, nc.vector.tensor_reduce(mx[:, :], hot[:, :, :], AX.X, ALU.max))
                dve.then_wait(v, nc.vector.tensor_tensor(hot[:, :, :], hot[:, :, :], spread(mx[:, :], 2, LE),
                                                         ALU.is_equal))
                v.wait_ge(ex_out.sem, 1)
                dve.then_wait(v, nc.vector.tensor_reduce(sm[:, :], ex[:, :, :], AX.X, ALU.add))
                dve.then_wait(v, nc.vector.reciprocal(sm[:, :], sm[:, :]))
                dve.then_wait(v, nc.vector.scalar_tensor_tensor(hot[:, :, :], hot[:, :, :], LSCALE,
                                                                spread(sm[:, :], 2, LE), ALU.mult, ALU.mult))

                def tail(i):
                    v.wait_ge(y_ps.sem, i + 1)
                    if i >= 2:
                        v.wait_ge(x_ready.sem, i - 1)
                    dve.then_wait(v, nc.vector.tensor_tensor(work.r[:, i % 2, :], m.ps[:, 3 + 4 * (i % 2), 0:DM],
                                                             m.x[:, i, :], ALU.add))
                    ln_stats(nc, v, work, i, dve, mv_ready)

                for i in range(TILES):
                    v.wait_ge(h_ps.sem, i + 1)
                    if i >= 2:
                        v.wait_ge(hT_ps.sem, i - 1)
                    h_sb.by(nc.vector.tensor_tensor(hm[:, i % 2, :, :],
                                                    m.ps[:, 5 + i % 2, :].rearrange("p (e r) -> p e r", r=LR),
                                                    spread(hot[:, i, :], 2, LR), ALU.mult))
                    if i >= 1:
                        tail(i - 1)
                    if i >= 2:
                        ln_apply(nc, v, m, work, i - 2, i - 2, rs_ready, x_ready)
                tail(TILES - 1)
                for i in (TILES - 2, TILES - 1):
                    ln_apply(nc, v, m, work, i, i, rs_ready, x_ready)

            @block.gpsimd
            def _(pool):
                for i in range(TILES):
                    ln_scale(nc, pool, m, work, i, pl, mv_ready, rs_ready)


def load_qkv(nc, m, a, sp):
    sp.dma_start(m.w_down[:, :, :], k_tiles(a["L1_attn_w_down"])).then_inc(m.qkv_in.sem, 16)
    sp.dma_start(m.b_down[:, :], a["L1_attn_b_down"].unsqueeze(1), allow_slow_non_contiguous=True
                 ).then_inc(m.qkv_in.sem, 16)
    sp.dma_start(m.w_up[:, :], a["L1_attn_w_up"]).then_inc(m.qkv_in.sem, 16)
    sp.dma_start(m.b_up[:, :], a["L1_attn_b_up"].partition_broadcast(P)).then_inc(m.qkv_in.sem, 16)
    sp.dma_start(m.b_q[:, :], a["L1_attn_b_q"].partition_broadcast(P)).then_inc(m.qkv_in.sem, 16)
    for k, name in enumerate(("L1_attn_qn_w", "L1_attn_kn_w")):
        sp.dma_start(m.norm_qk[:, k, :], a[name].partition_broadcast(P)).then_inc(m.qkv_in.sem, 16)
    sp.dma_start(m.dist, a["c_dist"]).then_inc(m.qkv_in.sem, 16)
    sp.dma_start(m.cos_row[:, :, :], a["c_cos"]).then_inc(m.qkv_in.sem, 16)
    sp.dma_start(m.sin_row[:, :, :], a["c_sin"]).then_inc(m.qkv_in.sem, 16)
    sp.dma_start(m.w_q[:, :, :], k_tiles(a["L1_attn_w_q"])).then_inc(m.qkv_in.sem, 16)
QKV_LOADS = 11


class Selection:

    def __init__(self, sig, first, s, top, later, not_self):
        self.first, self.s, self.top, self.later, self.not_self = first, s, top, later, not_self
        self.masks, self.s_ps, self.s_sb, self.kept, self.s_turned, self.biased, self.dve = (sig(n) for n in (
            "masks", "sel_ps", "sel_sb", "kept", "sel_turned", "sel_biased", "sel_dve"))

    def buffer(self, i):
        j = i % TPH
        return self.s[:, i % 2, 0:P * (j + 1)], self.s[:, i % 2, P * j:P * (j + 1)]


def form_masks(nc, pool, q):
    q.masks.by(nc.gpsimd.memset(q.later, 0.0))
    q.masks.then_wait(pool, nc.gpsimd.memset(q.not_self, 1.0))
    q.masks.by(nc.gpsimd.affine_select(q.later, q.later, [[-1, P]], ALU.is_ge, LATER, base=0, channel_multiplier=1))
    q.masks.by(nc.gpsimd.affine_select(q.not_self, q.not_self, [[-1, P]], ALU.not_equal, 0.0, base=0,
                                       channel_multiplier=1))


def select_scores(nc, pe, m, q, i):
    b, j = i // TPH, i % TPH
    if i > q.first:
        pe.wait_ge(q.biased.sem, i - q.first)
    q.s_ps.by(nc.tensor.matmul(m.ps[:, 7, 0:P * (j + 1)], m.qT[0:SEL_DIM, 0, P * i:P * (i + 1)],
                               m.kT[0:SEL_DIM, 0, SEQ * b:SEQ * b + P * (j + 1)], start=True, stop=True))


def select_copy(nc, sc, m, q, i):
    n = i - q.first
    sc.wait_ge(q.s_ps.sem, n + 1)
    if n >= 2:
        sc.wait_ge(q.s_turned.sem, n - 1)
    s, own = q.buffer(i)
    q.s_sb.by(nc.scalar.copy(s, m.ps[:, 7, 0:s.shape[1]]))


def select_rounds(nc, v, q, i, lo, hi):
    s, own = q.buffer(i)
    if lo == 0:
        v.wait_ge(q.s_sb.sem, i - q.first + 1)
        v.wait_ge(q.masks.sem, 4)
        q.dve.then_wait(v, nc.vector.tensor_tensor(own, own, q.later, ALU.add))
    for _ in range(lo, hi):
        q.dve.then_wait(v, nc.vector.max(q.top, s))
        q.dve.then_wait(v, nc.vector.match_replace(s, q.top, s, TAKEN))
    if hi == SEL_TOPK // 8:
        q.dve.then_wait(v, nc.vector.tensor_scalar(s, s, TAKEN / 2, None, ALU.is_gt))
        q.kept.by(nc.vector.tensor_tensor(own, own, q.not_self, ALU.mult))


def select_turn(nc, pe, m, q, i):
    pe.wait_ge(q.kept.sem, i - q.first + 1)
    for k in range(i % TPH + 1):
        last = nc.tensor.transpose(m.ps[:, 7, P * k:P * (k + 1)], q.s[:, i % 2, P * k:P * (k + 1)], m.ident[:, :])
    q.s_turned.by(last)


def select_bias(nc, v, m, q, i):
    b, j = i // TPH, i % TPH
    v.wait_ge(q.s_turned.sem, i - q.first + 1)
    for k in range(j + 1):
        c = KEY_COL[k] + P * (j - k)
        last = nc.vector.scalar_tensor_tensor(m.bias[b][:, c:c + P], m.ps[:, 7, P * k:P * (k + 1)], FAR,
                                              m.dist[:, c:c + P], ALU.mult, ALU.add)
    q.biased.by(last)


def prepare_attention(nc, m, a):
    with ExitStack() as ctx:
        sig = lambda name: Signal(ctx, nc, "qkv_" + name)
        sb = lambda name, shape: ctx.enter_context(nc.sbuf_tensor("qkv_" + name, shape, F32))
        latT = sb("latT", [LATENT, NT])
        cw = sb("cw", [P, 2, TPH, HD])
        sw = sb("sw", [P, 2, TPH, HD])
        qb = sb("qb", [P, 2, QKH, HD])
        t1 = sb("t1", [P, QKH, HD])
        sq = m.cos_row
        ss = sb("ss5", [P, 2, QKH])
        half20 = sb("half20", [P, QKH])
        s = sb("s", [P, 2, SEQ])
        top = sb("top", [P, 8])
        xt_ps, xt_sb, lat_ps, lat_sb, tab = (sig(n) for n in ("xt_ps", "xt_sb", "lat_ps", "lat_sb", "tab"))
        q_ps, kv_ps, qb_ready, v_ready, squared = (sig(n) for n in ("q_ps", "kv_ps", "qb_ready", "v_ready",
                                                                   "squared"))
        rs_ready, cos_ready, sin_ready, rot, normed = (sig(n) for n in ("rs_ready", "cos_ready", "sin_ready", "rot",
                                                                       "normed"))
        turned, qk_sb, pl, ones = (sig(n) for n in ("turned", "qk_sb", "pool5", "ones"))
        NG = QKH // 4
        TURN, SELECT = 2, 5
        KEYS = NG - 1
        q = Selection(sig, 0, s, top[:, :], m.sin_row[:, 0, :], m.sin_row[:, 1, :])
        with nc.Block() as block:
            @block.sync
            def _(sp):
                load_qkv(nc, m, a, sp)

            @block.tensor
            def _(pe):
                pe.wait_ge(m.qkv_in.sem, 16 * QKV_LOADS)
                transpose_rows(pe, nc, m, 0, lambda i: None, xt_ps)
                pe.wait_ge(xt_sb.sem, 4)
                for h in range(HALVES):
                    for k in range(KD):
                        last = nc.tensor.matmul(m.ps[0:LATENT, 4 + h, :], m.w_down[:, k, :],
                                                m.xT[:, k, 512 * h:512 * (h + 1)], start=k == 0, stop=k == KD - 1)
                    lat_ps.by(last)
                pe.wait_ge(lat_sb.sem, 2)

                def project_kv(i):
                    if i >= 1:
                        pe.wait_ge(qb_ready.sem, 3 * i - 2)
                        pe.wait_ge(v_ready.sem, i)
                    for c in range(2):
                        last = nc.tensor.matmul(m.ps[:, 4 + c, :], latT[:, P * i:P * (i + 1)],
                                                m.w_up[:, 512 * c:512 * (c + 1)], start=True, stop=True)
                    kv_ps.by(last)

                def project_q(i, c):
                    if i >= 1 and c % 2 == 0:
                        pe.wait_ge(qb_ready.sem, 3 * i - 1 + c // 2)
                    for k in range(KD):
                        last = nc.tensor.matmul(m.ps[:, c, :], m.xT[:, k, P * i:P * (i + 1)],
                                                m.w_q[:, k, 512 * c:512 * (c + 1)], start=k == 0, stop=k == KD - 1)
                    if c % 2 == 1:
                        q_ps.by(last)

                def turn(i, g):
                    if g == KEYS:
                        pe.wait_ge(normed.sem, i + 1)
                    if turned.n >= 1:
                        pe.wait_ge(qk_sb.sem, turned.n)
                    for j in range(4):
                        last = nc.tensor.transpose(m.ps[:, 6, P * j:P * (j + 1)], qb[:, i % 2, 4 * g + j, :],
                                                   m.ident[:, :])
                    turned.by(last)

                for i in range(TILES + TURN):
                    now, turning = i < TILES, i >= TURN
                    n = i - SELECT
                    if now:
                        project_kv(i)
                    if 0 <= n < TPH:
                        pe.wait_ge(qk_sb.sem, NG * (n + 1))
                        select_scores(nc, pe, m, q, n)
                    if now:
                        project_q(i, 0)
                        project_q(i, 1)
                    if turning:
                        for g in (KEYS, 0, 1):
                            turn(i - TURN, g)
                    if now:
                        project_q(i, 2)
                    if turning:
                        turn(i - TURN, 2)
                    if 0 <= n < TPH - 1:
                        select_turn(nc, pe, m, q, n)
                    if now:
                        project_q(i, 3)
                    if turning:
                        turn(i - TURN, 3)
                select_turn(nc, pe, m, q, TPH - 1)

            @block.scalar
            def _(sc):
                for h in range(HALVES):
                    sc.wait_ge(lat_ps.sem, h + 1)
                    lat_sb.by(nc.scalar.activation(latT[:, 512 * h:512 * (h + 1)], m.ps[0:LATENT, 4 + h, :],
                                                   ACT.Identity, bias=m.b_down[:, 0:1]))

                def copy_turned(i, g):
                    sc.wait_ge(turned.sem, qk_sb.n + 1)
                    dst = (m.kT[:, :, P * i:P * (i + 1)] if g == KEYS else
                           m.qT[:, 4 * g:4 * g + 4, P * i:P * (i + 1)])
                    qk_sb.by(nc.scalar.copy(dst, m.ps[:, 6, :].rearrange("p (j t) -> p j t", t=P)))

                def square(i, heads, added):
                    sc.wait_ge(qb_ready.sem, 3 * i + added)
                    for h in heads:
                        if squared.n >= TPH:
                            sc.wait_ge(squared.sem, squared.n - TPH + 1)
                        squared.by(nc.scalar.activation(sq[:, squared.n % TPH, :], qb[:, i % 2, h, :], ACT.Square,
                                                        accum_out=ss[:, i % 2, h:h + 1]))

                for i in range(TILES + TURN):
                    turning = i >= TURN
                    if 0 <= i - SELECT < TPH:
                        select_copy(nc, sc, m, q, i - SELECT)
                    if turning:
                        for g in (KEYS, 0, 1):
                            copy_turned(i - TURN, g)
                    if turning:
                        copy_turned(i - TURN, 2)
                    if i < TILES:
                        if turning:
                            sc.wait_ge(normed.sem, i - TURN + 1)
                        square(i, range(16, 20), 1)
                        square(i, range(0, 8), 2)
                    if turning:
                        copy_turned(i - TURN, 3)
                    if i < TILES:
                        square(i, range(8, 16), 3)

            @block.vector
            def _(v):
                v.wait_ge(m.qkv_in.sem, 16 * QKV_LOADS)
                copy_transposed(v, nc.vector.tensor_copy, m, 0, xt_ps, xt_sb)
                for n in range(2):
                    nc.vector.tensor_tensor(cw[:, n, :, :], m.cos_row[:, :, :], spread(m.norm_qk[:, n, :], 1, TPH),
                                            ALU.mult)
                    for o in range(2):
                        last = nc.vector.tensor_tensor(sw[:, n, :, o::2], m.sin_row[:, :, o::2],
                                                       spread(m.norm_qk[:, n, 1 - o::2], 1, TPH), ALU.mult)
                    tab.by(last)
                v.wait_ge(tab.sem, 2)

                def turned_before(i, groups):
                    if i >= 2:
                        v.wait_ge(turned.sem, NG * (i - 2) + groups)

                def add_kv(i):
                    turned_before(i, 1)
                    v.wait_ge(kv_ps.sem, i + 1)
                    qb_ready.by(nc.vector.tensor_tensor(qb[:, i % 2, 16:20, :].rearrange("p h d -> p (h d)"),
                                                        m.ps[:, 4, :], m.b_up[:, 0:512], ALU.add))
                    v_ready.by(nc.vector.tensor_tensor(m.v[:, i, :, 0:HD],
                                                       m.ps[:, 5, :].rearrange("p (g d) -> p g d", d=HD),
                                                       m.b_up[:, 512:1024].rearrange("p (g d) -> p g d", d=HD),
                                                       ALU.add))

                def add_q(i, half):
                    turned_before(i, 3 + 2 * half)
                    v.wait_ge(q_ps.sem, 2 * i + half + 1)
                    qb_ready.by(nc.vector.tensor_tensor(
                        qb[:, i % 2, 8 * half:8 * half + 8, :].rearrange("p h d -> p (h d)"),
                        m.ps[:, 2 * half:2 * half + 2, :].rearrange("p b n -> p (b n)"),
                        m.b_q[:, 1024 * half:1024 * (half + 1)], ALU.add))

                def sin_part(i):
                    b, j = qb[:, i % 2, :, :], i % TPH
                    v.wait_ge(qb_ready.sem, 3 * i + 3)
                    if i >= 1:
                        v.wait_ge(rot.sem, i)
                    for n, h0, h1 in ((0, 0, 16), (1, 16, 20)):
                        for o in range(2):
                            last = nc.vector.tensor_tensor(t1[:, h0:h1, o::2], b[:, h0:h1, 1 - o::2],
                                                           spread(sw[:, n, j, o::2], 1, h1 - h0), ALU.mult)
                    sin_ready.by(last)

                def normalise(i):
                    v.wait_ge(rot.sem, i + 1)
                    v.wait_ge(rs_ready.sem, i + 1)
                    normed.by(nc.vector.tensor_tensor(qb[:, i % 2, :, :], qb[:, i % 2, :, :],
                                                      spread(ss[:, i % 2, :], 2, HD), ALU.mult))

                for i in range(TILES):
                    n = i - SELECT
                    add_kv(i)
                    add_q(i, 0)
                    add_q(i, 1)
                    if 0 <= n < TPH:
                        select_bias(nc, v, m, q, n)
                    sin_part(i)
                    if i >= 1:
                        normalise(i - 1)
                    if 0 <= n + 1 < TPH:
                        select_rounds(nc, v, q, n + 1, 0, SEL_TOPK // 8)
                normalise(TILES - 1)
                select_bias(nc, v, m, q, TPH - 1)

            @block.gpsimd
            def _(pool):
                ones.by(nc.gpsimd.memset(m.v[:, :, :, HD:HD + 1], 1.0))
                ones.then_wait(pool, nc.gpsimd.memset(half20[:, :], -0.5))
                pool.wait_ge(tab.sem, 2)
                form_masks(nc, pool, q)
                for i in range(TILES):
                    j = i % TPH
                    b = qb[:, i % 2, :, :]
                    pool.wait_ge(sin_ready.sem, i + 1)
                    pool.wait_ge(squared.sem, QKH * (i + 1))
                    for of_k, h0, h1 in ((0, 0, 16), (1, 16, 20)):
                        last = nc.gpsimd.tensor_tensor(b[:, h0:h1, :], b[:, h0:h1, :],
                                                       spread(cw[:, of_k, j, :], 1, h1 - h0), ALU.mult)
                    cos_ready.then_wait(pool, last)
                    rot.by(nc.gpsimd.tensor_tensor(b, b, t1[:, :, :], ALU.add))
                    pl.then_wait(pool, nc.gpsimd.tensor_scalar(ss[:, i % 2, :], ss[:, i % 2, :], 1.0 / HD, 1e-6,
                                                               ALU.mult, ALU.add))
                    rs_ready.by(nc.gpsimd.tensor_tensor(ss[:, i % 2, :], ss[:, i % 2, :], half20[:, :], ALU.pow))


def load_attention(nc, m, a, sp):
    sp.dma_start(m.gate_b[:, :], a["L1_attn_gate_b"].rearrange("h e -> e h"), allow_slow_non_contiguous=True
                 ).then_inc(m.attn_in.sem, 16)
    for h in range(2):
        sp.dma_start(m.gate_w[:, 8 * h:8 * h + 8, :],
                     a["L1_attn_gate_w"][8 * h:8 * h + 8, :, :].rearrange("h d e -> d h e")).then_inc(m.attn_in.sem, 16)
    sp.dma_start(m.w_o[:, :, :], a["L1_attn_w_o"].rearrange("(h d) n -> d h n", d=P)).then_inc(m.wo_in.sem, 16)
    sp.dma_start(m.b_o[:, :], a["L1_attn_b_o"].partition_broadcast(P)).then_inc(m.wo_in.sem, 16)
ATTN_LOADS = 3


def attend(nc, m, a):
    with ExitStack() as ctx:
        sig = lambda name: Signal(ctx, nc, "att_" + name)
        sb = lambda name, shape: ctx.enter_context(nc.sbuf_tensor("att_" + name, shape, F32))
        rd = sb("rd", [P, 2, TPH])
        c = 0
        parts = []
        for n in (NCOL, NCOL, SEQ, SEQ, SEQ):
            parts.append(m.rows[:, c:c + 2 * n].rearrange("p (u n) -> p u n", u=2))
            c += 2 * n
        t, p, yn, yT, tg = parts
        yn = yn.rearrange("p u (j d) -> p u j d", d=HD)
        gb = sb("gb", [P, AH])
        top = sb("top", [P, 8])
        late = Space(m.weights[:, 2 * NE * DM - 2 * SEQ - 2 * P:])
        q = Selection(sig, TPH, late.take(P, 2, SEQ), top[:, :], late.take(P, P), late.take(P, P))
        s_ps, capped, biased, p_ready, y_ps, y_sb = (sig(n) for n in ("s_ps", "capped", "biased", "p_ready", "y_ps",
                                                                     "y_sb"))
        yT_ps, yT_sb, g_ps, g_sb, z_ready, gb_ready, dve = (sig(n) for n in (
            "yT_ps", "yT_sb", "g_ps", "g_sb", "z_ready", "gb_ready", "dve7"))
        todo = [(b, h) for b in range(BATCH) for h in range(AH)]
        N = len(todo)
        flat = m.ps[:, 0:3, :].rearrange("p b n -> p (b n)")
        ROUNDS = [0, 3, 6, 8]
        TURN = len(ROUNDS) - 1

        def tile_step(n):
            return (TPH + n // (TURN + 1), n % (TURN + 1)) if n < TPH * (TURN + 1) else (None, -1)

        with nc.Block() as block:
            @block.sync
            def _(sp):
                load_attention(nc, m, a, sp)
                e = (2 * NE * DM - late.ap.shape[1]) // (2 * KD * EI)
                load_gate_up(nc, m, a, sp, slice(FIRST_EXPERTS.stop, e))
                sp.wait_ge(q.biased.sem, TPH)
                load_gate_up(nc, m, a, sp, slice(e, NE))

            @block.gpsimd
            def _(pool):
                form_masks(nc, pool, q)

            @block.tensor
            def _(pe):
                def scores(n):
                    b, h = todo[n]
                    if n >= 1:
                        pe.wait_ge(capped.sem, n)
                    for i in range(TPH):
                        w = SEQ - P * i
                        last = nc.tensor.matmul(flat[:, KEY_COL[i]:KEY_COL[i] + w],
                                                m.kT[:, h // KVG, SEQ * b + P * i:SEQ * b + P * (i + 1)],
                                                m.qT[:, h, SEQ * b + P * i:SEQ * (b + 1)], start=True, stop=True)
                    s_ps.by(last)

                def values(n):
                    b, h = todo[n]
                    pe.wait_ge(p_ready.sem, n + 1)
                    if n >= 1:
                        pe.wait_ge(y_sb.sem, n)
                    for j in range(TPH):
                        out = m.ps[:, 3, VW * j:VW * (j + 1)] if j < 3 else m.ps[:, 4, 0:VW]
                        for i in range(j + 1):
                            c = KEY_COL[i] + P * (j - i)
                            last = nc.tensor.matmul(out, p[:, n % 2, c:c + P], m.v[:, TPH * b + i, h // KVG, :],
                                                    start=i == 0, stop=i == j)
                    y_ps.by(last)

                def turn(n):
                    pe.wait_ge(y_sb.sem, n + 1)
                    if n >= 1:
                        pe.wait_ge(yT_sb.sem, n)
                    for j in range(TPH):
                        last = nc.tensor.transpose(m.ps[:, 5, P * j:P * (j + 1)], yn[:, n % 2, j, :], m.ident[:, :])
                    yT_ps.by(last)

                def gate(n):
                    if n == 0:
                        pe.wait_ge(m.attn_in.sem, 16 * ATTN_LOADS)
                    pe.wait_ge(yT_sb.sem, n + 1)
                    if n >= 1:
                        pe.wait_ge(g_sb.sem, n)
                    g_ps.by(nc.tensor.matmul(m.ps[:, 6, :], m.gate_w[:, todo[n][1], :], yT[:, n % 2, :], start=True,
                                             stop=True))

                scores(0)
                for n in range(N):
                    i, step = tile_step(n)
                    if step == 0:
                        select_scores(nc, pe, m, q, i)
                    if step == TURN:
                        select_turn(nc, pe, m, q, i)
                    if n + 1 < N:
                        scores(n + 1)
                    if n >= 1:
                        turn(n - 1)
                    values(n)
                    if n >= 1:
                        gate(n - 1)
                turn(N - 1)
                gate(N - 1)

            @block.scalar
            def _(sc):
                def cap(n):
                    sc.wait_ge(s_ps.sem, n + 1)
                    if n >= 2:
                        sc.wait_ge(p_ready.sem, n - 1)
                    capped.by(nc.scalar.activation(t[:, n % 2, :], flat[:, 0:NCOL], ACT.Tanh,
                                                   scale=1.0 / (HD ** 0.5 * SOFTCAP)))

                def gating(n):
                    if n == 0:
                        sc.wait_ge(gb_ready.sem, 1)
                    sc.wait_ge(yT_ps.sem, n + 1)
                    if n >= 2:
                        sc.wait_ge(z_ready.sem, n - 1)
                    yT_sb.by(nc.scalar.copy(yT[:, n % 2, :], m.ps[:, 5, :]))
                    sc.wait_ge(g_ps.sem, n + 1)
                    g_sb.by(nc.scalar.activation(tg[:, n % 2, :], m.ps[:, 6, :], ACT.Tanh,
                                                 bias=gb[:, todo[n][1]:todo[n][1] + 1]))

                cap(0)
                for n in range(N):
                    i, step = tile_step(n)
                    if step == 0:
                        select_copy(nc, sc, m, q, i)
                    sc.wait_ge(biased.sem, n + 1)
                    if n >= 2:
                        sc.wait_ge(y_ps.sem, n - 1)
                    p_ready.by(nc.scalar.activation(p[:, n % 2, :], t[:, n % 2, :], ACT.Exp, scale=SOFTCAP))
                    if n + 1 < N:
                        cap(n + 1)
                    if n >= 1:
                        gating(n - 1)
                gating(N - 1)

            def normalise(v, n):
                v.wait_ge(y_ps.sem, n + 1)
                if n >= 2:
                    v.wait_ge(yT_ps.sem, n - 1)
                y3 = m.ps[:, 3, 0:3 * VW].rearrange("p (j d) -> p j d", d=VW)
                nc.vector.reciprocal(rd[:, n % 2, 0:3], y3[:, :, HD])
                dve.then_wait(v, nc.vector.reciprocal(rd[:, n % 2, 3:4], m.ps[:, 4, HD:HD + 1]))
                nc.vector.scalar_tensor_tensor(yn[:, n % 2, 0:3, :], y3[:, :, 0:HD], 0.5,
                                               spread(rd[:, n % 2, 0:3], 2, HD), ALU.mult, ALU.mult)
                y_sb.by(nc.vector.tensor_scalar(yn[:, n % 2, 3, :], m.ps[:, 4, 0:HD], rd[:, n % 2, 3:4], 0.5,
                                                ALU.mult, ALU.mult))

            @block.vector
            def _(v):

                def finish(n):
                    b, h = todo[n]
                    v.wait_ge(g_sb.sem, n + 1)
                    z_ready.by(nc.vector.scalar_tensor_tensor(m.qT[:, h, SEQ * b:SEQ * (b + 1)], tg[:, n % 2, :], 1.0,
                                                              yT[:, n % 2, :], ALU.add, ALU.mult))

                for n in range(N):
                    b, h = todo[n]
                    v.wait_ge(capped.sem, n + 1)
                    if n == AH:
                        v.wait_ge(q.biased.sem, TPH)
                    if n == 1:
                        v.wait_ge(m.attn_in.sem, 16 * ATTN_LOADS)
                        gb_ready.by(nc.vector.tensor_scalar(gb[:, :], m.gate_b[:, :], 0.5, None, ALU.mult))
                    biased.by(nc.vector.scalar_tensor_tensor(t[:, n % 2, :], m.bias[b], SLOPE[h] / SOFTCAP,
                                                             t[:, n % 2, :], ALU.mult, ALU.add))
                    if n >= 2:
                        finish(n - 2)
                    if n >= 1:
                        normalise(v, n - 1)
                    i, step = tile_step(n)
                    if 0 <= step < TURN:
                        select_rounds(nc, v, q, i, ROUNDS[step], ROUNDS[step + 1])
                    if step == TURN:
                        select_bias(nc, v, m, q, i)
                normalise(v, N - 1)
                finish(N - 2)
                finish(N - 1)


def attention_output(nc, m, a):
    with ExitStack() as ctx:
        sig = lambda name: Signal(ctx, nc, "out_" + name)
        sb = lambda name, shape: ctx.enter_context(nc.sbuf_tensor("out_" + name, shape, F32))
        work = ln_work(sb)
        o_ps, mv_ready, rs_ready, x_ready, xb, dve, pl = (sig(n) for n in ("o_ps", "mv_ready", "rs_ready", "x_ready",
                                                                          "xb", "dve8", "pool8"))
        with nc.Block() as block:
            @block.sync
            def _(sp):
                load_expert_weights(nc, m, a, sp)

            @block.tensor
            def _(pe):
                pe.wait_ge(m.wo_in.sem, 32)
                for i in range(TILES):
                    if i >= 2:
                        pe.wait_ge(mv_ready.sem, i - 1)
                    for h in range(AH):
                        last = nc.tensor.matmul(m.ps[:, i % 2, 0:DM], m.qT[:, h, P * i:P * (i + 1)], m.w_o[:, h, :],
                                                start=h == 0, stop=h == AH - 1)
                    o_ps.by(last)

            @block.vector
            def _(v):
                v.wait_ge(m.wo_in.sem, 32)
                for i in range(TILES):
                    xb.by(nc.vector.tensor_tensor(m.x[:, i, :], m.x[:, i, :], m.b_o[:, :], ALU.add))
                    v.wait_ge(o_ps.sem, i + 1)
                    v.wait_ge(xb.sem, i + 1)
                    if i >= 2:
                        v.wait_ge(x_ready.sem, i - 1)
                    dve.then_wait(v, nc.vector.tensor_tensor(work.r[:, i % 2, :], m.ps[:, i % 2, 0:DM], m.x[:, i, :],
                                                             ALU.add))
                    ln_stats(nc, v, work, i, dve, mv_ready)
                    ln_apply(nc, v, m, work, i, i, rs_ready, x_ready)

            @block.gpsimd
            def _(pool):
                for i in range(TILES):
                    ln_scale(nc, pool, m, work, i, pl, mv_ready, rs_ready)


FIRST_EXPERTS = slice(0, NE // 2)


def load_gate_up(nc, m, a, sp, e):
    for u, name in enumerate(("L1_ffn_W_gate", "L1_ffn_W_up")):
        for k in range(KD):
            sp.dma_start(m.w_gu[:, e, k, u, :], a[name][e, P * k:P * (k + 1), :].rearrange("e p i -> p e i")
                         ).then_inc(m.gu_in.sem, 16)
GATE_UP_LOADS = 3 * 2 * KD


def load_expert_weights(nc, m, a, sp):
    w = m.early
    sp.dma_start(w.router, a["L1_ffn_router_w"]).then_inc(m.early_in.sem, 16)
    sp.dma_start(w.e_bias, a["L1_ffn_e_bias"].partition_broadcast(P)).then_inc(m.early_in.sem, 16)
    sp.dma_start(w.before, a["c_before"]).then_inc(m.early_in.sem, 16)
    sp.dma_start(w.lower, a["c_lower"]).then_inc(m.early_in.sem, 16)
    sp.dma_start(w.token, a["c_iota"]).then_inc(m.early_in.sem, 16)
    sp.dma_start(w.own, a["c_own"]).then_inc(m.early_in.sem, 16)
    sp.dma_start(w.info[:, :, 0:1], a["c_token"], allow_slow_non_contiguous=True).then_inc(m.early_in.sem, 16)
    load_gate_up(nc, m, a, sp, FIRST_EXPERTS)
    for h in range(2):
        e = slice(16 * h, 16 * h + 16)
        sp.dma_start(m.w_down_e[:, e, :], a["L1_ffn_W_down"][e, :, :].rearrange("e i d -> i e d")
                     ).then_inc(m.down_in.sem, 16)
EARLY_LOADS = 7


def route_and_run_experts(nc, m, a, out):
    with ExitStack() as ctx:
        sig = lambda name: Signal(ctx, nc, "moe_" + name)
        spaces = m.free
        sb = lambda name, shape: next(s for s in spaces if s.fits(shape)).take(*shape)
        rT = sb("rT", [P, KD, NE])
        every = sb("every", [P, P])
        restart = sb("restart", [P, TILES, NE])
        score = sb("score", [P, TILES, NE])
        mk = sb("mk", [P, TILES, NE])
        pre = sb("pre", [P, TILES, NE])
        cum = sb("cum", [P, TILES, NE])
        top = sb("top", [P, TILES, 8])
        gs = sb("gs", [P, 4, TILES * NG])
        cmp_ = sb("cmp", [P, 2, TILES, NG, NG])
        gm = sb("gm", [P, TILES * NG])
        cnt = sb("cnt", [P, TILES])
        pos = sb("pos", [P, TILES, NE])
        slot_token = sb("slot_token", [P, ST])
        slot_weight = sb("slot_weight", [P, ST])
        hot = sb("hot", [P, 2, NE, CAP])
        xp = sb("xp", [P, KD, SLOTS + PAIR_ROWS - CAP])
        w_row = xp.rearrange("p k s -> p (k s)")[:, 0:3 * KD * DM].rearrange("p (n k d) -> p n k d", n=3, k=KD)
        sg = sb("sg", [P, 2, 2 * EI])
        hT = sb("hT", [P, 2, 2 * P])
        yp = sb("yp", [P, 2, 2, DM])
        y = sb("y", [P, ST, DM])
        sw = sb("sw", [P, ST, NE])
        wT = sb("wT", [P, 3, KD, DM])
        hs = sb("hs", [P, KD, NT])
        lin = sb("lin", [P, 2, 2, 512])
        sh = sb("sh", [P, 2, 512])
        work = ln_work(sb)
        router, eb, before, lower, token, own, info = (m.early.router, m.early.e_bias, m.early.before, m.early.lower,
                                                       m.early.token, m.early.own, m.early.info)
        back = m.weights[:, 0:ST * NT].rearrange("p (s t) -> p s t", t=NT)
        BACK_EXPERTS = -(-ST * NT // (2 * KD * EI))

        xt_ps, xt_sb, rw_ps, rw_sb = (sig(n) for n in ("xt_ps", "xt_sb", "rw_ps", "rw_sb"))
        l_ps, sc_ready, ready, dve, chosen, earlier, before_ps, info_ready = (sig(n) for n in (
            "l_ps", "sc_ready", "ready", "dve9", "chosen", "earlier", "before_ps", "info_ready"))
        hot_ready, used, xp_sb, facts_read = (sig(n) for n in ("hot_ready", "used", "xp_sb", "facts_read"))
        gu_ps, sg_ready, h_ready, hT_ps, hT_sb, y_ps, y_sb, y_out, y_early, y_late = (sig(n) for n in (
            "gu_ps", "sg_ready", "h_ready", "hT_ps", "hT_sb", "y_ps", "y_sb", "y_out", "y_early", "y_late"))
        w_in, w_ps, w_sb, sh_ps, sh_lin, sh_ready, pl = (sig(n) for n in (
            "w_in", "w_ps", "w_sb", "sh_ps", "sh_lin", "sh_ready", "pool9"))
        back_ready, o_ps, mv_ready, rs_ready, x_ready = (sig(n) for n in (
            "back_ready", "o_ps", "mv_ready", "rs_ready", "x_ready"))
        PAIRS = NE // 2
        NGR = PAIRS // 2
        ready_tiles = [2 * 2 * CAP * (g + 1) // P for g in range(NGR)]
        EARLY = NGR - 3
        SPLIT = ready_tiles[EARLY - 1]

        with nc.Block() as block:
            @block.sync
            def _(sp):
                for n, name in enumerate(("gate", "up", "down")):
                    sp.dma_start(w_row[:, n, :, :], k_tiles(a["L1_ffn_shared_" + name])).then_inc(w_in.sem, 16)
                by_pair = m.y_dram.rearrange("(n u c) d -> u c n d", u=2, c=CAP)
                by_tile = rows(m.y_dram)
                for g in range(NGR):
                    sp.wait_ge(y_sb.sem, g + 1)
                    for u in range(2):
                        sp.dma_start(by_pair[u, :, 2 * g:2 * g + 2, :], yp[PAIR_ROWS * u:PAIR_ROWS * u + CAP, g % 2, :, :]
                                     ).then_inc(y_out.sem, 16)
                    sp.wait_ge(y_out.sem, 32 * (g + 1))
                    t = slice(ready_tiles[g - 1] if g else 0, ready_tiles[g])
                    arrived = y_early if g < EARLY else y_late
                    sp.dma_start(y[:, t, :], by_tile[:, t, :]).then_inc(arrived.sem, 16)
                for i in range(TILES):
                    sp.wait_ge(x_ready.sem, i + 1)
                    sp.dma_start(rows(out)[:, i, :], m.x[:, i, :]).then_inc(m.stored.sem, 16)
                sp.wait_ge(m.stored.sem, 16 * TILES)

            @block.tensor
            def _(pe):
                pe.wait_ge(m.early_in.sem, 16 * EARLY_LOADS)
                transpose_rows(pe, nc, m, 0, lambda i: None, xt_ps)
                for k in range(KD):
                    last = nc.tensor.transpose(m.ps[:, 4, NE * k:NE * (k + 1)], router[:, P * k:P * (k + 1)],
                                               m.ident[0:NE, 0:NE])
                rw_ps.by(last)
                pe.wait_ge(xt_sb.sem, 4)
                pe.wait_ge(rw_sb.sem, 1)
                for i in range(TILES):
                    for k in range(KD):
                        last = nc.tensor.matmul(m.ps[:, 5, NE * i:NE * (i + 1)], m.xT[:, k, P * i:P * (i + 1)],
                                                rT[:, k, :], start=k == 0, stop=k == KD - 1)
                l_ps.by(last)
                pe.wait_ge(w_in.sem, 48)
                for n in range(3):
                    if n >= 2:
                        pe.wait_ge(w_sb.sem, n - 1)
                    for j in range(KD):
                        for k in range(KD):
                            c = DM * k + P * j
                            last = nc.tensor.transpose(m.ps[:, 6 + n % 2, c:c + P], w_row[:, n, j, P * k:P * (k + 1)],
                                                       m.ident[:, :])
                    w_ps.by(last)
                pe.wait_ge(w_sb.sem, 2)
                for n in range(KD * HALVES):
                    j, h = n // HALVES, n % HALVES
                    if n >= 2:
                        pe.wait_ge(sh_lin.sem, n - 1)
                    for u in range(2):
                        for k in range(KD):
                            last = nc.tensor.matmul(m.ps[:, 2 * (n % 2) + u, :], wT[:, u, k, P * j:P * (j + 1)],
                                                    m.xT[:, k, 512 * h:512 * (h + 1)], start=k == 0, stop=k == KD - 1)
                    sh_ps.by(last)
                pe.wait_ge(chosen.sem, 1)
                flat = lambda t: t.rearrange("p i e -> p (i e)")
                nc.tensor.matmul(m.ps[:, 4, 0:TILES * NE], before, flat(pre), start=True, stop=False)
                pe.wait_ge(earlier.sem, 1)
                pe.wait_ge(ready.sem, 3)
                before_ps.by(nc.tensor.matmul(m.ps[:, 4, 0:TILES * NE], every, flat(cum), start=False, stop=True))
                pe.wait_ge(info_ready.sem, 1)
                pe.wait_ge(sh_lin.sem, KD * HALVES)
                pe.wait_ge(w_sb.sem, 3)
                for i in range(TILES):
                    pe.wait_ge(hot_ready.sem, i + 1)
                    flat_hot = hot[:, i % 2, :, :].rearrange("p e c -> p (e c)")
                    for k in range(KD):
                        for c in range(3):
                            w = min(512, SLOTS - 512 * c)
                            nc.tensor.matmul(m.ps[:, 3 * k + c, 0:w], m.x[:, i, P * k:P * (k + 1)],
                                             flat_hot[:, 512 * c:512 * c + w], start=i == 0, stop=i == TILES - 1)
                    for s in range(ST):
                        last = nc.tensor.matmul(m.ps[:, 6, (1 + NE) * s:(1 + NE) * (s + 1)],
                                                flat_hot[:, P * s:P * (s + 1)], info[:, i, :],
                                                start=i == 0 and s == 0, stop=i == TILES - 1, skip_group_check=True)
                    used.by(last)
                pe.wait_ge(xp_sb.sem, KD + 1)
                pe.wait_ge(m.gu_in.sem, 16 * GATE_UP_LOADS)

                def gate_up(g):
                    if g >= 4:
                        pe.wait_ge(h_ready.sem, g - 3)
                    for j in range(2):
                        for u in range(2):
                            e = 2 * (2 * g + j) + u
                            for k in range(KD):
                                last = nc.tensor.matmul(
                                    m.ps[PAIR_ROWS * u:PAIR_ROWS * (u + 1), g % 4, 2 * EI * j:2 * EI * (j + 1)],
                                    xp[:, k, CAP * e:CAP * e + PAIR_ROWS],
                                    m.w_gu[:, e, k, :, :].rearrange("p u i -> p (u i)"), start=k == 0,
                                    stop=k == KD - 1)
                    gu_ps.by(last)

                def turn(g):
                    pe.wait_ge(h_ready.sem, g + 1)
                    if g == 0:
                        pe.wait_ge(facts_read.sem, 2)
                    if g >= 1:
                        pe.wait_ge(hT_sb.sem, g)
                    for j in range(2):
                        last = nc.tensor.transpose(m.ps[:, 4, P * j:P * (j + 1)], sg[:, g % 2, EI * j:EI * (j + 1)],
                                                   m.ident[:, :])
                    hT_ps.by(last)

                def down(g):
                    pe.wait_ge(hT_sb.sem, g + 1)
                    if g == 0:
                        pe.wait_ge(m.down_in.sem, 32)
                    if g >= 2:
                        pe.wait_ge(y_sb.sem, g - 1)
                    for j in range(2):
                        for u in range(2):
                            c = P * j + PAIR_ROWS * u
                            last = nc.tensor.matmul(
                                m.ps[PAIR_ROWS * u:PAIR_ROWS * (u + 1), 5 + g % 2, DM * j:DM * (j + 1)],
                                hT[:, g % 2, c:c + PAIR_ROWS], m.w_down_e[:, 2 * (2 * g + j) + u, :], start=True,
                                stop=True)
                    y_ps.by(last)

                def sum_slots(i, tiles, last_ones):
                    dst = m.ps[:, i // 2, DM * (i % 2):DM * (i % 2 + 1)]
                    for s in tiles:
                        last = nc.tensor.matmul(dst, back[:, s, P * i:P * (i + 1)], y[:, s, :], start=False,
                                                stop=last_ones and s == ST - 1, skip_group_check=True)
                    return last

                def sum_shared(i):
                    if i % 2 == 0:
                        pe.wait_ge(h_ready.sem, NGR - 3 + i // 2)
                    for k in range(KD):
                        nc.tensor.matmul(m.ps[:, i // 2, DM * (i % 2):DM * (i % 2 + 1)], hs[:, k, P * i:P * (i + 1)],
                                         wT[:, 2, k, :], start=i % 2 == 0 and k == 0, stop=False,
                                         skip_group_check=True)

                for g in range(NGR):
                    gate_up(g)
                    if g >= 1:
                        turn(g - 1)
                    if g >= 2:
                        down(g - 2)
                pe.wait_ge(sh_ready.sem, KD * HALVES)
                pe.wait_ge(back_ready.sem, SPLIT)
                pe.wait_ge(y_early.sem, 16 * EARLY)
                for i in range(TILES):
                    sum_shared(i)
                    sum_slots(i, range(SPLIT), False)
                    if i == 0:
                        turn(NGR - 1)
                        down(NGR - 2)
                    if i == 1:
                        down(NGR - 1)
                pe.wait_ge(back_ready.sem, ST)
                pe.wait_ge(y_late.sem, 16 * (NGR - EARLY))
                for i in range(TILES):
                    o_ps.by(sum_slots(i, range(SPLIT, ST), True))

            @block.scalar
            def _(sc):
                sc.wait_ge(rw_ps.sem, 1)
                rw_sb.by(nc.scalar.copy(rT.rearrange("p k e -> p (k e)"), m.ps[:, 4, 0:KD * NE]))
                sc.wait_ge(l_ps.sem, 1)
                sc_ready.by(nc.scalar.activation(score.rearrange("p i e -> p (i e)"), m.ps[:, 5, 0:TILES * NE],
                                                 ACT.Sigmoid))
                for n in range(3):
                    sc.wait_ge(w_ps.sem, n + 1)
                    w_sb.by(nc.scalar.copy(wT[:, n, :, :].rearrange("p k d -> p (k d)"), m.ps[:, 6 + n % 2, :]))
                for n in range(KD * HALVES):
                    sc.wait_ge(sh_ps.sem, n + 1)
                    if n >= 2:
                        sc.wait_ge(sh_ready.sem, n - 1)
                    nc.scalar.activation(sh[:, n % 2, :], m.ps[:, 2 * (n % 2), :], ACT.Sigmoid)
                    sh_lin.by(nc.scalar.copy(lin[:, n % 2, :, :].rearrange("p u t -> p (u t)"),
                                             m.ps[:, 2 * (n % 2):2 * (n % 2) + 2, :].rearrange("p u t -> p (u t)")))
                sc.wait_ge(used.sem, TILES)
                flat = m.ps[:, 0:6, :].rearrange("p (k b) n -> p k (b n)", k=KD)
                xp_sb.by(nc.scalar.copy(xp[:, 0, 0:SLOTS], flat[:, 0, 0:SLOTS]))

                def copy_hT(g):
                    sc.wait_ge(hT_ps.sem, g + 1)
                    if g >= 2:
                        sc.wait_ge(y_ps.sem, g - 1)
                    hT_sb.by(nc.scalar.copy(hT[:, g % 2, :], m.ps[:, 4, 0:2 * P]))

                def copy_y(g):
                    sc.wait_ge(y_ps.sem, g + 1)
                    if g >= 2:
                        sc.wait_ge(y_out.sem, 32 * (g - 1))
                    y_sb.by(nc.scalar.copy(yp[:, g % 2, :, :].rearrange("p n d -> p (n d)"), m.ps[:, 5 + g % 2, :]))

                for g in range(NGR):
                    sc.wait_ge(gu_ps.sem, g + 1)
                    if g >= 2:
                        sc.wait_ge(hT_ps.sem, g - 1)
                    gate = m.ps[:, g % 4, :].rearrange("p (j u i) -> p j u i", j=2, u=2)[:, :, 0, :]
                    sg_ready.by(nc.scalar.activation(sg[:, g % 2, :].rearrange("p (j i) -> p j i", j=2), gate,
                                                     ACT.Sigmoid))
                    if g >= 1:
                        copy_hT(g - 1)
                    if g >= 2:
                        copy_y(g - 2)
                copy_hT(NGR - 1)
                copy_y(NGR - 2)
                copy_y(NGR - 1)

            @block.gpsimd
            def _(pool):
                ready.by(nc.gpsimd.memset(restart[:, :, 1:], 1.0))
                ready.by(nc.gpsimd.memset(restart[:, :, 0:1], 0.0))
                ready.by(nc.gpsimd.memset(every, 1.0))
                for n in range(KD * HALVES):
                    j, h = n // HALVES, n % HALVES
                    pool.wait_ge(sh_lin.sem, n + 1)
                    dst = hs[:, j, 512 * h:512 * (h + 1)]
                    pl.then_wait(pool, nc.gpsimd.tensor_tensor(dst, sh[:, n % 2, :], lin[:, n % 2, 0, :], ALU.mult))
                    sh_ready.by(nc.gpsimd.tensor_tensor(dst, dst, lin[:, n % 2, 1, :], ALU.mult))
                pool.wait_ge(w_ps.sem, 3)
                xp_sb.by(nc.gpsimd.memset(xp[:, :, SLOTS:], 0.0))
                for i in range(TILES):
                    ln_scale(nc, pool, m, work, i, pl, mv_ready, rs_ready)

            @block.vector
            def _(v):
                step = lambda ins: dve.then_wait(v, ins)
                tt, ts, stt = nc.vector.tensor_tensor, nc.vector.tensor_scalar, nc.vector.scalar_tensor_tensor
                copy_transposed(v, nc.vector.tensor_copy, m, 0, xt_ps, xt_sb)
                v.wait_ge(m.early_in.sem, 16 * EARLY_LOADS)
                v.wait_ge(sc_ready.sem, 1)
                step(tt(mk, score, spread(eb, 1, TILES), ALU.add))
                q = mk.rearrange("p i (g j) -> p (i g) j", j=NE // NG)
                tt(gs[:, 0, :], q[:, :, 0], q[:, :, 1], ALU.max)
                tt(gs[:, 1, :], q[:, :, 0], q[:, :, 1], ALU.min)
                tt(gs[:, 2, :], q[:, :, 2], q[:, :, 3], ALU.max)
                step(tt(gs[:, 3, :], q[:, :, 2], q[:, :, 3], ALU.min))
                step(tt(gs[:, 3, :], gs[:, 1, :], gs[:, 3, :], ALU.max))
                step(tt(gs[:, 1, :], gs[:, 0, :], gs[:, 2, :], ALU.min))
                step(tt(gs[:, 1, :], gs[:, 1, :], gs[:, 3, :], ALU.max))
                step(tt(gs[:, 0, :], gs[:, 0, :], gs[:, 2, :], ALU.max))
                step(tt(gs[:, 0, :], gs[:, 0, :], gs[:, 1, :], ALU.add))
                g3 = gs[:, 0, :].rearrange("p (i g) -> p i g", g=NG)
                for i in range(TILES):
                    others, mine = spread(g3[:, i, :], 1, NG), spread(g3[:, i, :], 2, NG)
                    tt(cmp_[:, 0, i, :, :], others, mine, ALU.is_gt)
                    last = tt(cmp_[:, 1, i, :, :], others, mine, ALU.is_equal)
                step(last)
                c3 = lambda n: cmp_[:, n, :, :, :].rearrange("p i g h -> p i (g h)")
                step(tt(c3(1), c3(1), spread(lower.rearrange("p g h -> p (g h)"), 1, TILES), ALU.mult))
                step(tt(c3(0), c3(0), c3(1), ALU.add))
                step(nc.vector.tensor_reduce(gm, cmp_[:, 0, :, :, :].rearrange("p i g h -> p (i g) h"), AX.X, ALU.add))
                step(ts(gm, gm, TKG - 0.5, None, ALU.is_lt))
                step(tt(q, q, spread(gm, 2, NE // NG), ALU.mult))
                for i in range(TILES):
                    last = nc.vector.max(top[:, i, :], mk[:, i, :])
                step(last)
                fourth = spread(top[:, :, TOPK - 1], 2, NE)
                step(tt(pos, mk, fourth, ALU.is_gt))
                step(tt(mk, mk, fourth, ALU.is_equal))
                step(nc.vector.tensor_reduce(cnt, pos, AX.X, ALU.add))
                step(ts(cnt, cnt, -1.0, TOPK + 0.5, ALU.mult, ALU.add))
                v.wait_ge(ready.sem, 3)
                flat = lambda t: t.rearrange("p i e -> p (i e)")
                step(nc.vector.tensor_tensor_scan(flat(pre), flat(restart), flat(mk), 0.0, ALU.mult, ALU.add))
                step(tt(pre, pre, spread(cnt, 2, NE), ALU.is_lt))
                step(tt(pre, pre, mk, ALU.mult))
                chosen.then_wait(v, tt(pre, pre, pos, ALU.add))
                step(ts(cum[:, 0, :], pre[:, 0, :], 0.0, None, ALU.mult))
                for i in range(1, TILES):
                    (step if i < TILES - 1 else earlier.by)(tt(cum[:, i, :], cum[:, i - 1, :], pre[:, i - 1, :],
                                                               ALU.add))
                step(tt(mk, score, pre, ALU.mult))
                step(nc.vector.tensor_reduce(cnt, mk, AX.X, ALU.add))
                step(ts(cnt, cnt, 1e-20, None, ALU.add))
                step(nc.vector.reciprocal(cnt, cnt))
                info_ready.then_wait(v, stt(info[:, :, 1:], mk, MSCALE, spread(cnt, 2, NE), ALU.mult, ALU.mult))
                v.wait_ge(before_ps.sem, 1)
                step(stt(flat(pos), m.ps[:, 4, 0:TILES * NE], 1.0, flat(pre), ALU.add, ALU.mult))
                step(ts(pos, pos, -1.0, None, ALU.add))
                for i in range(TILES):
                    if i >= 2:
                        v.wait_ge(used.sem, i - 1)
                    hot_ready.by(tt(hot[:, i % 2, :, :], spread(token[:, 0:CAP], 1, NE), spread(pos[:, i, :], 2, CAP),
                                    ALU.is_equal))
                v.wait_ge(used.sem, TILES)
                ps3 = m.ps[:, 0:6, :].rearrange("p (k b) n -> p k (b n)", k=KD)
                xp_sb.by(nc.vector.tensor_copy(xp[:, 1, 0:SLOTS], ps3[:, 1, 0:SLOTS]))
                facts = m.ps[:, 6, 0:ST * (1 + NE)].rearrange("p (s e) -> p s e", e=1 + NE)
                facts_read.by(nc.vector.tensor_copy(slot_token, facts[:, :, 0]))
                facts_read.then_wait(v, tt(sw, facts[:, :, 1:], own, ALU.mult))
                step(nc.vector.tensor_reduce(slot_weight, sw, AX.X, ALU.add))
                for g in range(NGR):
                    u4 = m.ps[:, g % 4, :].rearrange("p (j u i) -> p j u i", j=2, u=2)
                    h = sg[:, g % 2, :].rearrange("p (j i) -> p j i", j=2)
                    v.wait_ge(sg_ready.sem, g + 1)
                    step(tt(h, u4[:, :, 0, :], h, ALU.mult))
                    h_ready.by(tt(h, h, u4[:, :, 1, :], ALU.mult))
                    if 4 * (g + 1) >= BACK_EXPERTS and back_ready.n == 0:
                        for s in range(ST):
                            back_ready.by(ts(back[:, s, :], token, slot_token[:, s:s + 1], slot_weight[:, s:s + 1],
                                             ALU.is_equal, ALU.mult))
                for i in range(TILES):
                    v.wait_ge(o_ps.sem, 2 * (i // 2) + 2)
                    if i >= 2:
                        v.wait_ge(x_ready.sem, i - 1)
                    step(tt(work.r[:, i % 2, :], m.ps[:, i // 2, DM * (i % 2):DM * (i % 2 + 1)], m.x[:, i, :],
                            ALU.add))
                    ln_stats(nc, v, work, i, dve, mv_ready)
                    if i >= 1:
                        ln_apply(nc, v, m, work, i - 1, i - 1, rs_ready, x_ready)
                ln_apply(nc, v, m, work, TILES - 1, TILES - 1, rs_ready, x_ready)


def constants():
    p = np.arange(P)
    f = lambda x: np.ascontiguousarray(x, dtype=np.float32)
    c = {
        "c_ident": f(np.eye(P)),
        "c_eye_q": f(p[:, None] % Q == np.arange(Q)[None, :]),
        "c_sel_last": f(np.broadcast_to((p[:, None] == Q * np.arange(G)[None, :] + Q - 1)[:, :, None], (P, G, P))),
        "c_in_chunk": f(p[:, None] // Q == np.arange(G)[None, :]),
        "c_first8": f(np.broadcast_to(LE - np.arange(LE), (P, LE))),
    }
    c["c_before"] = f(p[:, None] < p[None, :])
    c["c_lower"] = f(np.broadcast_to(np.arange(NG)[None, :] < np.arange(NG)[:, None], (P, NG, NG)))
    c["c_iota"] = f(np.broadcast_to(np.arange(NT), (P, NT)))
    c["c_token"] = f(p[:, None, None] + P * np.arange(TILES)[None, :, None])
    slot = p[:, None] + P * np.arange(ST)[None, :]
    c["c_own"] = f(slot[:, :, None] // CAP == np.arange(NE)[None, None, :])
    pos = np.arange(SEQ, dtype=np.float32)
    inv = (1.0 / np.power(np.float32(10000.0), np.arange(0, HD, 2, dtype=np.float32) / np.float32(HD))).astype(np.float32)
    ang = (pos[:, None] * np.concatenate([inv, inv])[None, 0::2]).astype(np.float32)
    cos, sin = np.repeat(np.cos(ang), 2, axis=1), np.repeat(np.sin(ang), 2, axis=1)
    sin = sin * np.where(np.arange(HD) % 2 == 0, -1.0, 1.0)
    c["c_cos"] = f(cos.reshape(TPH, P, HD).transpose(1, 0, 2))
    c["c_sin"] = f(sin.reshape(TPH, P, HD).transpose(1, 0, 2))
    dist = np.zeros((P, NCOL))
    for k in range(TPH):
        q = np.arange(P * k, SEQ)[None, :]
        key = P * k + p[:, None]
        dist[:, KEY_COL[k]:KEY_COL[k] + SEQ - P * k] = np.where(q >= key, -(q - key), LATER)
    c["c_dist"] = f(dist)
    return c


def build(nc, a, out, upto=99):
    ctx = ExitStack()
    with ctx:
        m = Memory()
        sb = lambda name, shape, dt=F32: ctx.enter_context(nc.sbuf_tensor(name, shape, dt))
        m.ps = ctx.enter_context(nc.psum_tensor("ps", [P, 8, 512], F32))
        m.x = sb("x", [P, TILES, DM])
        m.xT = sb("xT", [P, KD, NT])
        m.ident = sb("ident", [P, P])
        m.half = sb("half", [P, 1])
        m.wz_in, m.late_in, m.const_in, m.small_in, m.dt_in = (Signal(ctx, nc, n) for n in (
            "wz_in", "late_in", "const_in", "small_in", "dt_in"))
        m.lora_in, m.qkv_in, m.attn_in = (Signal(ctx, nc, n) for n in ("lora_in", "qkv_in", "attn_in"))
        m.decay_in = [Signal(ctx, nc, f"decay_in{j}") for j in range(2)]
        m.wo_in, m.early_in, m.gu_in, m.down_in, m.stored = (Signal(ctx, nc, n) for n in (
            "wo_in", "early_in", "gu_in", "down_in", "stored"))
        with ExitStack() as attention:
            sba = lambda name, shape: attention.enter_context(nc.sbuf_tensor(name, shape, F32))
            m.w_down = sba("w_down", [P, KD, LATENT])
            m.b_down = sba("b_down", [LATENT, 1])
            m.b_o = sba("b_o", [P, DM])
            m.gate_b = sba("gate_b", [P, AH])
            m.w_q = sba("w_q", [P, KD, AH * HD])
            first_layer(nc, m, a, upto)
            if upto < 5:
                return store(nc, m, out)
            m.qT = sba("qT", [P, AH, NT])
            m.kv = sba("kv", [P, NKV * NT + TILES * NKV * VW])
            m.kT = m.kv[:, 0:NKV * NT].rearrange("p (g t) -> p g t", t=NT)
            m.v = m.kv[:, NKV * NT:].rearrange("p (i g d) -> p i g d", g=NKV, d=VW)
            bias = sba("bias", [P, BATCH, NCOL])
            m.bias = [bias[:, b, :] for b in range(BATCH)]
            m.dist = m.bias[1]
            with ExitStack() as once:
                sbo = lambda name, shape: once.enter_context(nc.sbuf_tensor(name, shape, F32))
                m.w_up = sbo("w_up", [LATENT, 2 * NKV * HD])
                m.b_up = sbo("b_up", [P, 2 * NKV * HD])
                m.b_q = sbo("b_q", [P, AH * HD])
                m.norm_qk = sbo("norm_qk", [P, 2, HD])
                m.cos_row = sbo("cos_row", [P, TPH, HD])
                m.sin_row = sbo("sin_row", [P, TPH, HD])
                prepare_attention(nc, m, a)
            m.w_o = m.w_q[:, :, :].rearrange("p k (h n) -> p (k h) n", n=DM)
            m.gate_w = m.xT[:, :, :].rearrange("p k (h e) -> p (k h) e", e=HD)
            m.weights = sba("weights", [P, 2 * NE * DM])
            m.rows = m.weights[:, 0:NE * DM]
            m.w_gu = m.weights[:, :].rearrange("p (e k u i) -> p e k u i", k=KD, u=2, i=EI)
            m.w_down_e = m.kv[:, 0:NE * DM].rearrange("p (e d) -> p e d", d=DM)
            attend(nc, m, a)
            early = Space(bias[:, :, :].rearrange("p b n -> p (b n)"))
            m.early = Memory()
            m.early.router, m.early.e_bias, m.early.before = early.take(NE, DM), early.take(P, NE), early.take(P, P)
            m.early.lower, m.early.token = early.take(P, NG, NG), early.take(P, NT)
            m.early.own, m.early.info = early.take(P, ST, NE), early.take(P, TILES, 1 + NE)
            attention_output(nc, m, a)
            nc.all_engine_barrier(sems_to_clear=range(m.stored.sem.num + 1, SEMAPHORES))
            m.free = [Space(m.qT[:, :, :].rearrange("p h t -> p (h t)")),
                      Space(m.w_q[:, :, :].rearrange("p k n -> p (k n)")), early]
            m.y_dram = nc.dram_tensor("y_dram", (SLOTS, DM), F32, kind="Internal").ap()
            route_and_run_experts(nc, m, a, out)


def first_layer(nc, m, a, upto):
        with ExitStack() as lora:
            sbl = lambda name, shape: lora.enter_context(nc.sbuf_tensor(name, shape, F32))
            m.lw_a = sbl("lw_a", [P, LE * LR // P, DM])
            m.lw_b = sbl("lw_b", [P, KD, LE, LR])
            m.lw_g = sbl("lw_g", [LE, DM])
            m.first8 = sbl("first8", [P, LE])
            mixer_layer(nc, m, a, upto)
            if upto >= 4:
                lora_experts(nc, m, a)


def mixer_layer(nc, m, a, upto):
        with ExitStack() as mixer:
            sbm = lambda name, shape: mixer.enter_context(nc.sbuf_tensor(name, shape, F32))
            m.w_in = sbm("w_in", [P, KD, PROJ])
            m.w_out = sbm("w_out", [P, INTER // P, DM])
            m.norm_w = sbm("norm_w", [P, INTER // P])
            m.conv_w = sbm("conv_w", [P, CT, KCONV])
            m.conv_b = sbm("conv_b", [P, CT])
            m.d_row = sbm("d_row", [P, HEADS])
            m.eye_q = sbm("eye_q", [P, Q])
            m.sel_last = sbm("sel_last", [P, G, P])
            m.in_chunk = sbm("in_chunk", [P, G])
            m.xc = sbm("xc", [P, CT, NT])
            m.dtT = sbm("dtT", [P, SEQ])
            m.sinceT = sbm("sinceT", [P, SEQ])
            m.decay = sbm("decay", [P, 2, HEADS, Q])
            m.x_row = sbm("x_row", [P, TILES, INTER])
            m.b_row = sbm("b_row", [P, TILES, NSTATE])
            m.since_row = sbm("since_row", [P, TILES, HEADS])
            m.da_dram = nc.dram_tensor("da_dram", (BATCH * CHUNKS, HEADS, Q), F32, kind="Internal").ap()
            project_and_convolve(nc, m, a)
            with ExitStack() as pair:
                m.dt_end = pair.enter_context(nc.sbuf_tensor("dt_end", [P, TILES, HEADS, PDIM], F32))
                if upto >= 2:
                    within_chunks(nc, m, a)
                if upto >= 3:
                    carry_states(nc, m, a)


def store(nc, m, out):
    with ExitStack() as ctx:
        stored = Signal(ctx, nc, "stored")
        with nc.Block() as block:
            @block.sync
            def _(sp):
                sp.dma_start(rows(out), m.x[:, :, :]).then_inc(stored.sem, 16)
                sp.wait_ge(stored.sem, 16)


def kernel(**inputs):
    import concourse.bacc as bacc
    from concourse.bass_utils import run_bass_kernel_spmd

    nc = bacc.Bacc("TRN2", target_bir_lowering=False, num_devices=1)
    arrays, a = {}, {}
    for name, value in {**inputs, **constants()}.items():
        value = np.ascontiguousarray(value)
        arrays[f"in_{name}"] = value
        a[name] = nc.dram_tensor(f"in_{name}", value.shape, mybir.dt.from_np(value.dtype), kind="ExternalInput").ap()
    a["x"] = a["L0_attn_hidden_states"].rearrange("b t d -> (b t) d")
    out = nc.dram_tensor("out_0", (BATCH, SEQ, DM), F32, kind="ExternalOutput").ap()
    build(nc, a, out.rearrange("b t d -> (b t) d"))
    results = run_bass_kernel_spmd(nc, [arrays], core_ids=[0]).results
    return results[0]["out_0"]
```

```python
from contextlib import ExitStack

import numpy as np

import concourse.bass as bass
from concourse import mybir

F32 = mybir.dt.float32
BF16 = mybir.dt.bfloat16
PARTS = 3
U32 = mybir.dt.uint32
ALU = mybir.AluOpType
ACT = mybir.ActivationFunctionType
AX = mybir.AxisListType

P = 128
BATCH, SEQ, DM = 2, 512, 256
NT = BATCH * SEQ
TILES = NT // P
HALVES = NT // 512
KD = DM // P
TPH = TILES // HALVES

INTER, HEADS, PDIM, NSTATE, KCONV = 512, 64, 8, 128, 4
CONV = INTER + 2 * NSTATE
CT = CONV // P
PROJ = 2 * INTER + 2 * NSTATE + HEADS
Q = 32
G = P // Q
CHUNKS = SEQ // Q
HQ = 16
RING = 8

LE, LR, LSCALE = 8, 64, 64.0 / 16.0

AH, HD, NKV, LATENT = 16, 128, 4, 64
KVG = AH // NKV
QKH = AH + NKV
SEL_TOPK, SEL_DIM = 64, 64
SOFTCAP = 30.0
SLOPE = [2.0 ** (-8.0 * (h + 1) / AH) for h in range(AH)]
KEY_COL = [0, 512, 1024, 896]
NCOL = 1280
VW = HD + 1
LATER, TAKEN, FAR = -1e30, -3e38, -1e30

NE, NG, TKG, TOPK, MSCALE = 32, 8, 3, 4, 2.5
CAP = -(-5 * NT // (4 * NE))
SLOTS = NE * CAP
ST = SLOTS // P
EI = 128
PAIR_ROWS = P // 2

LN_EPS = 1e-5
SEMAPHORES = 256


class Signal:

    def __init__(self, ctx, nc, name):
        self.sem = ctx.enter_context(nc.semaphore(name))
        self.n = 0

    def by(self, ins):
        ins.then_inc(self.sem, 1)
        self.n += 1

    def then_wait(self, eng, ins):
        self.by(ins)
        eng.wait_ge(self.sem, self.n)


def spread(ap, axis, n):
    a = ap.unsqueeze(axis)
    shape = list(a.shape)
    shape[axis] = n
    return a.broadcast_to(shape)


class Memory:
    pass


class Space:

    def __init__(self, ap):
        self.ap, self.at = ap, 0

    def fits(self, shape):
        return self.at + int(np.prod(shape[1:])) <= self.ap.shape[1]

    def take(self, parts, *shape):
        n = int(np.prod(shape))
        assert self.at + n <= self.ap.shape[1], (self.at, n)
        piece = self.ap[0:parts, self.at:self.at + n]
        self.at += n
        names = "abcd"[:len(shape)]
        if len(shape) > 1:
            piece = piece.rearrange(f"p ({' '.join(names)}) -> p {' '.join(names)}",
                                    **{k: v for k, v in zip(names[1:], shape[1:])})
        return piece


def rows(dram):
    return dram.rearrange("(i p) d -> p i d", p=P)


def k_tiles(dram):
    return dram.rearrange("(k p) n -> p k n", p=P)


def transpose_rows(pe, nc, m, bank, ready, done):
    for h in range(HALVES):
        for k in range(KD):
            for j in range(TPH):
                i = h * TPH + j
                ready(i)
                last = nc.tensor.transpose(m.ps[:, bank + h * KD + k, P * j:P * (j + 1)],
                                           m.x[:, i, P * k:P * (k + 1)], m.ident[:, :])
            done.by(last)


def copy_transposed(eng, copy, m, bank, transposed, copied):
    for h in range(HALVES):
        for k in range(KD):
            n = h * KD + k
            eng.wait_ge(transposed.sem, n + 1)
            copied.by(copy(m.xT[:, k, 512 * h:512 * (h + 1)], m.ps[:, bank + n, :]))


def load_decay(nc, m, sp, i):
    for g in range(G):
        sp.dma_start(m.decay[Q * g:Q * (g + 1), i % 2, :, :].rearrange("p h t -> p (h t)"),
                     m.da_dram[G * i + g, :, :].rearrange("h t -> (h t)").partition_broadcast(Q)
                     ).then_inc(m.decay_in[i % 2].sem, 16)


def project_and_convolve(nc, m, a):
    with ExitStack() as ctx:
        sig = lambda name: Signal(ctx, nc, "proj_" + name)
        sb = lambda name, shape: ctx.enter_context(nc.sbuf_tensor("proj_" + name, shape, F32))
        raw = sb("raw", [P, CT, BATCH, KCONV - 1 + SEQ])
        acc = sb("acc", [P, 4, NT])
        th = sb("th", [P, 2, NT])
        hb = sb("hb", [P, CT])
        al = sb("al", [P, 2])
        dtb = sb("dtb", [P, 1])
        u = sb("u", [P, SEQ])
        e = sb("e", [P, SEQ])
        w = sb("w", [P, SEQ])
        lw = sb("lw", [P, SEQ])
        d1 = sb("d1", [P, SEQ])
        eq = sb("eq", [P, SEQ])

        x_in, w_in, ct_in = sig("x_in"), sig("w_in"), sig("ct_in")
        small_in, dt_in = m.small_in, m.dt_in
        xt_ps, xt_sb = sig("xt_ps"), sig("xt_sb")
        proj_ps, raw_sb, dt_sb = sig("proj_ps"), sig("raw_sb"), sig("dt_sb")
        pad_zero, dve, act = sig("pad_zero"), sig("dve1"), sig("act1")
        e_ready, w_ready, lw_ready, dt_ready, da_ready = (sig(n) for n in
                                                          ("e_ready", "w_ready", "lw_ready", "dt_ready", "da_ready"))
        daz_ready, daz_out = sig("daz_ready"), sig("daz_out")
        a_ready, conv_done, tapped, th_ready, silu_done, hb_ready = (sig(n) for n in
                                                           ("a_ready", "conv_done", "tapped", "th_ready",
                                                            "silu_done", "hb_ready"))
        order = [4, 5, 0, 1, 2, 3]
        W_DT = PROJ - HEADS

        with nc.Block() as block:
            @block.sync
            def _(sp):
                sp.dma_start(m.ident[:, :], a["c_ident"]).then_inc(x_in.sem, 16)
                for h in range(HALVES):
                    sp.dma_start(m.x[:, TPH * h:TPH * (h + 1), :],
                                 rows(a["x"])[:, TPH * h:TPH * (h + 1), :]).then_inc(x_in.sem, 16)
                sp.dma_start(m.w_in[:, :, INTER:PROJ], k_tiles(a["L0_attn_in_proj_w"])[:, :, INTER:PROJ]
                             ).then_inc(w_in.sem, 16)
                sp.dma_start(m.w_in[:, :, 0:INTER], k_tiles(a["L0_attn_in_proj_w"])[:, :, 0:INTER]
                             ).then_inc(m.wz_in.sem, 16)
                sp.dma_start(m.w_out[:, :, :], k_tiles(a["L0_attn_out_proj_w"])).then_inc(m.late_in.sem, 16)
                sp.dma_start(m.norm_w[:, :], a["L0_attn_norm_w"].rearrange("(k p) -> p k", p=P),
                             allow_slow_non_contiguous=True).then_inc(m.late_in.sem, 16)
                load_lora(nc, m, a, sp)
                sp.wait_ge(daz_ready.sem, 1)
                for b in range(BATCH):
                    sp.dma_start(m.da_dram[CHUNKS * b:CHUNKS * (b + 1), :, :].rearrange("c h t -> h c t"),
                                 w[HEADS * b:HEADS * (b + 1), :].rearrange("h (c t) -> h c t", t=Q),
                                 allow_slow_non_contiguous=True).then_inc(daz_out.sem, 16)
                sp.wait_ge(daz_out.sem, 32)
                for i in range(2):
                    load_decay(nc, m, sp, i)

            @block.gpsimd
            def _(pool):
                for b in range(BATCH):
                    own = slice(HEADS * b, HEADS * (b + 1))
                    pool.dma_start(al[own, 0:1], a["L0_attn_A_log"].unsqueeze(1),
                                   allow_slow_non_contiguous=True).then_inc(dt_in.sem, 16)
                    pool.dma_start(dtb[own, :], a["L0_attn_dt_bias"].unsqueeze(1),
                                   allow_slow_non_contiguous=True).then_inc(dt_in.sem, 16)
                pool.dma_start(m.conv_w[:, :, :], a["L0_attn_conv_w"].rearrange("(c p) k -> p c k", p=P),
                               allow_slow_non_contiguous=True).then_inc(small_in.sem, 16)
                pool.dma_start(m.conv_b[:, :], a["L0_attn_conv_b"].rearrange("(c p) -> p c", p=P),
                               allow_slow_non_contiguous=True).then_inc(small_in.sem, 16)
                pool.dma_start(m.d_row[:, :], a["L0_attn_D"].partition_broadcast(P)).then_inc(m.const_in.sem, 16)
                for t, name in ((m.eye_q[:, :], "c_eye_q"), (m.sel_last[:, :, :], "c_sel_last"),
                                (m.in_chunk[:, :], "c_in_chunk")):
                    pool.dma_start(t, a[name]).then_inc(m.const_in.sem, 16)
                pad_zero.by(nc.gpsimd.memset(raw[:, :, :, 0:KCONV - 1], 0.0))
                pad_zero.by(nc.gpsimd.memset(m.half[:, :], -0.5))
                pad_zero.by(nc.gpsimd.memset(d1[:, :], 0.0))

            @block.tensor
            def _(pe):
                pe.wait_ge(x_in.sem, 48)
                transpose_rows(pe, nc, m, 0, lambda i: None, xt_ps)
                pe.wait_ge(w_in.sem, 16)
                pe.wait_ge(xt_sb.sem, 4)
                n = 0
                for h in range(HALVES):
                    for k in range(KD):
                        last = nc.tensor.matmul(m.ps[HEADS * h:HEADS * (h + 1), 4 + n, :], m.w_in[:, k, W_DT:PROJ],
                                                m.xT[:, k, 512 * h:512 * (h + 1)], start=k == 0, stop=k == KD - 1)
                    proj_ps.by(last)
                    n += 1
                for ct in order:
                    for h in range(HALVES):
                        if n >= 8:
                            if n < 10:
                                pe.wait_ge(dt_sb.sem, n - 7)
                            else:
                                pe.wait_ge(raw_sb.sem, n - 9)
                        for k in range(KD):
                            last = nc.tensor.matmul(m.ps[:, (4 + n) % 8, :],
                                                    m.w_in[:, k, INTER + P * ct:INTER + P * (ct + 1)],
                                                    m.xT[:, k, 512 * h:512 * (h + 1)], start=k == 0, stop=k == KD - 1)
                        proj_ps.by(last)
                        n += 1

            @block.scalar
            def _(sc):
                sc.wait_ge(dt_in.sem, 64)
                act.then_wait(sc, nc.scalar.activation(al[:, 1:2], al[:, 0:1], ACT.Exp))
                a_ready.by(nc.scalar.mul(al[:, 0:1], al[:, 1:2], -1.0))
                sc.wait_ge(dt_sb.sem, 2)
                act.then_wait(sc, nc.scalar.activation(e[:, :], u[:, :], ACT.Abs))
                e_ready.by(nc.scalar.activation(e[:, :], e[:, :], ACT.Exp, scale=-1.0))
                sc.wait_ge(pad_zero.sem, 1)

                def copy_raw(n):
                    ct, h = order[n // 2], n % 2
                    sc.wait_ge(proj_ps.sem, n + 3)
                    raw_sb.by(nc.scalar.activation(raw[:, ct, h, KCONV - 1:], m.ps[:, (6 + n) % 8, :],
                                                   ACT.Copy, scale=0.25))

                def first_tap(n):
                    ct = order[n]
                    if n >= 4:
                        sc.wait_ge(silu_done.sem, n - 3)
                    tapped.by(nc.scalar.activation(acc[:, n % 4, :].rearrange("p (b t) -> p b t", b=BATCH),
                                                   raw[:, ct, :, 0:SEQ], ACT.Identity, scale=m.conv_w[:, ct, 0:1],
                                                   bias=hb[:, ct:ct + 1]))

                for n in range(4):
                    copy_raw(n)
                sc.wait_ge(raw_sb.sem, 4)
                sc.wait_ge(small_in.sem, 32)
                hb_ready.then_wait(sc, nc.scalar.mul(hb[:, :], m.conv_b[:, :], 0.5))
                first_tap(0)
                first_tap(1)
                sc.wait_ge(w_ready.sem, 1)
                lw_ready.by(nc.scalar.activation(lw[:, :], w[:, :], ACT.Ln))
                for n in range(4, 12):
                    copy_raw(n)
                sc.wait_ge(raw_sb.sem, 12)
                first_tap(2)
                first_tap(3)
                sc.wait_ge(dt_ready.sem, 1)
                sc.wait_ge(a_ready.sem, 1)
                da_ready.by(nc.scalar.activation(w[:, :], m.dtT[:, :], ACT.Exp, scale=al[:, 0:1]))
                for n, ct in enumerate(order):
                    sc.wait_ge(conv_done.sem, n + 1)
                    if n >= 2:
                        sc.wait_ge(silu_done.sem, n - 1)
                    th_ready.by(nc.scalar.activation(th[:, n % 2, :], acc[:, n % 4, :], ACT.Tanh))
                    if n + 4 < CT:
                        first_tap(n + 4)

            @block.vector
            def _(v):
                copy_transposed(v, nc.vector.tensor_copy, m, 0, xt_ps, xt_sb)
                v.wait_ge(dt_in.sem, 64)
                for h in range(HALVES):
                    v.wait_ge(proj_ps.sem, h + 1)
                    own = slice(HEADS * h, HEADS * (h + 1))
                    dt_sb.by(nc.vector.tensor_scalar(u[own, :], m.ps[own, 4 + h, :], dtb[own, 0:1], None, ALU.add))
                v.wait_ge(e_ready.sem, 1)
                w_ready.then_wait(v, nc.vector.tensor_scalar(w[:, :], e[:, :], 1.0, None, ALU.add))
                v.wait_ge(pad_zero.sem, 3)

                def convolve(n):
                    ct = order[n]
                    v.wait_ge(raw_sb.sem, 2 * n + 2)
                    out = acc[:, n % 4, :].rearrange("p (b t) -> p b t", b=BATCH)
                    v.wait_ge(tapped.sem, n + 1)
                    for k in range(1, KCONV):
                        last = nc.vector.scalar_tensor_tensor(out, raw[:, ct, :, k:k + SEQ], m.conv_w[:, ct, k:k + 1],
                                                              out, ALU.mult, ALU.add)
                        (conv_done if k == KCONV - 1 else dve).then_wait(v, last)

                def finish_silu(n):
                    v.wait_ge(th_ready.sem, n + 1)
                    silu_done.by(nc.vector.scalar_tensor_tensor(m.xc[:, order[n], :], th[:, n % 2, :], 1.0,
                                                                acc[:, n % 4, :], ALU.add, ALU.mult))

                v.wait_ge(small_in.sem, 32)
                convolve(0)
                v.wait_ge(lw_ready.sem, 1)
                dve.then_wait(v, nc.vector.tensor_scalar(w[:, :], w[:, :], -1.0, None, ALU.add))
                dve.then_wait(v, nc.vector.tensor_scalar(eq[:, :], w[:, :], 0.0, None, ALU.is_equal))
                nc.vector.tensor_tensor(lw[:, :], lw[:, :], eq[:, :], ALU.add).then_inc(dve.sem, 1)
                dve.n += 1
                dve.then_wait(v, nc.vector.tensor_tensor(w[:, :], w[:, :], eq[:, :], ALU.add))
                dve.then_wait(v, nc.vector.reciprocal(w[:, :], w[:, :]))
                dve.then_wait(v, nc.vector.tensor_tensor(lw[:, :], lw[:, :], w[:, :], ALU.mult))
                dve.then_wait(v, nc.vector.tensor_tensor(lw[:, :], lw[:, :], e[:, :], ALU.mult))
                dt_ready.by(nc.vector.scalar_tensor_tensor(m.dtT[:, :], u[:, :], 0.0, lw[:, :], ALU.max, ALU.add))
                convolve(1)
                v.wait_ge(da_ready.sem, 1)
                starts = lambda t: t[:, :].rearrange("h (c t) -> h c t", t=Q)[:, :, 0:1]
                dve.then_wait(v, nc.vector.tensor_copy(starts(d1), starts(w)))
                daz_ready.then_wait(v, nc.vector.memset(starts(w), 0.0))
                dve.by(nc.vector.tensor_tensor_scan(m.sinceT[:, :], w[:, :], d1[:, :], 0.0, ALU.mult, ALU.add))
                for n in range(2, CT):
                    finish_silu(n - 2)
                    convolve(n)
                finish_silu(CT - 2)
                finish_silu(CT - 1)


def within_chunks(nc, m, a):
    with ExitStack() as ctx:
        sig = lambda name: Signal(ctx, nc, "chunk_" + name)
        sb = lambda name, shape: ctx.enter_context(nc.sbuf_tensor("chunk_" + name, shape, F32))
        eye = sb("eye", [P, HQ, Q])
        gram = sb("gram", [P, 2, Q])
        dec = sb("dec", [P, 2, HEADS, Q])
        mix = sb("mix", [P, 2, HEADS, Q])
        dtx = sb("dtx", [P, 2, HEADS, PDIM])
        dtd = sb("dtd", [P, 2, HEADS, G, PDIM])
        dt_row = sb("dt_row", [P, TILES, HEADS])

        b_ps, b_sb, row_ps, row_sb = sig("b_ps"), sig("b_sb"), sig("row_ps"), sig("row_sb")
        z_ps, z_sb = sig("z_ps"), sig("z_sb")
        x_ps, x_sb, gram_ps, gram_sb = sig("x_ps"), sig("x_sb"), sig("gram_ps"), sig("gram_sb")
        scanned, mixed, dtx_ready, spreaded = (sig(n) for n in ("scanned", "mixed", "dtx_ready", "spreaded"))
        intra_ps, intra_sb, dtf_ready, eye_ready = (sig(n) for n in ("intra_ps", "intra_sb", "dtf_ready", "eye_ready"))
        NQ = HEADS // HQ
        with nc.Block() as block:
            @block.sync
            def _(sp):
                for i in range(2, TILES):
                    sp.wait_ge(scanned.sem, NQ * (i - 1))
                    load_decay(nc, m, sp, i)

            @block.tensor
            def _(pe):
                for i in range(TILES):
                    last = nc.tensor.transpose(m.ps[:, 4 + i // 4, P * (i % 4):P * (i % 4 + 1)],
                                               m.xc[:, 4, P * i:P * (i + 1)], m.ident[:, :])
                b_ps.by(last)
                for bank, src in ((6, m.dtT), (7, m.sinceT)):
                    by_tile = m.ps[:, bank, :].rearrange("p (b j h) -> p j b h", b=BATCH, j=TPH)
                    for j in range(TPH):
                        last = nc.tensor.transpose(by_tile[:, j, :, :], src[:, P * j:P * (j + 1)], m.ident[:, :])
                row_ps.by(last)
                pe.wait_ge(m.const_in.sem, 16 * 4)

                pe.wait_ge(m.wz_in.sem, 16)

                def feed(i):
                    if i >= 1:
                        pe.wait_ge(x_sb.sem, i)
                        pe.wait_ge(gram_sb.sem, i)
                    for c in range(4):
                        last = nc.tensor.transpose(m.ps[:, 2, P * c:P * (c + 1)], m.xc[:, c, P * i:P * (i + 1)],
                                                   m.ident[:, :])
                    x_ps.by(last)
                    t = slice(P * i, P * (i + 1))
                    gram_ps.by(nc.tensor.matmul(m.ps[:, 3, 0:P], m.xc[:, 4, t], m.xc[:, 5, t], start=True, stop=True))
                    if i >= 2:
                        pe.wait_ge(z_sb.sem, i - 1)
                    for k in range(KD):
                        last = nc.tensor.matmul(m.ps[:, i % 2, :], m.xT[:, k, P * i:P * (i + 1)],
                                                m.w_in[:, k, 0:INTER], start=k == 0, stop=k == KD - 1)
                    z_ps.by(last)
                feed(0)
                pe.wait_ge(b_sb.sem, 2)
                pe.wait_ge(row_sb.sem, 2)
                for i in range(TILES):
                    if i + 1 < TILES:
                        feed(i + 1)
                    pe.wait_ge(mixed.sem, i + 1)
                    pe.wait_ge(spreaded.sem, i + 1)
                    if i >= 2:
                        pe.wait_ge(intra_sb.sem, G * (i - 1))
                    own = slice(Q * (i % 2), Q * (i % 2 + 1))
                    for h in range(HEADS):
                        last = nc.tensor.matmul(m.ps[own, 4 + h // HQ, (G * PDIM) * (h % HQ):(G * PDIM) * (h % HQ + 1)],
                                                mix[:, i % 2, h, :],
                                                dtd[:, i % 2, h, :, :].rearrange("p g d -> p (g d)"),
                                                start=True, stop=True)
                    intra_ps.by(last)

            @block.scalar
            def _(sc):
                sc.wait_ge(b_ps.sem, 1)
                for j in range(2):
                    b_sb.by(nc.scalar.copy(m.b_row[:, 4 * j:4 * j + 4, :].rearrange("p i n -> p (i n)"),
                                           m.ps[:, 4 + j, :]))
                sc.wait_ge(row_ps.sem, 1)
                row_sb.by(nc.scalar.copy(dt_row[:, :, :].rearrange("p i h -> p (i h)"), m.ps[:, 6, :]))
                row_sb.by(nc.scalar.copy(m.since_row[:, :, :].rearrange("p i h -> p (i h)"), m.ps[:, 7, :]))

                def intra_out(i):
                    sc.wait_ge(intra_ps.sem, i + 1)
                    src = m.ps[Q * (i % 2):Q * (i % 2 + 1), 4:8, :].rearrange("t b (h g d) -> t b h g d", g=G, d=PDIM)
                    for g in range(G):
                        dst = m.xc[Q * g:Q * (g + 1), 0:4, P * i:P * (i + 1)]
                        intra_sb.by(nc.scalar.copy(dst.rearrange("t b (h d) -> t b h d", d=PDIM), src[:, :, :, g, :]))

                def feed_out(i):
                    sc.wait_ge(x_ps.sem, i + 1)
                    x_sb.by(nc.scalar.copy(m.x_row[:, i, :], m.ps[:, 2, :]))
                    sc.wait_ge(gram_ps.sem, i + 1)
                    if i >= 2:
                        sc.wait_ge(mixed.sem, i - 1)
                    for g in range(G):
                        last = nc.scalar.copy(gram[Q * g:Q * (g + 1), i % 2, :],
                                              m.ps[Q * g:Q * (g + 1), 3, Q * g:Q * (g + 1)])
                    gram_sb.by(last)

                feed_out(0)
                for i in range(TILES):
                    sc.wait_ge(dtx_ready.sem, i + 1)
                    if i >= 2:
                        sc.wait_ge(intra_ps.sem, i - 1)
                    for g in range(G):
                        last = nc.scalar.activation(dtd[:, i % 2, :, g, :], dtx[:, i % 2, :, :], ACT.Copy,
                                                    scale=m.in_chunk[:, g:g + 1])
                    spreaded.by(last)
                    if i + 1 < TILES:
                        feed_out(i + 1)
                    if i >= 1:
                        intra_out(i - 1)
                intra_out(TILES - 1)

            @block.vector
            def _(v):
                v.wait_ge(m.const_in.sem, 16 * 4)
                eye_ready.then_wait(v, nc.vector.tensor_copy(eye[:, :, :], spread(m.eye_q[:, :], 1, HQ)))
                v.wait_ge(row_sb.sem, 2)
                for i in range(TILES):
                    v.wait_ge(x_sb.sem, i + 1)
                    if i >= 2:
                        v.wait_ge(spreaded.sem, i - 1)
                    dtx_ready.by(nc.vector.tensor_tensor(
                        dtx[:, i % 2, :, :], m.x_row[:, i, :].rearrange("p (h d) -> p h d", d=PDIM),
                        spread(dt_row[:, i, :], 2, PDIM), ALU.mult))
                    if i >= 2:
                        v.wait_ge(mixed.sem, i - 1)
                    v.wait_ge(m.decay_in[i % 2].sem, 16 * G * (i // 2 + 1))
                    for q in range(NQ):
                        scanned.by(nc.vector.tensor_tensor_scan(
                            dec[:, i % 2, HQ * q:HQ * (q + 1), :].rearrange("p h t -> p (h t)"),
                            m.decay[:, i % 2, HQ * q:HQ * (q + 1), :].rearrange("p h t -> p (h t)"), eye[:, :, :].rearrange("p h t -> p (h t)"),
                            0.0, ALU.mult, ALU.add))
                    v.wait_ge(scanned.sem, NQ * (i + 1))
                    dtf_ready.by(nc.vector.tensor_tensor(m.dt_end[:, i, :, :], dtx[:, i % 2, :, :],
                                                         spread(dec[:, i % 2, :, Q - 1], 2, PDIM), ALU.mult))
                    v.wait_ge(z_ps.sem, i + 1)
                    z_sb.by(nc.vector.tensor_copy(m.z_row[:, i, :], m.ps[:, i % 2, :]))

            @block.gpsimd
            def _(pool):
                for i in range(TILES):
                    if i >= 2:
                        pool.wait_ge(intra_ps.sem, i - 1)
                    pool.wait_ge(scanned.sem, NQ * (i + 1))
                    pool.wait_ge(gram_sb.sem, i + 1)
                    mixed.by(nc.gpsimd.tensor_tensor(mix[:, i % 2, :, :], dec[:, i % 2, :, :],
                                                     spread(gram[:, i % 2, :], 1, HEADS), ALU.mult))


def carry_states(nc, m, a):
    with ExitStack() as ctx:
        sig = lambda name: Signal(ctx, nc, "state_" + name)
        sb = lambda name, shape: ctx.enter_context(nc.sbuf_tensor("state_" + name, shape, F32))
        st = sb("st", [P, BATCH, RING, HEADS, PDIM])
        tmp = sb("tmp", [P, 2, HEADS, PDIM])
        y = sb("y", [P, 2, HEADS, PDIM])
        xd = sb("xd", [P, 2, HEADS, PDIM])
        th = sb("thz", [P, 2, INTER])
        zs = sb("zs", [P, 2, INTER])
        sq = sb("sq", [P, INTER])
        ss = sb("ss", [P, TILES])
        rms = sb("rms", [P, TILES])
        gt = sb("gt", [P, 2, INTER])
        r = sb("r", [P, 2, DM])
        bs = sb("bs", [P, 2, 6])
        mv = sb("mv", [P, 2, 2])
        rs = sb("rs", [P, 2, 1])
        shift = sb("shift", [P, 2, 1])

        whole = m.decay[:, 0, :, :].rearrange("p h t -> p (h t)").rearrange("p (g i h) -> p g i h", i=TILES, h=HEADS)
        decay_sb = sig("decay_sb")
        zero, decay_ps, new_ps, carried, inter_ps = (sig(n) for n in ("zero", "decay_ps", "new_ps", "carried",
                                                                      "inter_ps"))
        y1, y2, xd_ready, th_ready, zs_ready = (sig(n) for n in ("y1", "y2", "xd_ready", "th_ready",
                                                                       "zs_ready"))
        ss_ready, gated, gt_ps, gt_sb, out_ps, rms_ready = (sig(n) for n in ("ss_ready", "gated", "gt_ps", "gt_sb",
                                                                             "out_ps", "rms_ready"))
        dve, pl, wn, mv_ready, rs_ready, resid = (sig(n) for n in ("dve3", "pool3", "wn", "mv_ready", "rs_ready",
                                                                  "resid"))
        tiles = [i // 2 + TPH * (i % 2) for i in range(TILES)]
        NEW, INTER_BANK = [0, 1, 2, 5], 3
        LAG = 2
        steps = [(n, g) for n in range(TILES) for g in range(G) if n < TILES - BATCH or g < G - 1]
        before = lambda n, g: sum(step < (n, g) for step in steps)
        with nc.Block() as block:
            @block.tensor
            def _(pe):
                for g in range(G):
                    decay_ps.by(nc.tensor.matmul(m.ps[:, 4 + g, :], m.sel_last[:, g, :],
                                                 m.since_row[:, :, :].rearrange("p i h -> p (i h)"), start=True,
                                                 stop=True))
                pe.wait_ge(zero.sem, 1)

                def turn_gated(n):
                    pe.wait_ge(gated.sem, n + 1)
                    if n >= 1:
                        pe.wait_ge(gt_sb.sem, n)
                    for c in range(4):
                        last = nc.tensor.transpose(m.ps[:, 6, P * c:P * (c + 1)], th[:, n % 2, P * c:P * (c + 1)],
                                                   m.ident[:, :])
                    gt_ps.by(last)

                def project_out(n):
                    pe.wait_ge(gt_sb.sem, n + 1)
                    if n == 0:
                        pe.wait_ge(wn.sem, 4)
                    if n >= 1:
                        pe.wait_ge(mv_ready.sem, n)
                    for c in range(4):
                        last = nc.tensor.matmul(m.ps[:, 7, 0:DM], gt[:, n % 2, P * c:P * (c + 1)], m.w_out[:, c, :],
                                                start=c == 0, stop=c == 3)
                    out_ps.by(last)

                def new_states(n):
                    i = tiles[n]
                    for g in range(G):
                        if (n, g) not in steps:
                            continue
                        k = before(n, g)
                        if k == NEW.index(5):
                            pe.wait_ge(decay_sb.sem, G)
                        if k >= len(NEW):
                            pe.wait_ge(carried.sem, k - len(NEW) + 1)
                        new_ps.by(nc.tensor.matmul(m.ps[:, NEW[k % len(NEW)], :], m.b_row[Q * g:Q * (g + 1), i, :],
                                                   m.dt_end[Q * g:Q * (g + 1), i, :, :].rearrange("p h d -> p (h d)"),
                                                   start=True, stop=True))

                new_states(0)
                for n, i in enumerate(tiles):
                    b = i // TPH
                    if n + 1 < TILES:
                        new_states(n + 1)
                    if n >= LAG:
                        turn_gated(n - LAG)
                    if n >= 2:
                        pe.wait_ge(y1.sem, n - 1)
                    for g in range(G):
                        c = G * (i % TPH) + g
                        if n >= BATCH or g:
                            pe.wait_ge(carried.sem, before(n - BATCH, G) if g == 0 else before(n, g))
                        last = nc.tensor.matmul(m.ps[Q * g:Q * (g + 1), INTER_BANK + n % 2, :],
                                                m.xc[:, 5, P * i + Q * g:P * i + Q * (g + 1)],
                                                st[:, b, c % RING, :, :].rearrange("p h d -> p (h d)"),
                                                start=True, stop=True)
                    inter_ps.by(last)
                    if n >= LAG:
                        project_out(n - LAG)
                for n in range(TILES - LAG, TILES):
                    turn_gated(n)
                    project_out(n)

            @block.scalar
            def _(sc):
                for g in range(G):
                    sc.wait_ge(decay_ps.sem, g + 1)
                    decay_sb.by(nc.scalar.copy(whole[:, g, :, :].rearrange("p i h -> p (i h)"), m.ps[:, 4 + g, :]))

                def copy_gated(n):
                    sc.wait_ge(gt_ps.sem, n + 1)
                    if n >= 2:
                        sc.wait_ge(out_ps.sem, n - 1)
                    gt_sb.by(nc.scalar.copy(gt[:, n % 2, :], m.ps[:, 6, :]))

                def normalise(n):
                    sc.wait_ge(rs_ready.sem, n + 1)
                    resid.by(nc.scalar.activation(m.x[:, tiles[n], :], r[:, n % 2, :], ACT.Identity,
                                                  bias=shift[:, n % 2, 0:1], scale=rs[:, n % 2, 0:1]))

                for n, i in enumerate(tiles):
                    if n >= LAG:
                        copy_gated(n - LAG)
                    if n >= 2:
                        sc.wait_ge(gt_ps.sem, n - 1)
                    th_ready.by(nc.scalar.activation(th[:, n % 2, :], m.z_row[:, i, :], ACT.Tanh, scale=0.125))
                    if n == TILES - 1:
                        copy_gated(n - 1)
                    sc.wait_ge(y2.sem, n + 1)
                    ss_ready.by(nc.scalar.activation(sq[:, :], y[:, n % 2, :, :].rearrange("p h d -> p (h d)"),
                                                     ACT.Square, accum_out=ss[:, n:n + 1]))
                    if n > LAG:
                        normalise(n - LAG - 1)
                normalise(TILES - LAG - 1)
                copy_gated(TILES - 1)
                for n in range(TILES - LAG, TILES):
                    normalise(n)

            @block.vector
            def _(v):
                for b in range(BATCH):
                    zero.by(nc.vector.memset(st[:, b, 0, :, :], 0.0))
                v.wait_ge(m.late_in.sem, 16 * 2)
                for c in range(4):
                    wn.by(nc.vector.tensor_scalar(m.w_out[:, c, :], m.w_out[:, c, :], m.norm_w[:, c:c + 1], None,
                                                  ALU.mult))

                def tail(n):
                    i = tiles[n]
                    v.wait_ge(out_ps.sem, n + 1)
                    v.wait_ge(rms_ready.sem, n + 1)
                    if n >= 2:
                        v.wait_ge(resid.sem, n - 1)
                    dve.then_wait(v, nc.vector.scalar_tensor_tensor(r[:, n % 2, :], m.ps[:, 7, 0:DM],
                                                                    rms[:, n:n + 1], m.x[:, i, :], ALU.mult, ALU.add))
                    dve.then_wait(v, nc.vector.bn_stats(bs[:, n % 2, :], r[:, n % 2, :]))
                    mv_ready.by(nc.vector.bn_aggr(mv[:, n % 2, :], bs[:, n % 2, :]))

                def carry(n):
                    i = tiles[n]
                    b = i // TPH
                    if n == 0:
                        v.wait_ge(decay_sb.sem, G)
                        v.wait_ge(zero.sem, BATCH)
                    for g in range(G):
                        if (n, g) not in steps:
                            continue
                        c, k = G * (i % TPH) + g, before(n, g)
                        if k:
                            v.wait_ge(carried.sem, k)
                        if n >= 4:
                            v.wait_ge(inter_ps.sem, n - 3)
                        dve.then_wait(v, nc.vector.tensor_tensor(
                            tmp[:, k % 2, :, :], st[:, b, c % RING, :, :],
                            spread(whole[:, g, i, :], 2, PDIM), ALU.mult))
                        v.wait_ge(new_ps.sem, k + 1)
                        carried.by(nc.vector.tensor_tensor(
                            st[:, b, (c + 1) % RING, :, :], tmp[:, k % 2, :, :],
                            m.ps[:, NEW[k % len(NEW)], :].rearrange("p (h d) -> p h d", d=PDIM), ALU.add))

                carry(0)
                for n, i in enumerate(tiles):
                    if n + 1 < TILES:
                        carry(n + 1)
                    v.wait_ge(th_ready.sem, n + 1)
                    if n >= 2:
                        v.wait_ge(gated.sem, n - 1)
                    zs_ready.by(nc.vector.scalar_tensor_tensor(zs[:, n % 2, :], th[:, n % 2, :], 1.0, m.z_row[:, i, :],
                                                               ALU.add, ALU.mult))
                    if n == TILES - 1:
                        v.wait_ge(y2.sem, n - 1)
                        dve.then_wait(v, nc.vector.tensor_tensor(
                            xd[:, n % 2, :, :], m.x_row[:, i, :].rearrange("p (h d) -> p h d", d=PDIM),
                            spread(m.d_row[:, :], 2, PDIM), ALU.mult))
                        xd4 = xd[:, n % 2, :, :].rearrange("p (c h) d -> p c (h d)", c=4)
                        xd_ready.by(nc.vector.tensor_tensor(xd4, xd4, m.xc[:, 0:4, P * i:P * (i + 1)], ALU.add))
                    v.wait_ge(inter_ps.sem, n + 1)
                    if n >= 2:
                        v.wait_ge(ss_ready.sem, n - 1)
                    y1.by(nc.vector.tensor_tensor(y[:, n % 2, :, :],
                                                  m.ps[:, INTER_BANK + n % 2, :].rearrange("p (h d) -> p h d", d=PDIM),
                                                  spread(m.since_row[:, i, :], 2, PDIM), ALU.mult))
                    if n >= LAG:
                        tail(n - LAG)
                for n in range(TILES - LAG, TILES):
                    tail(n)

            @block.gpsimd
            def _(pool):
                pool.wait_ge(m.const_in.sem, 16 * 4)

                def row_scales(n):
                    pool.wait_ge(ss_ready.sem, n + 1)
                    pl.then_wait(pool, nc.gpsimd.tensor_scalar(rms[:, n:n + 1], ss[:, n:n + 1], 64.0 / INTER, 64e-5,
                                                               ALU.mult, ALU.add))
                    rms_ready.by(nc.gpsimd.tensor_tensor(rms[:, n:n + 1], rms[:, n:n + 1], m.half[:, :],
                                                               ALU.pow))

                def ln_scale(n):
                    pool.wait_ge(mv_ready.sem, n + 1)
                    pl.then_wait(pool, nc.gpsimd.tensor_scalar(rs[:, n % 2, :], mv[:, n % 2, 1:2], LN_EPS, None,
                                                               ALU.add))
                    pl.then_wait(pool, nc.gpsimd.tensor_tensor(rs[:, n % 2, :], rs[:, n % 2, :], m.half[:, :],
                                                               ALU.pow))
                    rs_ready.by(nc.gpsimd.tensor_scalar(shift[:, n % 2, :], mv[:, n % 2, 0:1], rs[:, n % 2, 0:1],
                                                        -1.0, ALU.mult, ALU.mult))

                for n in range(TILES):
                    if n < TILES - 1:
                        i = tiles[n]
                        pl.then_wait(pool, nc.gpsimd.tensor_tensor(
                            xd[:, n % 2, :, :], m.x_row[:, i, :].rearrange("p (h d) -> p h d", d=PDIM),
                            spread(m.d_row[:, :], 2, PDIM), ALU.mult))
                        xd4 = xd[:, n % 2, :, :].rearrange("p (c h) d -> p c (h d)", c=4)
                        pl.then_wait(pool, nc.gpsimd.tensor_tensor(xd4, xd4, m.xc[:, 0:4, P * i:P * (i + 1)],
                                                                   ALU.add))
                    else:
                        pool.wait_ge(xd_ready.sem, 1)
                    pool.wait_ge(y1.sem, n + 1)
                    y2.then_wait(pool, nc.gpsimd.tensor_tensor(y[:, n % 2, :, :], y[:, n % 2, :, :], xd[:, n % 2, :, :],
                                                               ALU.add))
                    pool.wait_ge(zs_ready.sem, n + 1)
                    gated.by(nc.gpsimd.tensor_tensor(th[:, n % 2, :], y[:, n % 2, :, :].rearrange("p h d -> p (h d)"),
                                                     zs[:, n % 2, :], ALU.mult))
                    row_scales(n)
                    if n >= LAG:
                        ln_scale(n - LAG)
                for n in range(TILES - LAG, TILES):
                    ln_scale(n)


def ln_stats(nc, v, work, n, step, mv_ready):
    step.then_wait(v, nc.vector.bn_stats(work.bs[:, n % 2, :], work.r[:, n % 2, :]))
    mv_ready.by(nc.vector.bn_aggr(work.mv[:, n % 2, :], work.bs[:, n % 2, :]))


def ln_scale(nc, pool, m, work, n, step, mv_ready, rs_ready):
    pool.wait_ge(mv_ready.sem, n + 1)
    step.then_wait(pool, nc.gpsimd.tensor_scalar(work.rs[:, n % 2, :], work.mv[:, n % 2, 1:2], LN_EPS, None, ALU.add))
    rs_ready.by(nc.gpsimd.tensor_tensor(work.rs[:, n % 2, :], work.rs[:, n % 2, :], m.half[:, :], ALU.pow))


def ln_apply(nc, v, m, work, n, i, rs_ready, x_ready):
    v.wait_ge(rs_ready.sem, n + 1)
    x_ready.by(nc.vector.tensor_scalar(m.x[:, i, :], work.r[:, n % 2, :], work.mv[:, n % 2, 0:1],
                                       work.rs[:, n % 2, 0:1], ALU.subtract, ALU.mult))


def ln_work(sb):
    w = Memory()
    w.r, w.bs, w.mv, w.rs = sb("r", [P, 2, DM]), sb("bs", [P, 2, 6]), sb("mv", [P, 2, 2]), sb("rs", [P, 2, 1])
    return w


def load_lora(nc, m, a, sp):
    sp.dma_start(m.lw_a[:, :, :], a["L0_ffn_A"].rearrange("e r d -> (e r) d").rearrange("(j p) d -> p j d", p=P)
                 ).then_inc(m.lora_in.sem, 16)
    for h in range(KD):
        sp.dma_start(m.lw_b[:, h, :, :], a["L0_ffn_Bw"][:, P * h:P * (h + 1), :].rearrange("e p r -> p e r")
                     ).then_inc(m.lora_in.sem, 16)
    sp.dma_start(m.lw_g[:, :], a["L0_ffn_Wg"]).then_inc(m.lora_in.sem, 16)
    sp.dma_start(m.first8[:, :], a["c_first8"]).then_inc(m.lora_in.sem, 16)


def lora_experts(nc, m, a):
    with ExitStack() as ctx:
        sig = lambda name: Signal(ctx, nc, "lora_" + name)
        sb = lambda name, shape: ctx.enter_context(nc.sbuf_tensor("lora_" + name, shape, F32))
        aT = sb("aT", [P, KD, LE * LR])
        bT = sb("bT", [P, LE * LR // P, DM])
        gT = sb("gT", [P, KD, LE])
        lg = sb("lg", [P, TILES, LE])
        ex = sb("ex", [P, TILES, LE])
        hot = sb("hot", [P, TILES, LE])
        mx = sb("mx", [P, TILES])
        sm = sb("sm", [P, TILES])
        hm = sb("hm", [P, 2, LE, LR])
        hT = sb("hT", [P, 2, LE * LR])
        work = ln_work(sb)
        xt_ps, xt_sb, wt_ps, wt_sb = sig("xt_ps"), sig("xt_sb"), sig("wt_ps"), sig("wt_sb")
        lg_ps, ex_in, ex_out, h_ps, h_sb = (sig(n) for n in ("lg_ps", "ex_in", "ex_out", "h_ps", "h_sb"))
        hT_ps, hT_sb, y_ps, dve, pl = (sig(n) for n in ("hT_ps", "hT_sb", "y_ps", "dve4", "pool4"))
        mv_ready, rs_ready, x_ready = sig("mv_ready"), sig("rs_ready"), sig("x_ready")
        NJ = LE * LR // P
        with nc.Block() as block:
            @block.sync
            def _(sp):
                load_query_weights(nc, m, a, sp)

            @block.tensor
            def _(pe):
                pe.wait_ge(m.lora_in.sem, 16 * 5)
                for k in range(KD):
                    last = nc.tensor.transpose(m.ps[:, 4, LE * k:LE * (k + 1)], m.lw_g[:, P * k:P * (k + 1)],
                                               m.ident[0:LE, 0:LE])
                wt_ps.by(last)
                for k in range(KD):
                    for j in range(NJ):
                        last = nc.tensor.transpose(m.ps[:, 5 + k, P * j:P * (j + 1)], m.lw_a[:, j, P * k:P * (k + 1)],
                                                   m.ident[:, :])
                    wt_ps.by(last)
                for jj in range(2):
                    if jj == 1:
                        pe.wait_ge(wt_sb.sem, 1)
                    for j in (2 * jj, 2 * jj + 1):
                        for h in range(KD):
                            last = nc.tensor.transpose(
                                m.ps[:, 7 if jj == 0 else 4, DM * (j % 2) + P * h:DM * (j % 2) + P * (h + 1)],
                                m.lw_b[:, h, 2 * j:2 * j + 2, :].rearrange("p e r -> p (e r)"), m.ident[:, :])
                    wt_ps.by(last)
                transpose_rows(pe, nc, m, 0, lambda i: None, xt_ps)
                pe.wait_ge(xt_sb.sem, 4)
                pe.wait_ge(wt_sb.sem, 5)
                for i in range(TILES):
                    for k in range(KD):
                        last = nc.tensor.matmul(m.ps[:, 0, LE * i:LE * (i + 1)], m.xT[:, k, P * i:P * (i + 1)],
                                                gT[:, k, :], start=k == 0, stop=k == KD - 1)
                lg_ps.by(last)

                def turn(i):
                    pe.wait_ge(h_sb.sem, i + 1)
                    for j in range(NJ):
                        last = nc.tensor.transpose(m.ps[:, 1 + i % 2, P * j:P * (j + 1)],
                                                   hm[:, i % 2, 2 * j:2 * j + 2, :].rearrange("p e r -> p (e r)"),
                                                   m.ident[:, :])
                    hT_ps.by(last)

                def down(i):
                    pe.wait_ge(hT_sb.sem, i + 1)
                    if i >= 2:
                        pe.wait_ge(mv_ready.sem, i - 1)
                    for j in range(NJ):
                        last = nc.tensor.matmul(m.ps[:, 3 + 4 * (i % 2), 0:DM], hT[:, i % 2, P * j:P * (j + 1)],
                                                bT[:, j, :], start=j == 0, stop=j == NJ - 1)
                    y_ps.by(last)

                for i in range(TILES):
                    if i >= 2:
                        pe.wait_ge(h_sb.sem, i - 1)
                    for k in range(KD):
                        last = nc.tensor.matmul(m.ps[:, 5 + i % 2, :], m.xT[:, k, P * i:P * (i + 1)], aT[:, k, :],
                                                start=k == 0, stop=k == KD - 1)
                    h_ps.by(last)
                    if i >= 1:
                        turn(i - 1)
                    if i >= 2:
                        down(i - 2)
                turn(TILES - 1)
                down(TILES - 2)
                down(TILES - 1)

            @block.scalar
            def _(sc):
                for n, (bank, dst) in enumerate(((4, gT[:, :, :].rearrange("p k e -> p (k e)")),
                                                 (5, aT[:, 0, :]), (6, aT[:, 1, :]),
                                                 (7, bT[:, 0:2, :].rearrange("p j o -> p (j o)")),
                                                 (4, bT[:, 2:4, :].rearrange("p j o -> p (j o)")))):
                    sc.wait_ge(wt_ps.sem, n + 1)
                    wt_sb.by(nc.scalar.copy(dst, m.ps[:, bank, 0:dst.shape[1]]))
                sc.wait_ge(ex_in.sem, 1)
                ex_out.by(nc.scalar.activation(ex[:, :, :], lg[:, :, :], ACT.Exp))
                for i in range(TILES):
                    sc.wait_ge(hT_ps.sem, i + 1)
                    if i >= 2:
                        sc.wait_ge(y_ps.sem, i - 1)
                    hT_sb.by(nc.scalar.copy(hT[:, i % 2, :], m.ps[:, 1 + i % 2, :]))

            @block.vector
            def _(v):
                copy_transposed(v, nc.vector.tensor_copy, m, 0, xt_ps, xt_sb)
                v.wait_ge(lg_ps.sem, 1)
                lps = m.ps[:, 0, 0:TILES * LE].rearrange("p (i e) -> p i e", e=LE)
                dve.then_wait(v, nc.vector.tensor_reduce(mx[:, :], lps, AX.X, ALU.max))
                ex_in.then_wait(v, nc.vector.tensor_tensor(lg[:, :, :], lps, spread(mx[:, :], 2, LE), ALU.subtract))
                dve.then_wait(v, nc.vector.tensor_scalar(hot[:, :, :], lg[:, :, :], 0.0, None, ALU.is_equal))
                dve.then_wait(v, nc.vector.tensor_tensor(hot[:, :, :], hot[:, :, :], spread(m.first8[:, :], 1, TILES),
                                                         ALU.mult))
                dve.then_wait(v, nc.vector.tensor_reduce(mx[:, :], hot[:, :, :], AX.X, ALU.max))
                dve.then_wait(v, nc.vector.tensor_tensor(hot[:, :, :], hot[:, :, :], spread(mx[:, :], 2, LE),
                                                         ALU.is_equal))
                v.wait_ge(ex_out.sem, 1)
                dve.then_wait(v, nc.vector.tensor_reduce(sm[:, :], ex[:, :, :], AX.X, ALU.add))
                dve.then_wait(v, nc.vector.reciprocal(sm[:, :], sm[:, :]))
                dve.then_wait(v, nc.vector.scalar_tensor_tensor(hot[:, :, :], hot[:, :, :], LSCALE,
                                                                spread(sm[:, :], 2, LE), ALU.mult, ALU.mult))

                def tail(i):
                    v.wait_ge(y_ps.sem, i + 1)
                    if i >= 2:
                        v.wait_ge(x_ready.sem, i - 1)
                    dve.then_wait(v, nc.vector.tensor_tensor(work.r[:, i % 2, :], m.ps[:, 3 + 4 * (i % 2), 0:DM],
                                                             m.x[:, i, :], ALU.add))
                    ln_stats(nc, v, work, i, dve, mv_ready)

                for i in range(TILES):
                    v.wait_ge(h_ps.sem, i + 1)
                    if i >= 2:
                        v.wait_ge(hT_ps.sem, i - 1)
                    h_sb.by(nc.vector.tensor_tensor(hm[:, i % 2, :, :],
                                                    m.ps[:, 5 + i % 2, :].rearrange("p (e r) -> p e r", r=LR),
                                                    spread(hot[:, i, :], 2, LR), ALU.mult))
                    if i >= 3:
                        ln_apply(nc, v, m, work, i - 3, i - 3, rs_ready, x_ready)
                    if i >= 2:
                        tail(i - 2)
                for i in (TILES - 2, TILES - 1):
                    ln_apply(nc, v, m, work, i - 1, i - 1, rs_ready, x_ready)
                    tail(i)
                ln_apply(nc, v, m, work, TILES - 1, TILES - 1, rs_ready, x_ready)

            @block.gpsimd
            def _(pool):
                for i in range(TILES):
                    ln_scale(nc, pool, m, work, i, pl, mv_ready, rs_ready)


def load_query_weights(nc, m, a, sp):
    sp.dma_start(m.w_down[:, :, :], k_tiles(a["L1_attn_w_down"])).then_inc(m.wq_in.sem, 16)
    sp.dma_start(m.b_down[:, :], a["L1_attn_b_down"].unsqueeze(1), allow_slow_non_contiguous=True
                 ).then_inc(m.wq_in.sem, 16)
    sp.dma_start(m.w_q[:, :, :], k_tiles(a["L1_attn_w_q"])).then_inc(m.wq_in.sem, 16)


def load_qkv(nc, m, a, sp):
    for k, name in enumerate(("L1_attn_qn_w", "L1_attn_kn_w")):
        sp.dma_start(m.norm_qk[:, k, :], a[name].partition_broadcast(P)).then_inc(m.tables_in.sem, 16)
    sp.dma_start(m.sin_row[:, :, :], a["c_sin"]).then_inc(m.tables_in.sem, 16)
    sp.dma_start(m.cos_row[:, :, :], a["c_cos"]).then_inc(m.tables_in.sem, 16)
    sp.dma_start(m.w_up[:, :], a["L1_attn_w_up"]).then_inc(m.w_up_in.sem, 16)
    sp.dma_start(m.b_up[:, :], a["L1_attn_b_up"].partition_broadcast(P)).then_inc(m.biases_in.sem, 16)
    sp.dma_start(m.b_q[:, :], a["L1_attn_b_q"].partition_broadcast(P)).then_inc(m.biases_in.sem, 16)
    sp.dma_start(m.dist, a["c_dist"]).then_inc(m.dist_in.sem, 16)


class Selection:

    def __init__(self, sig, first, s, top, later, not_self):
        self.first, self.s, self.top, self.later, self.not_self = first, s, top, later, not_self
        self.masks, self.s_ps, self.s_sb, self.kept, self.s_turned, self.biased, self.dve = (sig(n) for n in (
            "masks", "sel_ps", "sel_sb", "kept", "sel_turned", "sel_biased", "sel_dve"))

    def buffer(self, i):
        j = i % TPH
        return self.s[:, i % 2, 0:P * (j + 1)], self.s[:, i % 2, P * j:P * (j + 1)]


def form_masks(nc, pool, q):
    q.masks.by(nc.gpsimd.memset(q.later, 0.0))
    q.masks.then_wait(pool, nc.gpsimd.memset(q.not_self, 1.0))
    q.masks.by(nc.gpsimd.affine_select(q.later, q.later, [[-1, P]], ALU.is_ge, LATER, base=0, channel_multiplier=1))
    q.masks.by(nc.gpsimd.affine_select(q.not_self, q.not_self, [[-1, P]], ALU.not_equal, 0.0, base=0,
                                       channel_multiplier=1))


def select_scores(nc, pe, m, q, i):
    b, j = i // TPH, i % TPH
    if i > q.first:
        pe.wait_ge(q.biased.sem, i - q.first)
    q.s_ps.by(nc.tensor.matmul(m.ps[:, 7, 0:P * (j + 1)], m.qT[0:SEL_DIM, 0, P * i:P * (i + 1)],
                               m.kT[0:SEL_DIM, 0, SEQ * b:SEQ * b + P * (j + 1)], start=True, stop=True))


def select_copy(nc, sc, m, q, i):
    n = i - q.first
    sc.wait_ge(q.s_ps.sem, n + 1)
    if n >= 2:
        sc.wait_ge(q.s_turned.sem, n - 1)
    s, own = q.buffer(i)
    q.s_sb.by(nc.scalar.copy(s, m.ps[:, 7, 0:s.shape[1]]))


def select_rounds(nc, v, q, i, lo, hi):
    s, own = q.buffer(i)
    if lo == 0:
        v.wait_ge(q.s_sb.sem, i - q.first + 1)
        v.wait_ge(q.masks.sem, 4)
        q.dve.then_wait(v, nc.vector.tensor_tensor(own, own, q.later, ALU.add))
    for _ in range(lo, hi):
        q.dve.then_wait(v, nc.vector.max(q.top, s))
        q.dve.then_wait(v, nc.vector.match_replace(s, q.top, s, TAKEN))
    if hi == SEL_TOPK // 8:
        q.dve.then_wait(v, nc.vector.tensor_scalar(s, s, TAKEN / 2, None, ALU.is_gt))
        q.kept.by(nc.vector.tensor_tensor(own, own, q.not_self, ALU.mult))


def select_turn(nc, pe, m, q, i):
    pe.wait_ge(q.kept.sem, i - q.first + 1)
    for k in range(i % TPH + 1):
        last = nc.tensor.transpose(m.ps[:, 7, P * k:P * (k + 1)], q.s[:, i % 2, P * k:P * (k + 1)], m.ident[:, :])
    q.s_turned.by(last)


def select_bias(nc, v, m, q, i):
    b, j = i // TPH, i % TPH
    v.wait_ge(q.s_turned.sem, i - q.first + 1)
    for k in range(j + 1):
        c = KEY_COL[k] + P * (j - k)
        last = nc.vector.scalar_tensor_tensor(m.bias[b][:, c:c + P], m.ps[:, 7, P * k:P * (k + 1)], FAR,
                                              m.dist[:, c:c + P], ALU.mult, ALU.add)
    q.biased.by(last)


def prepare_attention(nc, m, a):
    with ExitStack() as ctx:
        sig = lambda name: Signal(ctx, nc, "qkv_" + name)
        sb = lambda name, shape: ctx.enter_context(nc.sbuf_tensor("qkv_" + name, shape, F32))
        latT = sb("latT", [LATENT, NT])
        cw = sb("cw", [P, 2, TPH, HD])
        sw = sb("sw", [P, 2, TPH, HD])
        qb = sb("qb", [P, 2, QKH, HD])
        t1 = sb("t1", [P, QKH, HD])
        sq = m.cos_row
        ss = sb("ss5", [P, 2, QKH])
        half20 = sb("half20", [P, QKH])
        s = sb("s", [P, 2, SEQ])
        top = sb("top", [P, 8])
        xt_ps, xt_sb, lat_ps, lat_sb, tab = (sig(n) for n in ("xt_ps", "xt_sb", "lat_ps", "lat_sb", "tab"))
        q_ps, kv_ps, qb_ready, v_ready, squared = (sig(n) for n in ("q_ps", "kv_ps", "qb_ready", "v_ready",
                                                                   "squared"))
        rs_ready, cos_ready, sin_ready, rot, normed = (sig(n) for n in ("rs_ready", "cos_ready", "sin_ready", "rot",
                                                                       "normed"))
        turned, qk_sb, pl, ones = (sig(n) for n in ("turned", "qk_sb", "pool5", "ones"))
        NG = QKH // 4
        PARTS = (((0, 0, 8),), ((0, 8, 16), (1, 16, 20)))
        KEYS_ON_DVE = 4
        key_rot = sig("key_rot")
        TURN, SELECT = 2, 5
        TWO_BANKS = NG * (SELECT - TURN)
        turn_bank = lambda k: 6 + k % 2 if k < TWO_BANKS else 6
        KEYS = NG - 1
        q = Selection(sig, 0, s, top[:, :], m.sin_row[:, 0, :], m.sin_row[:, 1, :])
        with nc.Block() as block:
            @block.sync
            def _(sp):
                load_qkv(nc, m, a, sp)

            @block.tensor
            def _(pe):
                transpose_rows(pe, nc, m, 0, lambda i: None, xt_ps)
                pe.wait_ge(m.wq_in.sem, 48)
                pe.wait_ge(xt_sb.sem, 4)
                for h in range(HALVES):
                    for k in range(KD):
                        last = nc.tensor.matmul(m.ps[0:LATENT, 4 + h, :], m.w_down[:, k, :],
                                                m.xT[:, k, 512 * h:512 * (h + 1)], start=k == 0, stop=k == KD - 1)
                    lat_ps.by(last)
                pe.wait_ge(lat_sb.sem, 2)
                pe.wait_ge(m.w_up_in.sem, 16)

                def project_kv(i):
                    if i >= 1:
                        pe.wait_ge(qb_ready.sem, 3 * i - 2)
                        pe.wait_ge(v_ready.sem, i)
                    for c in range(2):
                        last = nc.tensor.matmul(m.ps[:, 4 + c, :], latT[:, P * i:P * (i + 1)],
                                                m.w_up[:, 512 * c:512 * (c + 1)], start=True, stop=True)
                    kv_ps.by(last)

                def project_q(i, c):
                    if i >= 1 and c % 2 == 0:
                        pe.wait_ge(qb_ready.sem, 3 * i - 1 + c // 2)
                    for k in range(KD):
                        last = nc.tensor.matmul(m.ps[:, c, :], m.xT[:, k, P * i:P * (i + 1)],
                                                m.w_q[:, k, 512 * c:512 * (c + 1)], start=k == 0, stop=k == KD - 1)
                    if c % 2 == 1:
                        q_ps.by(last)

                def turn(i, g):
                    if g == KEYS:
                        pe.wait_ge(normed.sem, i + 1)
                    k = turned.n
                    behind = 2 if k < TWO_BANKS else 1
                    if k >= behind:
                        pe.wait_ge(qk_sb.sem, k - behind + 1)
                    for j in range(4):
                        last = nc.tensor.transpose(m.ps[:, turn_bank(k), P * j:P * (j + 1)], qb[:, i % 2, 4 * g + j, :],
                                                   m.ident[:, :])
                    turned.by(last)

                for i in range(TILES + TURN):
                    now, turning = i < TILES, i >= TURN
                    n = i - SELECT
                    if now:
                        project_kv(i)
                    if 0 <= n < TPH:
                        pe.wait_ge(qk_sb.sem, max(NG * (n + 1), TWO_BANKS))
                        select_scores(nc, pe, m, q, n)
                    if now:
                        project_q(i, 0)
                        project_q(i, 1)
                    if turning:
                        for g in (KEYS, 0, 1):
                            turn(i - TURN, g)
                    if now:
                        project_q(i, 2)
                    if turning:
                        turn(i - TURN, 2)
                    if 0 <= n < TPH - 1:
                        select_turn(nc, pe, m, q, n)
                    if now:
                        project_q(i, 3)
                    if turning:
                        turn(i - TURN, 3)
                select_turn(nc, pe, m, q, TPH - 1)

            @block.scalar
            def _(sc):
                sc.wait_ge(m.wq_in.sem, 48)
                for h in range(HALVES):
                    sc.wait_ge(lat_ps.sem, h + 1)
                    lat_sb.by(nc.scalar.activation(latT[:, 512 * h:512 * (h + 1)], m.ps[0:LATENT, 4 + h, :],
                                                   ACT.Identity, bias=m.b_down[:, 0:1]))

                def copy_turned(i, g):
                    k = qk_sb.n
                    sc.wait_ge(turned.sem, k + 1)
                    dst = (m.kT[:, :, P * i:P * (i + 1)] if g == KEYS else
                           m.qT[:, 4 * g:4 * g + 4, P * i:P * (i + 1)])
                    qk_sb.by(nc.scalar.copy(dst, m.ps[:, turn_bank(k), :].rearrange("p (j t) -> p j t", t=P)))

                def square(i, heads, added):
                    sc.wait_ge(qb_ready.sem, 3 * i + added)
                    for h in heads:
                        if squared.n >= TPH:
                            sc.wait_ge(squared.sem, squared.n - TPH + 1)
                        squared.by(nc.scalar.activation(sq[:, squared.n % TPH, :], qb[:, i % 2, h, :], ACT.Square,
                                                        accum_out=ss[:, i % 2, h:h + 1]))

                for i in range(TILES + TURN):
                    turning = i >= TURN
                    if 0 <= i - SELECT < TPH:
                        select_copy(nc, sc, m, q, i - SELECT)
                    if turning:
                        for g in (KEYS, 0, 1):
                            copy_turned(i - TURN, g)
                    if turning:
                        copy_turned(i - TURN, 2)
                    if i < TILES:
                        if turning:
                            sc.wait_ge(normed.sem, i - TURN + 1)
                        square(i, range(16, 20), 1)
                        square(i, range(0, 8), 2)
                    if turning:
                        copy_turned(i - TURN, 3)
                    if i < TILES:
                        square(i, range(8, 16), 3)

            @block.vector
            def _(v):
                copy_transposed(v, nc.vector.tensor_copy, m, 0, xt_ps, xt_sb)
                v.wait_ge(m.tables_in.sem, 64)
                for n in range(2):
                    nc.vector.tensor_tensor(cw[:, n, :, :], m.cos_row[:, :, :], spread(m.norm_qk[:, n, :], 1, TPH),
                                            ALU.mult)
                    for o in range(2):
                        last = nc.vector.tensor_tensor(sw[:, n, :, o::2], m.sin_row[:, :, o::2],
                                                       spread(m.norm_qk[:, n, 1 - o::2], 1, TPH), ALU.mult)
                    tab.by(last)
                v.wait_ge(tab.sem, 2)
                v.wait_ge(m.biases_in.sem, 32)

                def turned_before(i, groups):
                    if i >= 2:
                        v.wait_ge(turned.sem, NG * (i - 2) + groups)

                def add_kv(i):
                    turned_before(i, 1)
                    v.wait_ge(kv_ps.sem, i + 1)
                    qb_ready.by(nc.vector.tensor_tensor(qb[:, i % 2, 16:20, :].rearrange("p h d -> p (h d)"),
                                                        m.ps[:, 4, :], m.b_up[:, 0:512], ALU.add))
                    v_ready.by(nc.vector.tensor_tensor(m.v[:, i, :, 0:HD],
                                                       m.ps[:, 5, :].rearrange("p (g d) -> p g d", d=HD),
                                                       m.b_up[:, 512:1024].rearrange("p (g d) -> p g d", d=HD),
                                                       ALU.add))

                def add_q(i, half):
                    turned_before(i, 3 + 2 * half)
                    v.wait_ge(q_ps.sem, 2 * i + half + 1)
                    qb_ready.by(nc.vector.tensor_tensor(
                        qb[:, i % 2, 8 * half:8 * half + 8, :].rearrange("p h d -> p (h d)"),
                        m.ps[:, 2 * half:2 * half + 2, :].rearrange("p b n -> p (b n)"),
                        m.b_q[:, 1024 * half:1024 * (half + 1)], ALU.add))

                def sin_part(i, part):
                    b, j = qb[:, i % 2, :, :], i % TPH
                    v.wait_ge(qb_ready.sem, 3 * i + 2 + part)
                    if i >= 1:
                        v.wait_ge(rot.sem, 2 * i - 1 + part)
                    for n, h0, h1 in PARTS[part]:
                        for o in range(2):
                            last = nc.vector.tensor_tensor(t1[:, h0:h1, o::2], b[:, h0:h1, 1 - o::2],
                                                           spread(sw[:, n, j, o::2], 1, h1 - h0), ALU.mult)
                    sin_ready.by(last)

                def rotate_keys(i):
                    b, t = qb[:, i % 2, 16:20, :], t1[:, 16:20, :]
                    v.wait_ge(sin_ready.sem, 2 * i + 2)
                    v.wait_ge(squared.sem, QKH * i + 4)
                    key_rot.then_wait(v, nc.vector.tensor_tensor(b, b, spread(cw[:, 1, i % TPH, :], 1, 4), ALU.mult))
                    key_rot.then_wait(v, nc.vector.tensor_tensor(b, b, t, ALU.add))

                def normalise(i):
                    v.wait_ge(rot.sem, 2 * i + 2)
                    v.wait_ge(rs_ready.sem, i + 1)
                    normed.by(nc.vector.tensor_tensor(qb[:, i % 2, :, :], qb[:, i % 2, :, :],
                                                      spread(ss[:, i % 2, :], 2, HD), ALU.mult))

                for i in range(TILES):
                    n = i - SELECT
                    add_kv(i)
                    add_q(i, 0)
                    sin_part(i, 0)
                    add_q(i, 1)
                    sin_part(i, 1)
                    if i < KEYS_ON_DVE:
                        rotate_keys(i)
                    if n == 0:
                        v.wait_ge(m.dist_in.sem, 16)
                    if 0 <= n < TPH:
                        select_bias(nc, v, m, q, n)
                    if i >= 1:
                        normalise(i - 1)
                    if 0 <= n + 1 < TPH:
                        select_rounds(nc, v, q, n + 1, 0, SEL_TOPK // 8)
                normalise(TILES - 1)
                select_bias(nc, v, m, q, TPH - 1)

            @block.gpsimd
            def _(pool):
                ones.by(nc.gpsimd.memset(m.v[:, :, :, HD:HD + 1], 1.0))
                ones.then_wait(pool, nc.gpsimd.memset(half20[:, :], -0.5))
                pool.wait_ge(tab.sem, 2)
                form_masks(nc, pool, q)
                for i in range(TILES):
                    j = i % TPH
                    b = qb[:, i % 2, :, :]
                    for part, steps in enumerate(PARTS):
                        if i < KEYS_ON_DVE:
                            steps = steps[:1]
                        pool.wait_ge(sin_ready.sem, 2 * i + part + 1)
                        pool.wait_ge(squared.sem, QKH * i + (12 if part == 0 else QKH))
                        for of_k, h0, h1 in steps:
                            last = nc.gpsimd.tensor_tensor(b[:, h0:h1, :], b[:, h0:h1, :],
                                                           spread(cw[:, of_k, j, :], 1, h1 - h0), ALU.mult)
                        cos_ready.then_wait(pool, last)
                        h0, h1 = steps[0][1], steps[-1][2]
                        rot.by(nc.gpsimd.tensor_tensor(b[:, h0:h1, :], b[:, h0:h1, :], t1[:, h0:h1, :], ALU.add))
                    pl.then_wait(pool, nc.gpsimd.tensor_scalar(ss[:, i % 2, :], ss[:, i % 2, :], 1.0 / HD, 1e-6,
                                                               ALU.mult, ALU.add))
                    rs_ready.by(nc.gpsimd.tensor_tensor(ss[:, i % 2, :], ss[:, i % 2, :], half20[:, :], ALU.pow))


def load_attention(nc, m, a, sp):
    sp.dma_start(m.gate_b[:, :], a["L1_attn_gate_b"].rearrange("h e -> e h"), allow_slow_non_contiguous=True
                 ).then_inc(m.attn_in.sem, 16)
    for h in range(2):
        sp.dma_start(m.gate_w[:, 8 * h:8 * h + 8, :],
                     a["L1_attn_gate_w"][8 * h:8 * h + 8, :, :].rearrange("h d e -> d h e")).then_inc(m.attn_in.sem, 16)
    sp.dma_start(m.w_o[:, :, :], a["L1_attn_w_o"].rearrange("(h d) n -> d h n", d=P)).then_inc(m.wo_in.sem, 16)
    sp.dma_start(m.b_o[:, :], a["L1_attn_b_o"].partition_broadcast(P)).then_inc(m.wo_in.sem, 16)
ATTN_LOADS = 3


def attend(nc, m, a):
    with ExitStack() as ctx:
        sig = lambda name: Signal(ctx, nc, "att_" + name)
        sb = lambda name, shape: ctx.enter_context(nc.sbuf_tensor("att_" + name, shape, F32))
        rd = sb("rd", [P, 2, TPH])
        c = 0
        parts = []
        for n in (NCOL, NCOL, SEQ, SEQ, SEQ):
            parts.append(m.rows[:, c:c + 2 * n].rearrange("p (u n) -> p u n", u=2))
            c += 2 * n
        t, p, yn, yT, tg = parts
        yn = yn.rearrange("p u (j d) -> p u j d", d=HD)
        gb = sb("gb", [P, AH])
        top = sb("top", [P, 8])
        late = Space(m.weights[:, 2 * NE * DM - 2 * SEQ - 2 * P:])
        q = Selection(sig, TPH, late.take(P, 2, SEQ), top[:, :], late.take(P, P), late.take(P, P))
        s_ps, capped, biased, p_ready, y_ps, y_sb = (sig(n) for n in ("s_ps", "capped", "biased", "p_ready", "y_ps",
                                                                     "y_sb"))
        yT_ps, yT_sb, g_ps, g_sb, z_ready, gb_ready, dve = (sig(n) for n in (
            "yT_ps", "yT_sb", "g_ps", "g_sb", "z_ready", "gb_ready", "dve7"))
        todo = [(b, h) for b in range(BATCH) for h in range(AH)]
        N = len(todo)
        flat = m.ps[:, 0:3, :].rearrange("p b n -> p (b n)")
        ROUNDS = [0, 3, 6, 8]
        TURN = len(ROUNDS) - 1

        def tile_step(n):
            return (TPH + n // (TURN + 1), n % (TURN + 1)) if n < TPH * (TURN + 1) else (None, -1)

        with nc.Block() as block:
            @block.sync
            def _(sp):
                load_attention(nc, m, a, sp)
                e = (2 * NE * DM - late.ap.shape[1]) // (2 * KD * EI)
                load_gate_up(nc, m, a, sp, slice(FIRST_EXPERTS.stop, e))
                sp.wait_ge(q.biased.sem, TPH)
                load_gate_up(nc, m, a, sp, slice(e, NE))

            @block.gpsimd
            def _(pool):
                form_masks(nc, pool, q)

            @block.tensor
            def _(pe):
                def scores(n):
                    b, h = todo[n]
                    if n >= 1:
                        pe.wait_ge(capped.sem, n)
                    for i in range(TPH):
                        w = SEQ - P * i
                        last = nc.tensor.matmul(flat[:, KEY_COL[i]:KEY_COL[i] + w],
                                                m.kT[:, h // KVG, SEQ * b + P * i:SEQ * b + P * (i + 1)],
                                                m.qT[:, h, SEQ * b + P * i:SEQ * (b + 1)], start=True, stop=True)
                    s_ps.by(last)

                def values(n):
                    b, h = todo[n]
                    pe.wait_ge(p_ready.sem, n + 1)
                    if n >= 1:
                        pe.wait_ge(y_sb.sem, n)
                    for j in range(TPH):
                        out = m.ps[:, 3, VW * j:VW * (j + 1)] if j < 3 else m.ps[:, 4, 0:VW]
                        for i in range(j + 1):
                            c = KEY_COL[i] + P * (j - i)
                            last = nc.tensor.matmul(out, p[:, n % 2, c:c + P], m.v[:, TPH * b + i, h // KVG, :],
                                                    start=i == 0, stop=i == j)
                    y_ps.by(last)

                def turn(n):
                    pe.wait_ge(y_sb.sem, n + 1)
                    if n >= 1:
                        pe.wait_ge(yT_sb.sem, n)
                    for j in range(TPH):
                        last = nc.tensor.transpose(m.ps[:, 5, P * j:P * (j + 1)], yn[:, n % 2, j, :], m.ident[:, :])
                    yT_ps.by(last)

                def gate(n):
                    if n == 0:
                        pe.wait_ge(m.attn_in.sem, 16 * ATTN_LOADS)
                    pe.wait_ge(yT_sb.sem, n + 1)
                    if n >= 1:
                        pe.wait_ge(g_sb.sem, n)
                    g_ps.by(nc.tensor.matmul(m.ps[:, 6, :], m.gate_w[:, todo[n][1], :], yT[:, n % 2, :], start=True,
                                             stop=True))

                scores(0)
                for n in range(N):
                    i, step = tile_step(n)
                    if step == 0:
                        select_scores(nc, pe, m, q, i)
                    if step == TURN:
                        select_turn(nc, pe, m, q, i)
                    if n + 1 < N:
                        scores(n + 1)
                    if n >= 1:
                        turn(n - 1)
                    values(n)
                    if n >= 1:
                        gate(n - 1)
                turn(N - 1)
                gate(N - 1)

            @block.scalar
            def _(sc):
                def cap(n):
                    sc.wait_ge(s_ps.sem, n + 1)
                    if n >= 2:
                        sc.wait_ge(p_ready.sem, n - 1)
                    capped.by(nc.scalar.activation(t[:, n % 2, :], flat[:, 0:NCOL], ACT.Tanh,
                                                   scale=1.0 / (HD ** 0.5 * SOFTCAP)))

                def gating(n):
                    if n == 0:
                        sc.wait_ge(gb_ready.sem, 1)
                    sc.wait_ge(yT_ps.sem, n + 1)
                    if n >= 2:
                        sc.wait_ge(z_ready.sem, n - 1)
                    yT_sb.by(nc.scalar.copy(yT[:, n % 2, :], m.ps[:, 5, :]))
                    sc.wait_ge(g_ps.sem, n + 1)
                    g_sb.by(nc.scalar.activation(tg[:, n % 2, :], m.ps[:, 6, :], ACT.Tanh,
                                                 bias=gb[:, todo[n][1]:todo[n][1] + 1]))

                cap(0)
                for n in range(N):
                    i, step = tile_step(n)
                    if step == 0:
                        select_copy(nc, sc, m, q, i)
                    sc.wait_ge(biased.sem, n + 1)
                    if n >= 2:
                        sc.wait_ge(y_ps.sem, n - 1)
                    p_ready.by(nc.scalar.activation(p[:, n % 2, :], t[:, n % 2, :], ACT.Exp, scale=SOFTCAP))
                    if n + 1 < N:
                        cap(n + 1)
                    if n >= 1:
                        gating(n - 1)
                gating(N - 1)

            def normalise(v, n):
                v.wait_ge(y_ps.sem, n + 1)
                if n >= 2:
                    v.wait_ge(yT_ps.sem, n - 1)
                y3 = m.ps[:, 3, 0:3 * VW].rearrange("p (j d) -> p j d", d=VW)
                nc.vector.reciprocal(rd[:, n % 2, 0:3], y3[:, :, HD])
                dve.then_wait(v, nc.vector.reciprocal(rd[:, n % 2, 3:4], m.ps[:, 4, HD:HD + 1]))
                nc.vector.scalar_tensor_tensor(yn[:, n % 2, 0:3, :], y3[:, :, 0:HD], 0.5,
                                               spread(rd[:, n % 2, 0:3], 2, HD), ALU.mult, ALU.mult)
                y_sb.by(nc.vector.tensor_scalar(yn[:, n % 2, 3, :], m.ps[:, 4, 0:HD], rd[:, n % 2, 3:4], 0.5,
                                                ALU.mult, ALU.mult))

            @block.vector
            def _(v):

                def finish(n):
                    b, h = todo[n]
                    v.wait_ge(g_sb.sem, n + 1)
                    z_ready.by(nc.vector.scalar_tensor_tensor(m.qT[:, h, SEQ * b:SEQ * (b + 1)], tg[:, n % 2, :], 1.0,
                                                              yT[:, n % 2, :], ALU.add, ALU.mult))

                for n in range(N):
                    b, h = todo[n]
                    v.wait_ge(capped.sem, n + 1)
                    if n == AH:
                        v.wait_ge(q.biased.sem, TPH)
                    if n == 1:
                        v.wait_ge(m.attn_in.sem, 16 * ATTN_LOADS)
                        gb_ready.by(nc.vector.tensor_scalar(gb[:, :], m.gate_b[:, :], 0.5, None, ALU.mult))
                    biased.by(nc.vector.scalar_tensor_tensor(t[:, n % 2, :], m.bias[b], SLOPE[h] / SOFTCAP,
                                                             t[:, n % 2, :], ALU.mult, ALU.add))
                    if n >= 1:
                        normalise(v, n - 1)
                    if n >= 2:
                        finish(n - 2)
                    i, step = tile_step(n)
                    if 0 <= step < TURN:
                        select_rounds(nc, v, q, i, ROUNDS[step], ROUNDS[step + 1])
                    if step == TURN:
                        select_bias(nc, v, m, q, i)
                normalise(v, N - 1)
                finish(N - 2)
                finish(N - 1)


def attention_output(nc, m, a):
    with ExitStack() as ctx:
        sig = lambda name: Signal(ctx, nc, "out_" + name)
        sb = lambda name, shape: ctx.enter_context(nc.sbuf_tensor("out_" + name, shape, F32))
        work = ln_work(sb)
        o_ps, mv_ready, rs_ready, x_ready, xb, dve, pl = (sig(n) for n in ("o_ps", "mv_ready", "rs_ready", "x_ready",
                                                                          "xb", "dve8", "pool8"))
        xt_ps, xt_sb, rw_ps, rw_sb = sig("xt_ps"), sig("xt_sb"), sig("rw_ps"), sig("rw_sb")
        LAG = 2
        with nc.Block() as block:
            @block.sync
            def _(sp):
                load_expert_weights(nc, m, a, sp)

            @block.tensor
            def _(pe):
                def turn(i):
                    pe.wait_ge(x_ready.sem, i + 1)
                    if i >= 2:
                        pe.wait_ge(xt_sb.sem, i - 1)
                    for k in range(KD):
                        last = nc.tensor.transpose(m.ps[:, 2 + i % 2, P * k:P * (k + 1)], m.x[:, i, P * k:P * (k + 1)],
                                                   m.ident[:, :])
                    xt_ps.by(last)

                def router_logits(i):
                    pe.wait_ge(xt_sb.sem, i + 1)
                    pe.wait_ge(rw_sb.sem, 1)
                    for k in range(KD):
                        nc.tensor.matmul(m.ps[:, 5, NE * i:NE * (i + 1)], m.xT[:, k, P * i:P * (i + 1)],
                                         m.early.router_T[:, k, :], start=k == 0, stop=k == KD - 1)

                pe.wait_ge(m.wo_in.sem, 32)
                for i in range(TILES):
                    if i >= 2:
                        pe.wait_ge(mv_ready.sem, i - 1)
                    for h in range(AH):
                        last = nc.tensor.matmul(m.ps[:, i % 2, 0:DM], m.qT[:, h, P * i:P * (i + 1)], m.w_o[:, h, :],
                                                start=h == 0, stop=h == AH - 1)
                    o_ps.by(last)
                    if i == LAG - 1:
                        pe.wait_ge(m.early_in.sem, 16 * EARLY_LOADS)
                        for k in range(KD):
                            last = nc.tensor.transpose(m.ps[:, 4, NE * k:NE * (k + 1)],
                                                       m.early.router[:, P * k:P * (k + 1)], m.ident[0:NE, 0:NE])
                        rw_ps.by(last)
                    if i >= LAG:
                        turn(i - LAG)
                    if i > LAG:
                        router_logits(i - LAG - 1)
                for i in range(TILES - LAG, TILES):
                    turn(i)
                    router_logits(i - 1)
                router_logits(TILES - 1)

            @block.scalar
            def _(sc):
                def copy_turned(i):
                    sc.wait_ge(xt_ps.sem, i + 1)
                    xt_sb.by(nc.scalar.copy(m.xT[:, :, P * i:P * (i + 1)],
                                            m.ps[:, 2 + i % 2, 0:DM].rearrange("p (k t) -> p k t", k=KD)))

                sc.wait_ge(rw_ps.sem, 1)
                rw_sb.by(nc.scalar.copy(m.early.router_T.rearrange("p k e -> p (k e)"), m.ps[:, 4, 0:KD * NE]))
                for i in range(TILES):
                    copy_turned(i)

            @block.vector
            def _(v):
                v.wait_ge(m.wo_in.sem, 32)
                for i in range(TILES):
                    xb.by(nc.vector.tensor_tensor(m.x[:, i, :], m.x[:, i, :], m.b_o[:, :], ALU.add))
                    v.wait_ge(o_ps.sem, i + 1)
                    v.wait_ge(xb.sem, i + 1)
                    if i >= 2:
                        v.wait_ge(x_ready.sem, i - 1)
                    dve.then_wait(v, nc.vector.tensor_tensor(work.r[:, i % 2, :], m.ps[:, i % 2, 0:DM], m.x[:, i, :],
                                                             ALU.add))
                    ln_stats(nc, v, work, i, dve, mv_ready)
                    ln_apply(nc, v, m, work, i, i, rs_ready, x_ready)

            @block.gpsimd
            def _(pool):
                for i in range(TILES):
                    ln_scale(nc, pool, m, work, i, pl, mv_ready, rs_ready)


FIRST_EXPERTS = slice(0, NE // 2)


def load_gate_up(nc, m, a, sp, e):
    for u, name in enumerate(("L1_ffn_W_gate", "L1_ffn_W_up")):
        for k in range(KD):
            sp.dma_start(m.w_gu[:, e, k, u, :], a[name][e, P * k:P * (k + 1), :].rearrange("e p i -> p e i")
                         ).then_inc(m.gu_in.sem, 16)
GATE_UP_LOADS = 3 * 2 * KD


def load_expert_weights(nc, m, a, sp):
    w = m.early
    sp.dma_start(w.router, a["L1_ffn_router_w"]).then_inc(m.early_in.sem, 16)
    sp.dma_start(w.e_bias, a["L1_ffn_e_bias"].partition_broadcast(P)).then_inc(m.early_in.sem, 16)
    sp.dma_start(w.before, a["c_before"]).then_inc(m.early_in.sem, 16)
    sp.dma_start(w.lower, a["c_lower"]).then_inc(m.early_in.sem, 16)
    sp.dma_start(w.token, a["c_iota"]).then_inc(m.early_in.sem, 16)
    sp.dma_start(w.own, a["c_own"]).then_inc(m.early_in.sem, 16)
    sp.dma_start(w.number, a["c_token"]).then_inc(m.early_in.sem, 16)
    load_gate_up(nc, m, a, sp, FIRST_EXPERTS)
    for h in range(2):
        e = slice(16 * h, 16 * h + 16)
        sp.dma_start(m.w_down_e[:, e, :], a["L1_ffn_W_down"][e, :, :].rearrange("e i d -> i e d")
                     ).then_inc(m.down_in.sem, 16)
EARLY_LOADS = 7


def route_and_run_experts(nc, m, a, out):
    with ExitStack() as ctx:
        sig = lambda name: Signal(ctx, nc, "moe_" + name)
        spaces = m.free
        sb = lambda name, shape: next(s for s in spaces if s.fits(shape)).take(*shape)
        every = sb("every", [P, P])
        restart = sb("restart", [P, TILES, NE])
        score = sb("score", [P, TILES, NE])
        mk = sb("mk", [P, TILES, NE])
        pre = sb("pre", [P, TILES, NE])
        cum = sb("cum", [P, TILES, NE])
        top = sb("top", [P, TILES, 8])
        gs = sb("gs", [P, 4, TILES * NG])
        cmp_ = sb("cmp", [P, 2, TILES, NG, NG])
        gm = sb("gm", [P, TILES * NG])
        cnt = sb("cnt", [P, TILES])
        pos = sb("pos", [P, TILES, NE])
        slot_token = sb("slot_token", [P, ST])
        slot_weight = sb("slot_weight", [P, ST])
        half = lambda *shape: sb("", [P, int(np.prod(shape)) // 2]).bitcast(BF16)
        hot = half(2, NE, CAP).rearrange("p (u e c) -> p u e c", u=2, c=CAP)
        FACTS = 2 + PARTS * NE
        info = half(TILES, FACTS).rearrange("p (i f) -> p i f", f=FACTS)
        wgt = sb("wgt", [P, TILES, NE])
        xp = sb("xp", [P, KD, SLOTS + PAIR_ROWS - CAP])
        w_row = xp.rearrange("p k s -> p (k s)")[:, 0:3 * KD * DM].rearrange("p (n k d) -> p n k d", n=3, k=KD)
        sg_hT = sb("sg_hT", [P, 4 * 2 * EI])
        sg = sg_hT[:, 0:4 * EI].rearrange("p (u i) -> p u i", u=2)
        hT = sg_hT[:, 4 * EI:].rearrange("p (u i) -> p u i", u=2)
        rest = sg_hT.rearrange("p (u i d) -> p u i d", u=2, d=DM)
        y_yp = sb("y_yp", [P, (ST + 4) * DM])
        y = y_yp[:, 0:ST * DM].rearrange("p (s d) -> p s d", d=DM)
        yp = y_yp[:, ST * DM:].rearrange("p (u n d) -> p u n d", u=2, d=DM)
        x_part = y_yp[:, 0:TILES * PARTS * DM // 2].bitcast(BF16).rearrange("p (i n d) -> p i n d", n=PARTS, d=DM)
        sw = sb("sw", [P, ST, PARTS, NE])
        wT = sb("wT", [P, 3, KD, DM])
        hs = sb("hs", [P, KD, NT])
        lin = sb("lin", [P, 2, 2, 512])
        sh = sb("sh", [P, 2, 512])
        work = ln_work(sb)
        eb, before, lower, token, own = (m.early.e_bias, m.early.before, m.early.lower, m.early.token, m.early.own)
        number = m.early.number
        back = m.weights[:, 0:ST * NT].rearrange("p (s t) -> p s t", t=NT)
        BACK_EXPERTS = -(-ST * NT // (2 * KD * EI))

        sc_ready, ready, dve, chosen, earlier, before_ps, info_ready = (sig(n) for n in (
            "sc_ready", "ready", "dve9", "chosen", "earlier", "before_ps", "info_ready"))
        hot_ready, used, xp_sb, facts_read = (sig(n) for n in ("hot_ready", "used", "xp_sb", "facts_read"))
        gu_ps, sg_ready, h_ready, hT_ps, hT_sb, y_ps, y_sb, y_out, y_early, y_late = (sig(n) for n in (
            "gu_ps", "sg_ready", "h_ready", "hT_ps", "hT_sb", "y_ps", "y_sb", "y_out", "y_early", "y_late"))
        w_in, w_ps, w_sb, sh_ps, sh_lin, sh_ready, pl = (sig(n) for n in (
            "w_in", "w_ps", "w_sb", "sh_ps", "sh_lin", "sh_ready", "pool9"))
        part_ready, rest_ready, info_split = sig("part_ready"), sig("rest_ready"), sig("info_split")
        back_ready, o_ps, mv_ready, rs_ready, x_ready = (sig(n) for n in (
            "back_ready", "o_ps", "mv_ready", "rs_ready", "x_ready"))
        SPB = ST // 2
        PIECES, TPP = TILES // 2, 2
        PAIRS = NE // 2
        NGR = PAIRS // 2
        ready_tiles = [2 * 2 * CAP * (g + 1) // P for g in range(NGR)]
        EARLY = NGR - 3
        SPLIT = ready_tiles[EARLY - 1]

        part_order = ([(j, 0) for j in range(PIECES)]
                      + [(j, n) for pair in ((0, 1), (2, 3)) for n in (1, 2) for j in pair])
        rest_order = [(j, n) for j, n in part_order if n]

        with nc.Block() as block:
            @block.sync
            def _(sp):
                for n, name in enumerate(("gate", "up", "down")):
                    sp.dma_start(w_row[:, n, :, :], k_tiles(a["L1_ffn_shared_" + name])).then_inc(w_in.sem, 16)
                by_pair = m.y_dram.rearrange("(n u c) d -> u c n d", u=2, c=CAP)
                by_tile = rows(m.y_dram)
                for g in range(NGR):
                    sp.wait_ge(y_sb.sem, g + 1)
                    for u in range(2):
                        sp.dma_start(by_pair[u, :, 2 * g:2 * g + 2, :], yp[PAIR_ROWS * u:PAIR_ROWS * u + CAP, g % 2, :, :]
                                     ).then_inc(y_out.sem, 16)
                    sp.wait_ge(y_out.sem, 32 * (g + 1))
                    t = slice(ready_tiles[g - 1] if g else 0, ready_tiles[g])
                    arrived = y_early if g < EARLY else y_late
                    sp.dma_start(y[:, t, :], by_tile[:, t, :]).then_inc(arrived.sem, 16)
                for i in range(TILES):
                    sp.wait_ge(x_ready.sem, i + 1)
                    sp.dma_start(rows(out)[:, i, :], m.x[:, i, :]).then_inc(m.stored.sem, 16)
                sp.wait_ge(m.stored.sem, 16 * TILES)

            @block.tensor
            def _(pe):
                pe.wait_ge(m.early_in.sem, 16 * EARLY_LOADS)
                pe.wait_ge(w_in.sem, 48)
                for n in range(3):
                    if n >= 2:
                        pe.wait_ge(w_sb.sem, n - 1)
                    for j in range(KD):
                        for k in range(KD):
                            c = DM * k + P * j
                            last = nc.tensor.transpose(m.ps[:, 6 + n % 2, c:c + P], w_row[:, n, j, P * k:P * (k + 1)],
                                                       m.ident[:, :])
                    w_ps.by(last)
                pe.wait_ge(w_sb.sem, 2)
                def count_earlier():
                    pe.wait_ge(chosen.sem, 1)
                    flat = lambda t: t.rearrange("p i e -> p (i e)")
                    nc.tensor.matmul(m.ps[:, 4, 0:TILES * NE], before, flat(pre), start=True, stop=False)
                    pe.wait_ge(earlier.sem, 1)
                    pe.wait_ge(ready.sem, 3)
                    before_ps.by(nc.tensor.matmul(m.ps[:, 4, 0:TILES * NE], every, flat(cum), start=False, stop=True))

                for n in range(KD * HALVES):
                    j, h = n // HALVES, n % HALVES
                    if n == KD * HALVES - 1:
                        count_earlier()
                    if n >= 2:
                        pe.wait_ge(sh_lin.sem, n - 1)
                    for u in range(2):
                        for k in range(KD):
                            last = nc.tensor.matmul(m.ps[:, 2 * (n % 2) + u, :], wT[:, u, k, P * j:P * (j + 1)],
                                                    m.xT[:, k, 512 * h:512 * (h + 1)], start=k == 0, stop=k == KD - 1)
                    sh_ps.by(last)
                pe.wait_ge(part_ready.sem, PARTS * PIECES)
                pe.wait_ge(sh_lin.sem, KD * HALVES)
                pe.wait_ge(w_sb.sem, 3)
                for i in range(TILES):
                    pe.wait_ge(hot_ready.sem, i + 1)
                    flat_hot = hot[:, i % 2, :, :].rearrange("p e c -> p (e c)")
                    for k in range(KD):
                        for c in range(3):
                            w = min(512, SLOTS - 512 * c)
                            for n in range(PARTS):
                                nc.tensor.matmul(m.ps[:, 3 * k + c, 0:w], x_part[:, i, n, P * k:P * (k + 1)],
                                                 flat_hot[:, 512 * c:512 * c + w], start=i == 0 and n == 0,
                                                 stop=i == TILES - 1 and n == PARTS - 1)
                    if i == 0:
                        pe.wait_ge(info_split.sem, 1 + PARTS)
                    for s in range(ST):
                        c = FACTS * (s % SPB)
                        last = nc.tensor.matmul(m.ps[:, 6 + s // SPB, c:c + FACTS], flat_hot[:, P * s:P * (s + 1)],
                                                info[:, i, :], start=i == 0 and s % SPB == 0, stop=i == TILES - 1,
                                                skip_group_check=True)
                    used.by(last)
                pe.wait_ge(xp_sb.sem, KD + 1)
                pe.wait_ge(m.gu_in.sem, 16 * GATE_UP_LOADS)

                def gate_up(g):
                    if g >= 4:
                        pe.wait_ge(h_ready.sem, g - 3)
                    for j in range(2):
                        for u in range(2):
                            e = 2 * (2 * g + j) + u
                            for k in range(KD):
                                last = nc.tensor.matmul(
                                    m.ps[PAIR_ROWS * u:PAIR_ROWS * (u + 1), g % 4, 2 * EI * j:2 * EI * (j + 1)],
                                    xp[:, k, CAP * e:CAP * e + PAIR_ROWS],
                                    m.w_gu[:, e, k, :, :].rearrange("p u i -> p (u i)"), start=k == 0,
                                    stop=k == KD - 1)
                    gu_ps.by(last)

                def turn(g):
                    pe.wait_ge(h_ready.sem, g + 1)
                    if g == 0:
                        pe.wait_ge(facts_read.sem, 4)
                    if g >= 1:
                        pe.wait_ge(hT_sb.sem, g)
                    for j in range(2):
                        last = nc.tensor.transpose(m.ps[:, 4, P * j:P * (j + 1)], sg[:, g % 2, EI * j:EI * (j + 1)],
                                                   m.ident[:, :])
                    hT_ps.by(last)

                def down(g):
                    pe.wait_ge(hT_sb.sem, g + 1)
                    if g == 0:
                        pe.wait_ge(m.down_in.sem, 32)
                    if g >= 2:
                        pe.wait_ge(y_sb.sem, g - 1)
                    for j in range(2):
                        for u in range(2):
                            c = P * j + PAIR_ROWS * u
                            last = nc.tensor.matmul(
                                m.ps[PAIR_ROWS * u:PAIR_ROWS * (u + 1), 5 + g % 2, DM * j:DM * (j + 1)],
                                hT[:, g % 2, c:c + PAIR_ROWS], m.w_down_e[:, 2 * (2 * g + j) + u, :], start=True,
                                stop=True)
                    y_ps.by(last)

                def sum_slots(i, tiles, last_ones):
                    dst = m.ps[:, i // 2, DM * (i % 2):DM * (i % 2 + 1)]
                    for s in tiles:
                        last = nc.tensor.matmul(dst, back[:, s, P * i:P * (i + 1)], y[:, s, :], start=False,
                                                stop=last_ones and s == ST - 1, skip_group_check=True)
                    return last

                def sum_shared(i):
                    if i % 2 == 0:
                        pe.wait_ge(h_ready.sem, NGR - 3 + i // 2)
                    for k in range(KD):
                        nc.tensor.matmul(m.ps[:, i // 2, DM * (i % 2):DM * (i % 2 + 1)], hs[:, k, P * i:P * (i + 1)],
                                         wT[:, 2, k, :], start=i % 2 == 0 and k == 0, stop=False,
                                         skip_group_check=True)

                for g in range(NGR):
                    gate_up(g)
                    if g >= 1:
                        turn(g - 1)
                    if g >= 2:
                        down(g - 2)
                pe.wait_ge(sh_ready.sem, KD * HALVES)
                pe.wait_ge(back_ready.sem, SPLIT)
                pe.wait_ge(y_early.sem, 16 * EARLY)
                for i in range(TILES):
                    sum_shared(i)
                    sum_slots(i, range(SPLIT), False)
                    if i == 0:
                        turn(NGR - 1)
                        down(NGR - 2)
                    if i == 1:
                        down(NGR - 1)
                pe.wait_ge(back_ready.sem, ST)
                pe.wait_ge(y_late.sem, 16 * (NGR - EARLY))
                for i in range(TILES):
                    o_ps.by(sum_slots(i, range(SPLIT, ST), True))

            @block.scalar
            def _(sc):
                sc_ready.by(nc.scalar.activation(score.rearrange("p i e -> p (i e)"), m.ps[:, 5, 0:TILES * NE],
                                                 ACT.Sigmoid))

                def part(j, n):
                    t = slice(TPP * j, TPP * (j + 1))
                    if n:
                        sc.wait_ge(rest_ready.sem, rest_order.index((j, n)) + 1)
                    part_ready.by(nc.scalar.copy(x_part[:, t, n, :], rest[:, j % 2, :, :] if n else m.x[:, t, :]))

                def copy_weights(n):
                    sc.wait_ge(w_ps.sem, n + 1)
                    w_sb.by(nc.scalar.copy(wT[:, n, :, :].rearrange("p k d -> p (k d)"), m.ps[:, 6 + n % 2, :]))

                def shared(n):
                    sc.wait_ge(sh_ps.sem, n + 1)
                    if n >= 2:
                        sc.wait_ge(sh_ready.sem, n - 1)
                    nc.scalar.activation(sh[:, n % 2, :], m.ps[:, 2 * (n % 2), :], ACT.Sigmoid)
                    sh_lin.by(nc.scalar.copy(lin[:, n % 2, :, :].rearrange("p u t -> p (u t)"),
                                             m.ps[:, 2 * (n % 2):2 * (n % 2) + 2, :].rearrange("p u t -> p (u t)")))

                for j, n in part_order[0:6]:
                    part(j, n)
                copy_weights(0)
                copy_weights(1)
                for j, n in part_order[6:8]:
                    part(j, n)
                copy_weights(2)
                for j, n in part_order[8:10]:
                    part(j, n)
                shared(0)
                for j, n in part_order[10:12]:
                    part(j, n)
                for n in range(1, KD * HALVES):
                    shared(n)
                sc.wait_ge(used.sem, TILES)
                flat = m.ps[:, 0:6, :].rearrange("p (k b) n -> p k (b n)", k=KD)
                xp_sb.by(nc.scalar.copy(xp[:, 0, 0:SLOTS], flat[:, 0, 0:SLOTS]))

                def copy_hT(g):
                    sc.wait_ge(hT_ps.sem, g + 1)
                    if g >= 2:
                        sc.wait_ge(y_ps.sem, g - 1)
                    hT_sb.by(nc.scalar.copy(hT[:, g % 2, :], m.ps[:, 4, 0:2 * P]))

                def copy_y(g):
                    sc.wait_ge(y_ps.sem, g + 1)
                    if g >= 2:
                        sc.wait_ge(y_out.sem, 32 * (g - 1))
                    y_sb.by(nc.scalar.copy(yp[:, g % 2, :, :].rearrange("p n d -> p (n d)"), m.ps[:, 5 + g % 2, :]))

                for g in range(NGR):
                    sc.wait_ge(gu_ps.sem, g + 1)
                    if g >= 2:
                        sc.wait_ge(hT_ps.sem, g - 1)
                    gate = m.ps[:, g % 4, :].rearrange("p (j u i) -> p j u i", j=2, u=2)[:, :, 0, :]
                    sg_ready.by(nc.scalar.activation(sg[:, g % 2, :].rearrange("p (j i) -> p j i", j=2), gate,
                                                     ACT.Sigmoid))
                    if g >= 1:
                        copy_hT(g - 1)
                    if g >= 2:
                        copy_y(g - 2)
                copy_hT(NGR - 1)
                copy_y(NGR - 2)
                copy_y(NGR - 1)

            @block.gpsimd
            def _(pool):
                ready.by(nc.gpsimd.memset(restart[:, :, 1:], 1.0))
                ready.by(nc.gpsimd.memset(restart[:, :, 0:1], 0.0))
                ready.by(nc.gpsimd.memset(every, 1.0))
                for j, n in rest_order:
                    t = slice(TPP * j, TPP * (j + 1))
                    pool.wait_ge(part_ready.sem, part_order.index((j, n - 1)) + 1)
                    if n == 1 and j >= 2:
                        pool.wait_ge(part_ready.sem, part_order.index((j - 2, PARTS - 1)) + 1)
                    left = rest[:, j % 2, :, :]
                    rest_ready.then_wait(pool, nc.gpsimd.tensor_tensor(left, m.x[:, t, :] if n == 1 else left,
                                                                       x_part[:, t, n - 1, :], ALU.subtract))
                pool.wait_ge(m.early_in.sem, 16 * EARLY_LOADS)
                info_split.by(nc.gpsimd.tensor_copy(info[:, :, 0:2], number))
                for n in range(KD * HALVES):
                    j, h = n // HALVES, n % HALVES
                    if n == KD * HALVES - 1:
                        pool.wait_ge(info_ready.sem, 1)
                        for part in range(PARTS):
                            c = slice(2 + NE * part, 2 + NE * (part + 1))
                            info_split.then_wait(pool, nc.gpsimd.tensor_copy(info[:, :, c], wgt))
                            if part < PARTS - 1:
                                pl.then_wait(pool, nc.gpsimd.tensor_tensor(wgt, wgt, info[:, :, c], ALU.subtract))
                    pool.wait_ge(sh_lin.sem, n + 1)
                    dst = hs[:, j, 512 * h:512 * (h + 1)]
                    pl.then_wait(pool, nc.gpsimd.tensor_tensor(dst, sh[:, n % 2, :], lin[:, n % 2, 0, :], ALU.mult))
                    sh_ready.by(nc.gpsimd.tensor_tensor(dst, dst, lin[:, n % 2, 1, :], ALU.mult))
                pool.wait_ge(w_ps.sem, 3)
                xp_sb.by(nc.gpsimd.memset(xp[:, :, SLOTS:], 0.0))
                for i in range(TILES):
                    ln_scale(nc, pool, m, work, i, pl, mv_ready, rs_ready)

            @block.vector
            def _(v):
                step = lambda ins: dve.then_wait(v, ins)
                tt, ts, stt = nc.vector.tensor_tensor, nc.vector.tensor_scalar, nc.vector.scalar_tensor_tensor
                v.wait_ge(m.early_in.sem, 16 * EARLY_LOADS)
                v.wait_ge(sc_ready.sem, 1)
                step(tt(mk, score, spread(eb, 1, TILES), ALU.add))
                q = mk.rearrange("p i (g j) -> p (i g) j", j=NE // NG)
                tt(gs[:, 0, :], q[:, :, 0], q[:, :, 1], ALU.max)
                tt(gs[:, 1, :], q[:, :, 0], q[:, :, 1], ALU.min)
                tt(gs[:, 2, :], q[:, :, 2], q[:, :, 3], ALU.max)
                step(tt(gs[:, 3, :], q[:, :, 2], q[:, :, 3], ALU.min))
                step(tt(gs[:, 3, :], gs[:, 1, :], gs[:, 3, :], ALU.max))
                step(tt(gs[:, 1, :], gs[:, 0, :], gs[:, 2, :], ALU.min))
                step(tt(gs[:, 1, :], gs[:, 1, :], gs[:, 3, :], ALU.max))
                step(tt(gs[:, 0, :], gs[:, 0, :], gs[:, 2, :], ALU.max))
                step(tt(gs[:, 0, :], gs[:, 0, :], gs[:, 1, :], ALU.add))
                g3 = gs[:, 0, :].rearrange("p (i g) -> p i g", g=NG)
                for i in range(TILES):
                    others, mine = spread(g3[:, i, :], 1, NG), spread(g3[:, i, :], 2, NG)
                    tt(cmp_[:, 0, i, :, :], others, mine, ALU.is_gt)
                    last = tt(cmp_[:, 1, i, :, :], others, mine, ALU.is_equal)
                step(last)
                c3 = lambda n: cmp_[:, n, :, :, :].rearrange("p i g h -> p i (g h)")
                step(tt(c3(1), c3(1), spread(lower.rearrange("p g h -> p (g h)"), 1, TILES), ALU.mult))
                step(tt(c3(0), c3(0), c3(1), ALU.add))
                step(nc.vector.tensor_reduce(gm, cmp_[:, 0, :, :, :].rearrange("p i g h -> p (i g) h"), AX.X, ALU.add))
                step(ts(gm, gm, TKG - 0.5, None, ALU.is_lt))
                step(tt(q, q, spread(gm, 2, NE // NG), ALU.mult))
                for i in range(TILES):
                    last = nc.vector.max(top[:, i, :], mk[:, i, :])
                step(last)
                fourth = spread(top[:, :, TOPK - 1], 2, NE)
                step(tt(pos, mk, fourth, ALU.is_gt))
                step(tt(mk, mk, fourth, ALU.is_equal))
                step(nc.vector.tensor_reduce(cnt, pos, AX.X, ALU.add))
                step(ts(cnt, cnt, -1.0, TOPK + 0.5, ALU.mult, ALU.add))
                v.wait_ge(ready.sem, 3)
                flat = lambda t: t.rearrange("p i e -> p (i e)")
                step(nc.vector.tensor_tensor_scan(flat(pre), flat(restart), flat(mk), 0.0, ALU.mult, ALU.add))
                step(tt(pre, pre, spread(cnt, 2, NE), ALU.is_lt))
                step(tt(pre, pre, mk, ALU.mult))
                chosen.then_wait(v, tt(pre, pre, pos, ALU.add))
                step(ts(cum[:, 0, :], pre[:, 0, :], 0.0, None, ALU.mult))
                for i in range(1, TILES):
                    (step if i < TILES - 1 else earlier.by)(tt(cum[:, i, :], cum[:, i - 1, :], pre[:, i - 1, :],
                                                               ALU.add))
                step(tt(mk, score, pre, ALU.mult))
                step(nc.vector.tensor_reduce(cnt, mk, AX.X, ALU.add))
                step(ts(cnt, cnt, 1e-20, None, ALU.add))
                step(nc.vector.reciprocal(cnt, cnt))
                info_ready.then_wait(v, stt(wgt, mk, MSCALE, spread(cnt, 2, NE), ALU.mult, ALU.mult))
                v.wait_ge(before_ps.sem, 1)
                step(stt(flat(pos), m.ps[:, 4, 0:TILES * NE], 1.0, flat(pre), ALU.add, ALU.mult))
                step(ts(pos, pos, -1.0, None, ALU.add))
                for i in range(TILES):
                    if i >= 2:
                        v.wait_ge(used.sem, i - 1)
                    hot_ready.by(tt(hot[:, i % 2, :, :], spread(token[:, 0:CAP], 1, NE), spread(pos[:, i, :], 2, CAP),
                                    ALU.is_equal))
                v.wait_ge(used.sem, TILES)
                ps3 = m.ps[:, 0:6, :].rearrange("p (k b) n -> p k (b n)", k=KD)
                xp_sb.by(nc.vector.tensor_copy(xp[:, 1, 0:SLOTS], ps3[:, 1, 0:SLOTS]))
                for b in range(2):
                    facts = m.ps[:, 6 + b, 0:SPB * FACTS].rearrange("p (s f) -> p s f", f=FACTS)
                    t = slice(SPB * b, SPB * (b + 1))
                    facts_read.by(nc.vector.tensor_reduce(slot_token[:, t], facts[:, :, 0:2], AX.X, ALU.add))
                    facts_read.by(tt(sw[:, t, :, :], facts[:, :, 2:].rearrange("p s (n e) -> p s n e", e=NE),
                                     spread(own[:, t, :], 2, PARTS), ALU.mult))
                v.wait_ge(facts_read.sem, 4)
                step(nc.vector.tensor_reduce(slot_weight, sw.rearrange("p s n e -> p s (n e)"), AX.X, ALU.add))
                for g in range(NGR):
                    u4 = m.ps[:, g % 4, :].rearrange("p (j u i) -> p j u i", j=2, u=2)
                    h = sg[:, g % 2, :].rearrange("p (j i) -> p j i", j=2)
                    v.wait_ge(sg_ready.sem, g + 1)
                    step(tt(h, u4[:, :, 0, :], h, ALU.mult))
                    h_ready.by(tt(h, h, u4[:, :, 1, :], ALU.mult))
                    if 4 * (g + 1) >= BACK_EXPERTS and back_ready.n == 0:
                        for s in range(ST):
                            back_ready.by(ts(back[:, s, :], token, slot_token[:, s:s + 1], slot_weight[:, s:s + 1],
                                             ALU.is_equal, ALU.mult))
                for i in range(TILES):
                    v.wait_ge(o_ps.sem, 2 * (i // 2) + 2)
                    if i >= 2:
                        v.wait_ge(x_ready.sem, i - 1)
                    step(tt(work.r[:, i % 2, :], m.ps[:, i // 2, DM * (i % 2):DM * (i % 2 + 1)], m.x[:, i, :],
                            ALU.add))
                    ln_stats(nc, v, work, i, dve, mv_ready)
                    if i >= 1:
                        ln_apply(nc, v, m, work, i - 1, i - 1, rs_ready, x_ready)
                ln_apply(nc, v, m, work, TILES - 1, TILES - 1, rs_ready, x_ready)


def constants():
    p = np.arange(P)
    f = lambda x: np.ascontiguousarray(x, dtype=np.float32)
    c = {
        "c_ident": f(np.eye(P)),
        "c_eye_q": f(p[:, None] % Q == np.arange(Q)[None, :]),
        "c_sel_last": f(np.broadcast_to((p[:, None] == Q * np.arange(G)[None, :] + Q - 1)[:, :, None], (P, G, P))),
        "c_in_chunk": f(p[:, None] // Q == np.arange(G)[None, :]),
        "c_first8": f(np.broadcast_to(LE - np.arange(LE), (P, LE))),
    }
    c["c_before"] = f(p[:, None] < p[None, :])
    c["c_lower"] = f(np.broadcast_to(np.arange(NG)[None, :] < np.arange(NG)[:, None], (P, NG, NG)))
    c["c_iota"] = f(np.broadcast_to(np.arange(NT), (P, NT)))
    c["c_token"] = f(np.stack([np.broadcast_to(p[:, None], (P, TILES)),
                               np.broadcast_to(P * np.arange(TILES)[None, :], (P, TILES))], axis=2))
    slot = p[:, None] + P * np.arange(ST)[None, :]
    c["c_own"] = f(slot[:, :, None] // CAP == np.arange(NE)[None, None, :])
    pos = np.arange(SEQ, dtype=np.float32)
    inv = (1.0 / np.power(np.float32(10000.0), np.arange(0, HD, 2, dtype=np.float32) / np.float32(HD))).astype(np.float32)
    ang = (pos[:, None] * np.concatenate([inv, inv])[None, 0::2]).astype(np.float32)
    cos, sin = np.repeat(np.cos(ang), 2, axis=1), np.repeat(np.sin(ang), 2, axis=1)
    sin = sin * np.where(np.arange(HD) % 2 == 0, -1.0, 1.0)
    c["c_cos"] = f(cos.reshape(TPH, P, HD).transpose(1, 0, 2))
    c["c_sin"] = f(sin.reshape(TPH, P, HD).transpose(1, 0, 2))
    dist = np.zeros((P, NCOL))
    for k in range(TPH):
        q = np.arange(P * k, SEQ)[None, :]
        key = P * k + p[:, None]
        dist[:, KEY_COL[k]:KEY_COL[k] + SEQ - P * k] = np.where(q >= key, -(q - key), LATER)
    c["c_dist"] = f(dist)
    return c


def build(nc, a, out, upto=99):
    ctx = ExitStack()
    with ctx:
        m = Memory()
        sb = lambda name, shape, dt=F32: ctx.enter_context(nc.sbuf_tensor(name, shape, dt))
        m.ps = ctx.enter_context(nc.psum_tensor("ps", [P, 8, 512], F32))
        m.x = sb("x", [P, TILES, DM])
        m.xT = sb("xT", [P, KD, NT])
        m.ident = sb("ident", [P, P])
        m.half = sb("half", [P, 1])
        m.wz_in, m.late_in, m.const_in, m.small_in, m.dt_in = (Signal(ctx, nc, n) for n in (
            "wz_in", "late_in", "const_in", "small_in", "dt_in"))
        m.lora_in, m.wq_in, m.w_up_in, m.attn_in = (Signal(ctx, nc, n) for n in (
            "lora_in", "wq_in", "w_up_in", "attn_in"))
        m.tables_in, m.biases_in, m.dist_in = (Signal(ctx, nc, n) for n in ("tables_in", "biases_in", "dist_in"))
        m.decay_in = [Signal(ctx, nc, f"decay_in{j}") for j in range(2)]
        m.wo_in, m.early_in, m.gu_in, m.down_in, m.stored = (Signal(ctx, nc, n) for n in (
            "wo_in", "early_in", "gu_in", "down_in", "stored"))
        with ExitStack() as attention:
            sba = lambda name, shape: attention.enter_context(nc.sbuf_tensor(name, shape, F32))
            m.w_down = sba("w_down", [P, KD, LATENT])
            m.b_down = sba("b_down", [LATENT, 1])
            m.b_o = sba("b_o", [P, DM])
            m.gate_b = sba("gate_b", [P, AH])
            m.w_q = sba("w_q", [P, KD, AH * HD])
            first_layer(nc, m, a, upto)
            if upto < 5:
                return store(nc, m, out)
            m.qT = sba("qT", [P, AH, NT])
            m.kv = sba("kv", [P, NKV * NT + TILES * NKV * VW])
            m.kT = m.kv[:, 0:NKV * NT].rearrange("p (g t) -> p g t", t=NT)
            m.v = m.kv[:, NKV * NT:].rearrange("p (i g d) -> p i g d", g=NKV, d=VW)
            bias = sba("bias", [P, BATCH, NCOL])
            m.bias = [bias[:, b, :] for b in range(BATCH)]
            m.dist = m.bias[1]
            with ExitStack() as once:
                sbo = lambda name, shape: once.enter_context(nc.sbuf_tensor(name, shape, F32))
                m.w_up = sbo("w_up", [LATENT, 2 * NKV * HD])
                m.b_up = sbo("b_up", [P, 2 * NKV * HD])
                m.b_q = sbo("b_q", [P, AH * HD])
                m.norm_qk = sbo("norm_qk", [P, 2, HD])
                m.cos_row = sbo("cos_row", [P, TPH, HD])
                m.sin_row = sbo("sin_row", [P, TPH, HD])
                prepare_attention(nc, m, a)
            m.w_o = m.w_q[:, :, :].rearrange("p k (h n) -> p (k h) n", n=DM)
            m.gate_w = m.xT[:, :, :].rearrange("p k (h e) -> p (k h) e", e=HD)
            m.weights = sba("weights", [P, 2 * NE * DM])
            m.rows = m.weights[:, 0:NE * DM]
            m.w_gu = m.weights[:, :].rearrange("p (e k u i) -> p e k u i", k=KD, u=2, i=EI)
            m.w_down_e = m.kv[:, 0:NE * DM].rearrange("p (e d) -> p e d", d=DM)
            attend(nc, m, a)
            early = Space(bias[:, :, :].rearrange("p b n -> p (b n)"))
            m.early = Memory()
            m.early.router, m.early.e_bias, m.early.before = early.take(NE, DM), early.take(P, NE), early.take(P, P)
            m.early.lower, m.early.token = early.take(P, NG, NG), early.take(P, NT)
            m.early.own, m.early.number = early.take(P, ST, NE), early.take(P, TILES, 2)
            m.early.router_T = early.take(P, KD, NE)
            nc.all_engine_barrier(sems_to_clear=range(m.stored.sem.num + 1, SEMAPHORES))
            attention_output(nc, m, a)
            m.free = [Space(m.qT[:, :, :].rearrange("p h t -> p (h t)")),
                      Space(m.w_q[:, :, :].rearrange("p k n -> p (k n)")), early]
            m.y_dram = nc.dram_tensor("y_dram", (SLOTS, DM), F32, kind="Internal").ap()
            route_and_run_experts(nc, m, a, out)


def first_layer(nc, m, a, upto):
        with ExitStack() as lora:
            sbl = lambda name, shape: lora.enter_context(nc.sbuf_tensor(name, shape, F32))
            m.lw_a = sbl("lw_a", [P, LE * LR // P, DM])
            m.lw_b = sbl("lw_b", [P, KD, LE, LR])
            m.lw_g = sbl("lw_g", [LE, DM])
            m.first8 = sbl("first8", [P, LE])
            mixer_layer(nc, m, a, upto)
            if upto >= 4:
                lora_experts(nc, m, a)


def mixer_layer(nc, m, a, upto):
        with ExitStack() as mixer:
            sbm = lambda name, shape: mixer.enter_context(nc.sbuf_tensor(name, shape, F32))
            m.w_in = sbm("w_in", [P, KD, PROJ])
            m.w_out = sbm("w_out", [P, INTER // P, DM])
            m.norm_w = sbm("norm_w", [P, INTER // P])
            m.conv_w = sbm("conv_w", [P, CT, KCONV])
            m.conv_b = sbm("conv_b", [P, CT])
            m.d_row = sbm("d_row", [P, HEADS])
            m.eye_q = sbm("eye_q", [P, Q])
            m.sel_last = sbm("sel_last", [P, G, P])
            m.in_chunk = sbm("in_chunk", [P, G])
            m.xc = sbm("xc", [P, CT, NT])
            m.dtT = sbm("dtT", [P, SEQ])
            m.sinceT = sbm("sinceT", [P, SEQ])
            m.decay = sbm("decay", [P, 2, HEADS, Q])
            m.x_row = sbm("x_row", [P, TILES, INTER])
            m.z_row = m.w_q[:, :, :].rearrange("p k n -> p (k n)").rearrange("p (i n) -> p i n", n=INTER)
            m.b_row = sbm("b_row", [P, TILES, NSTATE])
            m.since_row = sbm("since_row", [P, TILES, HEADS])
            m.da_dram = nc.dram_tensor("da_dram", (BATCH * CHUNKS, HEADS, Q), F32, kind="Internal").ap()
            project_and_convolve(nc, m, a)
            with ExitStack() as pair:
                m.dt_end = pair.enter_context(nc.sbuf_tensor("dt_end", [P, TILES, HEADS, PDIM], F32))
                if upto >= 2:
                    within_chunks(nc, m, a)
                if upto >= 3:
                    carry_states(nc, m, a)


def store(nc, m, out):
    with ExitStack() as ctx:
        stored = Signal(ctx, nc, "stored")
        with nc.Block() as block:
            @block.sync
            def _(sp):
                sp.dma_start(rows(out), m.x[:, :, :]).then_inc(stored.sem, 16)
                sp.wait_ge(stored.sem, 16)


def kernel(**inputs):
    import concourse.bacc as bacc
    from concourse.bass_utils import run_bass_kernel_spmd

    nc = bacc.Bacc("TRN2", target_bir_lowering=False, num_devices=1)
    arrays, a = {}, {}
    for name, value in {**inputs, **constants()}.items():
        value = np.ascontiguousarray(value)
        arrays[f"in_{name}"] = value
        a[name] = nc.dram_tensor(f"in_{name}", value.shape, mybir.dt.from_np(value.dtype), kind="ExternalInput").ap()
    a["x"] = a["L0_attn_hidden_states"].rearrange("b t d -> (b t) d")
    out = nc.dram_tensor("out_0", (BATCH, SEQ, DM), F32, kind="ExternalOutput").ap()
    build(nc, a, out.rearrange("b t d -> (b t) d"))
    results = run_bass_kernel_spmd(nc, [arrays], core_ids=[0]).results
    return results[0]["out_0"]
```
